# Optimizing a Trainium2 kernel written in Bass

```python
import numpy as np
import jax
import jax.numpy as jnp

def _softmax(x, axis=-1):
    return jax.nn.softmax(x, axis=axis)

def _gelu(x):
    return jax.nn.gelu(x, approximate=True)

def _silu(x):
    return jax.nn.silu(x)

def _sigmoid(x):
    return jax.nn.sigmoid(x)

def _layernorm(x, axis=-1, eps=1e-05):
    m = jnp.mean(x, axis=axis, keepdims=True)
    v = jnp.var(x, axis=axis, keepdims=True)
    return (x - m) / jnp.sqrt(v + eps)

def _scatter_add(tgt, idx, src, axis=0):
    return tgt.at[idx].add(src)

def _segment_sum(src, seg, n):
    return jax.ops.segment_sum(src, seg, n)
kernel_name = 'mk_gnn_preln_d4_gnn_r16_1cbc2b'

def setup_inputs(seed: int=0):
    np.random.seed(seed)
    _w = jnp.asarray

    def _rec_inputs():
        import jax
        import jax.numpy as jnp
        _gk = jax.random.key(seed)
        x = -1.686e-05 + 1 * jax.random.normal(jax.random.fold_in(_gk, 1), (3125, 160), jnp.float32)
        _s = jax.random.randint(jax.random.fold_in(_gk, 2), (50000,), 0, 3125, jnp.int32)
        _d = jax.random.randint(jax.random.fold_in(_gk, 3), (50000,), 0, 3125, jnp.int32)
        _loop = jnp.arange(3125, dtype=jnp.int32)
        src = jnp.concatenate([_s, _d, _loop])
        dst = jnp.concatenate([_d, _s, _loop])
        _o = jnp.argsort(dst, stable=True)
        src = src[_o]
        dst = dst[_o]
        edge_attr_12 = jax.random.uniform(jax.random.fold_in(_gk, 12), (103125, 12), jnp.float32, 0.0, 1)
        edge_attr_16 = jax.random.uniform(jax.random.fold_in(_gk, 13), (103125, 16), jnp.float32, 0.0, 1)
        edge_attr_32 = 0.000196303 + 1.00016 * jax.random.normal(jax.random.fold_in(_gk, 14), (103125, 32), jnp.float32)
        edge_attr_4 = 0.000486536 + 0.999406 * jax.random.normal(jax.random.fold_in(_gk, 15), (103125, 4), jnp.float32)
        node_vec1 = jax.random.uniform(jax.random.fold_in(_gk, 17), (3125, 1), jnp.float32, 0.0, 0.999994)
        return (x, src, dst, edge_attr_12, edge_attr_16, edge_attr_32, edge_attr_4, node_vec1)
    x, src, dst, edge_attr_12, edge_attr_16, edge_attr_32, edge_attr_4, node_vec1 = _rec_inputs()

    def _L0_gnn_setup():
        import jax, jax.numpy as jnp
        import numpy as np
        N = 3125
        E = 25000
        MUL0 = 64
        MUL1 = 32
        NEF = 12
        RN = 100
        NUM_NEIGHBORS = 8.0
        WNUM = MUL0 + MUL0 + MUL1 + MUL1

        def _split(x):
            return (x[:, :MUL0], x[:, MUL0:].reshape(-1, MUL1, 3))

        def _fctp_scalar_attr(x0, x1, z, Ws, Wv):
            s = x0 @ Ws * z / np.sqrt(Ws.shape[0])
            v = jnp.einsum('nuc,uw->nwc', x1, Wv) * z[:, :, None] / np.sqrt(Wv.shape[0])
            return (s, v)
        key = jax.random.key(seed)
        ks = jax.random.split(key, 16)
        return {'node_input': jax.random.normal(ks[0], (N, MUL0 + 3 * MUL1), jnp.float32), 'node_attr': jax.random.uniform(ks[1], (N, 1), dtype=jnp.float32), 'edge_src': jax.random.randint(ks[2], (E,), 0, N), 'edge_dst': jax.random.randint(ks[3], (E,), 0, N), 'edge_attr': jax.random.normal(ks[4], (E, 4), jnp.float32), 'edge_features': jax.random.uniform(ks[5], (E, NEF), dtype=jnp.float32), 'W_sc0': jax.random.normal(ks[6], (MUL0, MUL0), jnp.float32), 'W_sc1': jax.random.normal(ks[7], (MUL1, MUL1), jnp.float32), 'W_l1_0': jax.random.normal(ks[8], (MUL0, MUL0), jnp.float32), 'W_l1_1': jax.random.normal(ks[9], (MUL1, MUL1), jnp.float32), 'W_fc1': jax.random.normal(ks[10], (NEF, RN), jnp.float32), 'W_fc2': jax.random.normal(ks[11], (RN, WNUM), jnp.float32), 'W_l2_0': jax.random.normal(ks[12], (MUL0 + MUL1, MUL0), jnp.float32), 'W_l2_1': jax.random.normal(ks[13], (MUL0 + MUL1, MUL1), jnp.float32)}
    _L0_gnn_all = _L0_gnn_setup()
    _L0_gnn_in = {k: v for k, v in _L0_gnn_all.items() if k in ('W_sc0', 'W_sc1', 'W_l1_0', 'W_l1_1', 'W_fc1', 'W_fc2', 'W_l2_0', 'W_l2_1')}
    del _L0_gnn_all

    def _L1_gnn_setup():
        import jax, jax.numpy as jnp
        import numpy as np
        MUL0_N, MUL1_N = (64, 32)
        MUL0_E, MUL1_E = (8, 8)
        MUL0_H, MUL1_H = (64, 32)
        N_NODES, N_EDGES = (3125, 50000)
        D_NODE = MUL0_N + 3 * MUL1_N
        D_EDGE = MUL0_E + 3 * MUL1_E
        D_HID = MUL0_H + 3 * MUL1_H

        def _split(x, mul0, mul1):
            s = x[..., :mul0]
            v = x[..., mul0:].reshape(x.shape[0], mul1, 3)
            return (s, v)

        def fctp_messages(x, e, W1, W2, W3, W4):
            xs, xv = _split(x, MUL0_N, MUL1_N)
            es, ev = _split(e, MUL0_E, MUL1_E)
            inv_sqrt2 = 1.0 / np.sqrt(2.0)
            s1 = jnp.einsum('ea,eb,abc->ec', xs, es, W1) * (1.0 / np.sqrt(MUL0_N * MUL0_E))
            s2 = jnp.einsum('eai,ebi,abc->ec', xv, ev, W2) * (1.0 / (np.sqrt(3.0) * np.sqrt(MUL1_N * MUL1_E)))
            out_s = (s1 + s2) * inv_sqrt2
            v1 = jnp.einsum('ea,ebi,abc->eci', xs, ev, W3) * (1.0 / np.sqrt(MUL0_N * MUL1_E))
            v2 = jnp.einsum('eai,eb,abc->eci', xv, es, W4) * (1.0 / np.sqrt(MUL1_N * MUL0_E))
            out_v = (v1 + v2) * inv_sqrt2
            return jnp.concatenate([out_s, out_v.reshape(out_v.shape[0], -1)], axis=-1)
        key = jax.random.key(seed)
        ks = jax.random.split(key, 12)
        node_features = jax.random.normal(ks[0], (N_NODES, D_NODE), dtype=jnp.float32)
        edge_index = jax.random.randint(ks[1], (2, N_EDGES), 0, N_NODES, dtype=jnp.int64)
        edge_attr_tensor = jax.random.normal(ks[2], (N_EDGES, D_EDGE), dtype=jnp.float32)
        node_attr_scalar_raw = jax.random.normal(ks[3], (N_NODES, 1), dtype=jnp.float32)
        W1 = jax.random.normal(ks[4], (MUL0_N, MUL0_E, MUL0_H), dtype=jnp.float32)
        W2 = jax.random.normal(ks[5], (MUL1_N, MUL1_E, MUL0_H), dtype=jnp.float32)
        W3 = jax.random.normal(ks[6], (MUL0_N, MUL1_E, MUL1_H), dtype=jnp.float32)
        W4 = jax.random.normal(ks[7], (MUL1_N, MUL0_E, MUL1_H), dtype=jnp.float32)
        Wm = jax.random.normal(ks[8], (D_HID, D_HID), dtype=jnp.float32) / np.sqrt(D_HID)
        bm = jnp.zeros((D_HID,), dtype=jnp.float32)
        Wu = jax.random.normal(ks[9], (D_NODE + D_HID, D_NODE), dtype=jnp.float32) / np.sqrt(D_NODE + D_HID)
        bu = jnp.zeros((D_NODE,), dtype=jnp.float32)
        return {'node_features': node_features, 'edge_index': edge_index, 'edge_attr_tensor': edge_attr_tensor, 'node_attr_scalar_raw': node_attr_scalar_raw, 'W1': W1, 'W2': W2, 'W3': W3, 'W4': W4, 'Wm': Wm, 'bm': bm, 'Wu': Wu, 'bu': bu}
    _L1_gnn_all = _L1_gnn_setup()
    _L1_gnn_in = {k: v for k, v in _L1_gnn_all.items() if k in ('W1', 'W2', 'W3', 'W4', 'Wm', 'bm', 'Wu', 'bu')}
    del _L1_gnn_all

    def _L2_gnn_setup():
        import jax, jax.numpy as jnp
        import numpy as np
        N = 1250
        E = 40000
        INV_SQRT3 = 0.5773502691896258
        INV8 = 0.125
        INV_SQRT32 = 0.17677669529663687
        INV64 = 0.015625
        INV32 = 0.03125
        INV_SQRT2048 = 0.022097086912079608
        key = jax.random.key(seed)
        ks = jax.random.split(key, 16)
        f32 = jnp.float32
        return {'node_features': jax.random.normal(ks[0], (N, 160), f32), 'edge_index': jax.random.randint(ks[1], (2, E), 0, N), 'edge_attr_tensor': jax.random.normal(ks[2], (E, 4), f32), 'node_attr_scalar_raw': jax.random.normal(ks[3], (N, 1), f32), 'Wm_ss': jax.random.normal(ks[4], (64, 64), f32), 'Wm_vv': jax.random.normal(ks[5], (32, 64), f32), 'Wm_sv': jax.random.normal(ks[6], (64, 32), f32), 'Wm_vs': jax.random.normal(ks[7], (32, 32), f32), 'Lm_s': jax.random.normal(ks[8], (64, 64), f32), 'Lm_v': jax.random.normal(ks[9], (32, 32), f32), 'Wu_ss': jax.random.normal(ks[10], (64, 64, 64), f32), 'Wu_vv': jax.random.normal(ks[11], (32, 32, 64), f32), 'Wu_sv': jax.random.normal(ks[12], (64, 32, 32), f32), 'Wu_vs': jax.random.normal(ks[13], (32, 64, 32), f32), 'Lu_s': jax.random.normal(ks[14], (64, 64), f32), 'Lu_v': jax.random.normal(ks[15], (32, 32), f32)}
    _L2_gnn_all = _L2_gnn_setup()
    _L2_gnn_in = {k: v for k, v in _L2_gnn_all.items() if k in ('Wm_ss', 'Wm_vv', 'Wm_sv', 'Wm_vs', 'Lm_s', 'Lm_v', 'Wu_ss', 'Wu_vv', 'Wu_sv', 'Wu_vs', 'Lu_s', 'Lu_v')}
    del _L2_gnn_all

    def _L3_gnn_setup():
        import jax, jax.numpy as jnp
        import numpy as np
        N, E = (1250, 20000)
        CS, CV = (64, 32)
        AS_, AV, H = (16, 8, 4)
        NB = 16
        SQRT3 = 1.7320508075688772
        SQRT2 = 1.4142135623730951
        EPS = 1e-05

        def _cg_tp(s, v, y0, y1, w_ss, w_sv, w_vs, w_vv0, w_vv1):
            out_s = jnp.concatenate([w_ss * s * y0[:, None], w_vv0 * (jnp.einsum('eci,ei->ec', v, y1) / SQRT3)], axis=-1)
            out_v = jnp.concatenate([(w_sv * s)[:, :, None] * y1[:, None, :], (w_vs * jnp.ones_like(v[..., 0]))[..., None] * v * y0[:, None, None], (w_vv1 * jnp.ones_like(v[..., 0]))[..., None] * (jnp.cross(v, y1[:, None, :]) / SQRT2)], axis=1)
            return (out_s, out_v)

        def _equiv_layernorm(s, v, gamma_s, beta_s, gamma_v):
            mu = jnp.mean(s, axis=-1, keepdims=True)
            var = jnp.var(s, axis=-1, keepdims=True)
            s_n = (s - mu) * jax.lax.rsqrt(var + EPS) * gamma_s + beta_s
            rms = jnp.sqrt(jnp.mean(jnp.sum(v * v, axis=-1), axis=-1, keepdims=True) + EPS)
            v_n = v / rms[..., None] * gamma_v[None, :, None]
            return (s_n, v_n)
        key = jax.random.key(seed)
        ks = jax.random.split(key, 26)

        def rn(k, shape, fan):
            return jax.random.normal(k, shape, jnp.float32) / np.sqrt(fan)
        D1S, D1V = (CS + CV, CS + 2 * CV)
        WN = 2 * CS + 3 * CV
        inp = {'node': jax.random.normal(ks[0], (N, CS + 3 * CV), jnp.float32), 'edge_index': jax.random.randint(ks[1], (2, E), 0, N, jnp.int64 if jax.config.jax_enable_x64 else jnp.int32), 'rbf': jax.random.uniform(ks[2], (E, NB), jnp.float32), 'rsh': jax.random.normal(ks[3], (E, 4), jnp.float32), 'gamma_s': jnp.ones((CS,), jnp.float32), 'beta_s': jnp.zeros((CS,), jnp.float32), 'gamma_v': jnp.ones((CV,), jnp.float32), 'Ws_src': rn(ks[4], (CS, CS), CS), 'Wv_src': rn(ks[5], (CV, CV), CV), 'Ws_dst': rn(ks[6], (CS, CS), CS), 'Wv_dst': rn(ks[7], (CV, CV), CV), 'W_rbf': rn(ks[8], (NB, WN), NB), 'W_alpha': rn(ks[9], (D1S, H * AS_), D1S), 'alpha_dot': rn(ks[10], (1, H, AS_), AS_), 'Ws_val': rn(ks[11], (D1S, CS), D1S), 'Wv_val': rn(ks[12], (D1V, CV), D1V), 'Wg': rn(ks[13], (CS, CV), CS), 'w2_ss': rn(ks[14], (CS,), 1), 'w2_sv': rn(ks[15], (CS,), 1), 'w2_vs': rn(ks[16], (CV,), 1), 'w2_vv0': rn(ks[17], (CV,), 1), 'w2_vv1': rn(ks[18], (CV,), 1), 'Ws_vlin': rn(ks[19], (D1S, H * AS_), D1S), 'Wv_vlin': rn(ks[20], (D1V, H * AV), D1V), 'Wps': rn(ks[21], (H * AS_, CS), H * AS_), 'Wpv': rn(ks[22], (H * AV, CV), H * AV)}
        return inp
    _L3_gnn_all = _L3_gnn_setup()
    _L3_gnn_in = {k: v for k, v in _L3_gnn_all.items() if k in ('gamma_s', 'beta_s', 'gamma_v', 'Ws_src', 'Wv_src', 'Ws_dst', 'Wv_dst', 'W_rbf', 'W_alpha', 'alpha_dot', 'Ws_val', 'Wv_val', 'Wg', 'w2_ss', 'w2_sv', 'w2_vs', 'w2_vv0', 'w2_vv1', 'Ws_vlin', 'Wv_vlin', 'Wps', 'Wpv')}
    del _L3_gnn_all
    return {'x': x, 'src': src, 'dst': dst, 'edge_attr_12': edge_attr_12, 'edge_attr_16': edge_attr_16, 'edge_attr_32': edge_attr_32, 'edge_attr_4': edge_attr_4, 'node_vec1': node_vec1, 'L0_gnn_W_sc0': _L0_gnn_in['W_sc0'], 'L0_gnn_W_sc1': _L0_gnn_in['W_sc1'], 'L0_gnn_W_l1_0': _L0_gnn_in['W_l1_0'], 'L0_gnn_W_l1_1': _L0_gnn_in['W_l1_1'], 'L0_gnn_W_fc1': _L0_gnn_in['W_fc1'], 'L0_gnn_W_fc2': _L0_gnn_in['W_fc2'], 'L0_gnn_W_l2_0': _L0_gnn_in['W_l2_0'], 'L0_gnn_W_l2_1': _L0_gnn_in['W_l2_1'], 'L1_gnn_W1': _L1_gnn_in['W1'], 'L1_gnn_W2': _L1_gnn_in['W2'], 'L1_gnn_W3': _L1_gnn_in['W3'], 'L1_gnn_W4': _L1_gnn_in['W4'], 'L1_gnn_Wm': _L1_gnn_in['Wm'], 'L1_gnn_bm': _L1_gnn_in['bm'], 'L1_gnn_Wu': _L1_gnn_in['Wu'], 'L1_gnn_bu': _L1_gnn_in['bu'], 'L2_gnn_Wm_ss': _L2_gnn_in['Wm_ss'], 'L2_gnn_Wm_vv': _L2_gnn_in['Wm_vv'], 'L2_gnn_Wm_sv': _L2_gnn_in['Wm_sv'], 'L2_gnn_Wm_vs': _L2_gnn_in['Wm_vs'], 'L2_gnn_Lm_s': _L2_gnn_in['Lm_s'], 'L2_gnn_Lm_v': _L2_gnn_in['Lm_v'], 'L2_gnn_Wu_ss': _L2_gnn_in['Wu_ss'], 'L2_gnn_Wu_vv': _L2_gnn_in['Wu_vv'], 'L2_gnn_Wu_sv': _L2_gnn_in['Wu_sv'], 'L2_gnn_Wu_vs': _L2_gnn_in['Wu_vs'], 'L2_gnn_Lu_s': _L2_gnn_in['Lu_s'], 'L2_gnn_Lu_v': _L2_gnn_in['Lu_v'], 'L3_gnn_gamma_s': _L3_gnn_in['gamma_s'], 'L3_gnn_beta_s': _L3_gnn_in['beta_s'], 'L3_gnn_gamma_v': _L3_gnn_in['gamma_v'], 'L3_gnn_Ws_src': _L3_gnn_in['Ws_src'], 'L3_gnn_Wv_src': _L3_gnn_in['Wv_src'], 'L3_gnn_Ws_dst': _L3_gnn_in['Ws_dst'], 'L3_gnn_Wv_dst': _L3_gnn_in['Wv_dst'], 'L3_gnn_W_rbf': _L3_gnn_in['W_rbf'], 'L3_gnn_W_alpha': _L3_gnn_in['W_alpha'], 'L3_gnn_alpha_dot': _L3_gnn_in['alpha_dot'], 'L3_gnn_Ws_val': _L3_gnn_in['Ws_val'], 'L3_gnn_Wv_val': _L3_gnn_in['Wv_val'], 'L3_gnn_Wg': _L3_gnn_in['Wg'], 'L3_gnn_w2_ss': _L3_gnn_in['w2_ss'], 'L3_gnn_w2_sv': _L3_gnn_in['w2_sv'], 'L3_gnn_w2_vs': _L3_gnn_in['w2_vs'], 'L3_gnn_w2_vv0': _L3_gnn_in['w2_vv0'], 'L3_gnn_w2_vv1': _L3_gnn_in['w2_vv1'], 'L3_gnn_Ws_vlin': _L3_gnn_in['Ws_vlin'], 'L3_gnn_Wv_vlin': _L3_gnn_in['Wv_vlin'], 'L3_gnn_Wps': _L3_gnn_in['Wps'], 'L3_gnn_Wpv': _L3_gnn_in['Wpv']}

def reference(x, src, dst, edge_attr_12, edge_attr_16, edge_attr_32, edge_attr_4, node_vec1, L0_gnn_W_sc0, L0_gnn_W_sc1, L0_gnn_W_l1_0, L0_gnn_W_l1_1, L0_gnn_W_fc1, L0_gnn_W_fc2, L0_gnn_W_l2_0, L0_gnn_W_l2_1, L1_gnn_W1, L1_gnn_W2, L1_gnn_W3, L1_gnn_W4, L1_gnn_Wm, L1_gnn_bm, L1_gnn_Wu, L1_gnn_bu, L2_gnn_Wm_ss, L2_gnn_Wm_vv, L2_gnn_Wm_sv, L2_gnn_Wm_vs, L2_gnn_Lm_s, L2_gnn_Lm_v, L2_gnn_Wu_ss, L2_gnn_Wu_vv, L2_gnn_Wu_sv, L2_gnn_Wu_vs, L2_gnn_Lu_s, L2_gnn_Lu_v, L3_gnn_gamma_s, L3_gnn_beta_s, L3_gnn_gamma_v, L3_gnn_Ws_src, L3_gnn_Wv_src, L3_gnn_Ws_dst, L3_gnn_Wv_dst, L3_gnn_W_rbf, L3_gnn_W_alpha, L3_gnn_alpha_dot, L3_gnn_Ws_val, L3_gnn_Wv_val, L3_gnn_Wg, L3_gnn_w2_ss, L3_gnn_w2_sv, L3_gnn_w2_vs, L3_gnn_w2_vv0, L3_gnn_w2_vv1, L3_gnn_Ws_vlin, L3_gnn_Wv_vlin, L3_gnn_Wps, L3_gnn_Wpv):
    import jax
    import jax.numpy as jnp

    def _L0_gnn_ref(node_input, node_attr, edge_src, edge_dst, edge_attr, edge_features, W_sc0, W_sc1, W_l1_0, W_l1_1, W_fc1, W_fc2, W_l2_0, W_l2_1):
        import jax, jax.numpy as jnp
        import numpy as np
        N = 3125
        E = 25000
        MUL0 = 64
        MUL1 = 32
        NEF = 12
        RN = 100
        NUM_NEIGHBORS = 8.0
        WNUM = MUL0 + MUL0 + MUL1 + MUL1

        def _split(x):
            return (x[:, :MUL0], x[:, MUL0:].reshape(-1, MUL1, 3))

        def _fctp_scalar_attr(x0, x1, z, Ws, Wv):
            s = x0 @ Ws * z / np.sqrt(Ws.shape[0])
            v = jnp.einsum('nuc,uw->nwc', x1, Wv) * z[:, :, None] / np.sqrt(Wv.shape[0])
            return (s, v)
        x0, x1 = _split(node_input)
        z = node_attr
        s0, s1 = _fctp_scalar_attr(x0, x1, z, W_sc0, W_sc1)
        h0, h1 = _fctp_scalar_attr(x0, x1, z, W_l1_0, W_l1_1)
        h = jax.nn.silu(edge_features @ W_fc1 / np.sqrt(NEF))
        w = h @ W_fc2 / np.sqrt(RN)
        w0 = w[:, :MUL0]
        w1 = w[:, MUL0:2 * MUL0]
        w2 = w[:, 2 * MUL0:2 * MUL0 + MUL1]
        w3 = w[:, 2 * MUL0 + MUL1:]
        e0 = h0[edge_src]
        e1 = h1[edge_src]
        y0 = edge_attr[:, :1]
        y1 = edge_attr[:, 1:]
        m0a = w0 * e0 * y0
        m0b = w3 * jnp.einsum('eui,ei->eu', e1, y1) / np.sqrt(3.0)
        m1a = (w1 * e0)[:, :, None] * y1[:, None, :]
        m1b = w2[:, :, None] * (e1 * y0[:, :, None])
        mid_s = jnp.concatenate([m0a, m0b], axis=1)
        mid_v = jnp.concatenate([m1a, m1b], axis=1)
        inv = 1.0 / np.sqrt(NUM_NEIGHBORS)
        ns = jax.ops.segment_sum(mid_s, edge_dst, num_segments=N) * inv
        nv = jax.ops.segment_sum(mid_v, edge_dst, num_segments=N) * inv
        o0, o1 = _fctp_scalar_attr(ns, nv, z, W_l2_0, W_l2_1)
        c_s, c_x = (np.sin(np.pi / 8), np.cos(np.pi / 8))
        out0 = c_s * s0 + c_x * o0
        out1 = c_s * s1 + c_x * o1
        return jnp.concatenate([out0, out1.reshape(N, -1)], axis=1)

    def _L1_gnn_ref(node_features, edge_index, edge_attr_tensor, node_attr_scalar_raw, W1, W2, W3, W4, Wm, bm, Wu, bu):
        import jax, jax.numpy as jnp
        import numpy as np
        MUL0_N, MUL1_N = (64, 32)
        MUL0_E, MUL1_E = (8, 8)
        MUL0_H, MUL1_H = (64, 32)
        N_NODES, N_EDGES = (3125, 50000)
        D_NODE = MUL0_N + 3 * MUL1_N
        D_EDGE = MUL0_E + 3 * MUL1_E
        D_HID = MUL0_H + 3 * MUL1_H

        def _split(x, mul0, mul1):
            s = x[..., :mul0]
            v = x[..., mul0:].reshape(x.shape[0], mul1, 3)
            return (s, v)

        def fctp_messages(x, e, W1, W2, W3, W4):
            xs, xv = _split(x, MUL0_N, MUL1_N)
            es, ev = _split(e, MUL0_E, MUL1_E)
            inv_sqrt2 = 1.0 / np.sqrt(2.0)
            s1 = jnp.einsum('ea,eb,abc->ec', xs, es, W1) * (1.0 / np.sqrt(MUL0_N * MUL0_E))
            s2 = jnp.einsum('eai,ebi,abc->ec', xv, ev, W2) * (1.0 / (np.sqrt(3.0) * np.sqrt(MUL1_N * MUL1_E)))
            out_s = (s1 + s2) * inv_sqrt2
            v1 = jnp.einsum('ea,ebi,abc->eci', xs, ev, W3) * (1.0 / np.sqrt(MUL0_N * MUL1_E))
            v2 = jnp.einsum('eai,eb,abc->eci', xv, es, W4) * (1.0 / np.sqrt(MUL1_N * MUL0_E))
            out_v = (v1 + v2) * inv_sqrt2
            return jnp.concatenate([out_s, out_v.reshape(out_v.shape[0], -1)], axis=-1)
        row, col = (edge_index[0], edge_index[1])
        tp = fctp_messages(node_features[col], edge_attr_tensor, W1, W2, W3, W4)
        messages = tp @ Wm + bm
        agg = jax.ops.segment_sum(messages, row, num_segments=N_NODES)
        upd = jnp.concatenate([node_features, agg], axis=-1) @ Wu + bu
        return node_features + upd

    def _L2_gnn_ref(node_features, edge_index, edge_attr_tensor, node_attr_scalar_raw, Wm_ss, Wm_vv, Wm_sv, Wm_vs, Lm_s, Lm_v, Wu_ss, Wu_vv, Wu_sv, Wu_vs, Lu_s, Lu_v):
        import jax, jax.numpy as jnp
        import numpy as np
        N = 1250
        E = 40000
        INV_SQRT3 = 0.5773502691896258
        INV8 = 0.125
        INV_SQRT32 = 0.17677669529663687
        INV64 = 0.015625
        INV32 = 0.03125
        INV_SQRT2048 = 0.022097086912079608
        n = node_features.shape[0]
        e = edge_attr_tensor.shape[0]
        row, col = (edge_index[0], edge_index[1])
        r_vec = edge_attr_tensor[:, :3]
        dist = edge_attr_tensor[:, 3:4]
        xj = node_features[col]
        s = xj[:, :64]
        v = xj[:, 64:].reshape(e, 32, 3)
        m0 = s @ Wm_ss * dist * INV8 + jnp.einsum('eui,ei->eu', v, r_vec) @ Wm_vv * (INV_SQRT3 * INV_SQRT32)
        m1 = (s @ Wm_sv)[:, :, None] * r_vec[:, None, :] * INV8 + jnp.einsum('eui,uw->ewi', v, Wm_vs) * dist[:, :, None] * INV_SQRT32
        m0 = m0 + s @ Lm_s * INV8
        m1 = m1 + jnp.einsum('eui,uw->ewi', v, Lm_v) * INV_SQRT32
        msg = jnp.concatenate([m0, m1.reshape(e, 96)], axis=-1)
        agg = jax.ops.segment_sum(msg, row, num_segments=n)
        a0 = agg[:, :64]
        a1 = agg[:, 64:].reshape(n, 32, 3)
        xs = node_features[:, :64]
        xv = node_features[:, 64:].reshape(n, 32, 3)
        u0 = jnp.einsum('nu,nv,uvw->nw', xs, a0, Wu_ss) * INV64 + jnp.einsum('nui,nvi,uvw->nw', xv, a1, Wu_vv) * (INV_SQRT3 * INV32)
        u1 = jnp.einsum('nu,nvi,uvw->nwi', xs, a1, Wu_sv) * INV_SQRT2048 + jnp.einsum('nui,nv,uvw->nwi', xv, a0, Wu_vs) * INV_SQRT2048
        u0 = u0 + xs @ Lu_s * INV8
        u1 = u1 + jnp.einsum('nui,uw->nwi', xv, Lu_v) * INV_SQRT32
        upd = jnp.concatenate([u0, u1.reshape(n, 96)], axis=-1)
        return node_features + upd

    def _L3_gnn_ref(node, rbf, rsh, gamma_s, beta_s, gamma_v, Ws_src, Wv_src, Ws_dst, Wv_dst, W_rbf, W_alpha, alpha_dot, Ws_val, Wv_val, Wg, w2_ss, w2_sv, w2_vs, w2_vv0, w2_vv1, Ws_vlin, Wv_vlin, Wps, Wpv, edge_index):
        import jax, jax.numpy as jnp
        import numpy as np
        N, E = (1250, 20000)
        CS, CV = (64, 32)
        AS_, AV, H = (16, 8, 4)
        NB = 16
        SQRT3 = 1.7320508075688772
        SQRT2 = 1.4142135623730951
        EPS = 1e-05

        def _cg_tp(s, v, y0, y1, w_ss, w_sv, w_vs, w_vv0, w_vv1):
            out_s = jnp.concatenate([w_ss * s * y0[:, None], w_vv0 * (jnp.einsum('eci,ei->ec', v, y1) / SQRT3)], axis=-1)
            out_v = jnp.concatenate([(w_sv * s)[:, :, None] * y1[:, None, :], (w_vs * jnp.ones_like(v[..., 0]))[..., None] * v * y0[:, None, None], (w_vv1 * jnp.ones_like(v[..., 0]))[..., None] * (jnp.cross(v, y1[:, None, :]) / SQRT2)], axis=1)
            return (out_s, out_v)

        def _equiv_layernorm(s, v, gamma_s, beta_s, gamma_v):
            mu = jnp.mean(s, axis=-1, keepdims=True)
            var = jnp.var(s, axis=-1, keepdims=True)
            s_n = (s - mu) * jax.lax.rsqrt(var + EPS) * gamma_s + beta_s
            rms = jnp.sqrt(jnp.mean(jnp.sum(v * v, axis=-1), axis=-1, keepdims=True) + EPS)
            v_n = v / rms[..., None] * gamma_v[None, :, None]
            return (s_n, v_n)
        n = node.shape[0]
        e = rsh.shape[0]
        s = node[:, :CS]
        v = node[:, CS:].reshape(n, CV, 3)
        s_n, v_n = _equiv_layernorm(s, v, gamma_s, beta_s, gamma_v)
        src, dst = (edge_index[0], edge_index[1])
        msg_s = (s_n @ Ws_src)[src] + (s_n @ Ws_dst)[dst]
        msg_v = jnp.einsum('ncx,cd->ndx', v_n, Wv_src)[src] + jnp.einsum('ncx,cd->ndx', v_n, Wv_dst)[dst]
        y0, y1 = (rsh[:, 0], rsh[:, 1:4])
        w1 = rbf @ W_rbf
        m1_s, m1_v = _cg_tp(msg_s, msg_v, y0, y1, w1[:, :CS], w1[:, CS:2 * CS], w1[:, 2 * CS:2 * CS + CV], w1[:, 2 * CS + CV:2 * CS + 2 * CV], w1[:, 2 * CS + 2 * CV:])
        a = (m1_s @ W_alpha).reshape(e, H, AS_)
        a = jnp.where(a > 0, a, 0.2 * a)
        a = jnp.sum(a * alpha_dot, axis=-1, keepdims=True)
        amax = jax.ops.segment_max(a, dst, num_segments=n)
        amax = jnp.where(jnp.isfinite(amax), amax, 0.0)
        ex = jnp.exp(a - amax[dst])
        den = jax.ops.segment_sum(ex, dst, num_segments=n)
        alpha = ex / (den[dst] + 1e-16)
        val_s = m1_s @ Ws_val
        val_v = jnp.einsum('ecx,cd->edx', m1_v, Wv_val)
        val_v = val_v * jax.nn.sigmoid(val_s @ Wg)[..., None]
        val_s = jax.nn.sigmoid(val_s)
        m2_s, m2_v = _cg_tp(val_s, val_v, y0, y1, w2_ss, w2_sv, w2_vs, w2_vv0, w2_vv1)
        hs = (m2_s @ Ws_vlin).reshape(e, H, AS_)
        hv = jnp.einsum('ecx,cd->edx', m2_v, Wv_vlin).reshape(e, H, AV, 3)
        h = jnp.concatenate([hs, hv.reshape(e, H, AV * 3)], axis=-1)
        agg = jax.ops.segment_sum(alpha * h, dst, num_segments=n)
        agg_s = agg[:, :, :AS_].reshape(n, H * AS_)
        agg_v = agg[:, :, AS_:].reshape(n, H * AV, 3)
        out = node + jnp.concatenate([agg_s @ Wps, jnp.einsum('ncx,cd->ndx', agg_v, Wpv).reshape(n, CV * 3)], axis=-1)
        return out
    edge_index = jnp.stack([src, dst])
    h = jnp.maximum(_layernorm(x, axis=-1), 0.0)
    x = x + _L0_gnn_ref(h, node_vec1, src, dst, edge_attr_4, edge_attr_12, L0_gnn_W_sc0, L0_gnn_W_sc1, L0_gnn_W_l1_0, L0_gnn_W_l1_1, L0_gnn_W_fc1, L0_gnn_W_fc2, L0_gnn_W_l2_0, L0_gnn_W_l2_1)
    h = jnp.maximum(_layernorm(x, axis=-1), 0.0)
    x = x + _L1_gnn_ref(h, edge_index, edge_attr_32, node_vec1, L1_gnn_W1, L1_gnn_W2, L1_gnn_W3, L1_gnn_W4, L1_gnn_Wm, L1_gnn_bm, L1_gnn_Wu, L1_gnn_bu)
    h = jnp.maximum(_layernorm(x, axis=-1), 0.0)
    x = x + _L2_gnn_ref(h, edge_index, edge_attr_4, node_vec1, L2_gnn_Wm_ss, L2_gnn_Wm_vv, L2_gnn_Wm_sv, L2_gnn_Wm_vs, L2_gnn_Lm_s, L2_gnn_Lm_v, L2_gnn_Wu_ss, L2_gnn_Wu_vv, L2_gnn_Wu_sv, L2_gnn_Wu_vs, L2_gnn_Lu_s, L2_gnn_Lu_v)
    h = jnp.maximum(_layernorm(x, axis=-1), 0.0)
    x = x + _L3_gnn_ref(h, edge_attr_16, edge_attr_4, L3_gnn_gamma_s, L3_gnn_beta_s, L3_gnn_gamma_v, L3_gnn_Ws_src, L3_gnn_Wv_src, L3_gnn_Ws_dst, L3_gnn_Wv_dst, L3_gnn_W_rbf, L3_gnn_W_alpha, L3_gnn_alpha_dot, L3_gnn_Ws_val, L3_gnn_Wv_val, L3_gnn_Wg, L3_gnn_w2_ss, L3_gnn_w2_sv, L3_gnn_w2_vs, L3_gnn_w2_vv0, L3_gnn_w2_vv1, L3_gnn_Ws_vlin, L3_gnn_Wv_vlin, L3_gnn_Wps, L3_gnn_Wpv, edge_index)
    return x

_drawn_inputs = setup_inputs


def setup_inputs(seed=0):
    import zlib

    import numpy as np

    out = dict(_drawn_inputs(seed))
    spreads = {'L1_gnn_bm': (0.0, 0.1),
     'L1_gnn_bu': (0.0, 0.1),
     'L3_gnn_gamma_s': (1.0, 0.2),
     'L3_gnn_beta_s': (0.0, 0.1),
     'L3_gnn_gamma_v': (1.0, 0.2)}
    factors = {}
    for name, (base, spread) in spreads.items():
        noise = np.random.default_rng([zlib.crc32(name.encode()), seed]).standard_normal(out[name].shape)
        drawn = base * np.exp(spread * noise) if base else spread * noise
        out[name] = jnp.asarray(drawn.astype(out[name].dtype))
    for name, factor in factors.items():
        out[name] = (out[name] * factor).astype(out[name].dtype)
    return out
```

```python
import itertools
from contextlib import ExitStack

import numpy as np

import concourse.bass as bass
from concourse import mybir

ALU = mybir.AluOpType
ACT = mybir.ActivationFunctionType
AX = mybir.AxisListType
F32 = mybir.dt.float32
F16 = mybir.dt.float16
I32 = mybir.dt.int32
U32 = mybir.dt.uint32

P = 128
N = 3125
E = 103125
D = 160
CS, CV = 64, 32
NB = -(-N // P)
NP = NB * P
LN_EPS = 1e-5

TPC = 28
CHUNK = P * TPC
NCH = -(-E // CHUNK)
NT = NCH * TPC
TAIL = E - (NCH - 1) * CHUNK
TAIL_P, TAIL_R = divmod(TAIL, TPC)

G = 8
BINS_D = NB
BINS_S = -(-N // G)
ALL_D = BINS_D + 1
ALL_S = BINS_S + 1
BINS = ALL_S + ALL_D
QUAD = 4
QUADS_D = -(-((E + BINS_D * (QUAD * P - 1)) // (QUAD * P)) // 2) * 2
SLOTS_D = QUADS_D * QUAD
BATCH_S = 16
SLOTS_S = -(-((E + BINS_S * (P - 1)) // P) // BATCH_S) * BATCH_S
PADS = -(-(NT * P - E) // P) + 1
ROWS_D = (SLOTS_D + max(PADS, 4 * QUAD)) * P
ROWS_S = (SLOTS_S + max(PADS, BATCH_S)) * P

D_SRC, D_LOC, D_E4, D_AGAIN, D_E12, D_E16 = 0, 1, 2, 6, 8, 20
WORDS_D = 36
PAIR = 2
PW = PAIR * WORDS_D
S_DST, S_LOC, S_E4, S_E32 = 0, 1, 2, 6
WORDS_S = 38


class Semaphores:

    stages = itertools.count()

    def __init__(self, nc):
        self.nc, self.handles, self.stage = nc, [], next(self.stages)

    def __enter__(self):
        return self

    def __call__(self, name):
        self.handles.append(self.nc.alloc_semaphore(name=f"{name}_{self.stage}"))
        return self.handles[-1]

    def __exit__(self, *error):
        if error[0] is None:
            self.nc.clear_and_free_semaphores(self.handles)
            self.nc.all_engine_barrier()


class Steps:

    def __init__(self, eng, sem, per=0, base=0):
        self.eng, self.sem, self.per, self.base, self.turn, self.k = eng, sem, per, base, None, 0

    def begin(self, turn):
        self.turn, self.k = turn, 0

    def done(self, ins):
        ins.then_inc(self.sem, 1)
        self.k += 1
        return self.k

    def value(self, k):
        return self.base + k if self.turn is None else self.turn * self.per + (self.base + k)

    def after(self, k=None):
        self.eng.wait_ge(self.sem, self.value(self.k if k is None else k))

    def link(self, ins):
        self.done(ins)
        self.after()

    def end(self):
        assert self.turn is None or self.k == self.per, (self.k, self.per)


def free(ap, *dims):
    return bass.AP(ap.tensor, ap.offset, [list(ap.ap[0])] + [list(d) for d in dims])


def by_part(v, axis_i):
    return v[..., CS + axis_i:D:3]


def stage_setup(nc, A, K):
    with ExitStack() as ctx:
        sb = lambda n, s, d=F32: ctx.enter_context(nc.sbuf_tensor(n, s, d))
        sem = ctx.enter_context(Semaphores(nc))
        raw = sb("x_raw", [P, NB, D])
        zero = sb("zero_rows", [P, 2048])
        x_in, cleared, x_padded, dve_steps, zeros_written, iota_done = (
            sem("x_in"), sem("cleared"), sem("x_padded"), sem("dve_steps"), sem("zeros_written"), sem("iota_done"))
        last = N - (NB - 1) * P
        with nc.Block() as block:
            @block.sync
            def _(sp):
                sp.wait_ge(x_padded, 1)
                sp.dma_start(raw[:, 0:NB - 1, :], A["x"][0:(NB - 1) * P, :].rearrange("(b p) f -> p b f", p=P)).then_inc(x_in, 16)
                sp.dma_start(raw[0:last, NB - 1, :], A["x"][(NB - 1) * P:N, :]).then_inc(x_in, 16)
                sp.dma_start(K["z"][:, 0:NB - 1], A["node_vec1"][0:(NB - 1) * P, :].rearrange("(b p) o -> p (b o)", p=P), allow_slow_non_contiguous=True).then_inc(x_in, 16)
                sp.dma_start(K["z"][0:last, NB - 1:NB], A["node_vec1"][(NB - 1) * P:N, :]).then_inc(x_in, 16)
                sp.wait_ge(x_in, 64)

            @block.scalar
            def _(act):
                act.wait_ge(cleared, 1)
                n = 0
                for buf, words in ((K["rows_d"], WORDS_D), (K["rows_s"], WORDS_S)):
                    flat = buf.rearrange("(p r) w -> p (r w)", p=P)
                    total = flat.shape[1]
                    for at in range(0, total, 2048):
                        w = min(2048, total - at)
                        act.dma_start(flat[:, at:at + w], zero[:, 0:w]).then_inc(zeros_written, 16)
                        n += 16
                act.wait_ge(zeros_written, n)

            @block.gpsimd
            def _(pool):
                st = Steps(pool, iota_done)
                st.done(nc.gpsimd.iota(K["iota_i"][:, :], pattern=[[1, 512]], base=0, channel_multiplier=0))
                st.done(nc.gpsimd.iota(K["part_i"][:, :], pattern=[[0, 1]], base=0, channel_multiplier=1))
                st.done(nc.gpsimd.iota(K["slot_i"][:, :], pattern=[[P, 10]], base=0, channel_multiplier=1))

            @block.vector
            def _(dve):
                v = Steps(dve, dve_steps)
                nc.vector.memset(raw[:, NB - 1, :], 0.0)
                nc.vector.memset(K["z"][:, NB - 1:NB], 0.0).then_inc(x_padded, 1)
                nc.vector.memset(zero[:, :], 0.0).then_inc(cleared, 1)
                dve.wait_ge(iota_done, 3)
                v.done(nc.vector.tensor_copy(K["iota_f"][:, :], K["iota_i"][:, :]))
                v.done(nc.vector.tensor_copy(K["part_f"][:, :], K["part_i"][:, :]))
                v.done(nc.vector.tensor_copy(K["slot_f"][:, :], K["slot_i"][:, :]))
                v.link(nc.vector.tensor_copy(K["iota_h"][:, :], K["iota_i"][:, :]))
                v.done(nc.vector.tensor_scalar(K["ident"][:, :], K["iota_f"][:, 0:P], K["part_f"][:, 0:1], None, ALU.is_equal))
                v.done(nc.vector.tensor_scalar(K["lower_h"][:, :], K["iota_f"][:, 0:P], K["part_f"][:, 0:1], None, ALU.is_gt))
                v.done(nc.vector.memset(K["ones_h"][:, :], 1.0))
                v.done(nc.vector.memset(K["slotsize_h"][:, :], float(P)))
                v.done(nc.vector.tensor_scalar(K["part1_f"][:, :], K["part_f"][:, :], 1.0, None, ALU.add))
                dve.wait_ge(x_in, 64)
                v.done(nc.vector.tensor_copy(K["X"][:, :, 0:CS], raw[:, :, 0:CS]))
                for i in range(3):
                    v.done(nc.vector.tensor_copy(K["X"][:, :, CS + CV * i:CS + CV * (i + 1)], by_part(raw, i)))
                v.after()


def stage_sort(nc, A, K):
    with ExitStack() as ctx:
        sb = lambda n, s, d=F32: ctx.enter_context(nc.sbuf_tensor(n, s, d))
        sem = ctx.enter_context(Semaphores(nc))
        src = sb("src_i", [P, NCH, TPC], I32)
        dst = sb("dst_i", [P, NCH, TPC], I32)
        key_i = sb("key_i", [P, NT], I32)
        key_s = sb("key_s", [P, NT])
        key_d = sb("key_d", [P, NT])
        loc_i = sb("loc_i", [P, NT], I32)
        loc_s = sb("loc_s", [P, NT])
        loc_d = sb("loc_d", [P, NT])
        onehot = sb("onehot", [P, 4, BINS], F16)
        before = sb("before", [P, 4, BINS], F16)
        total = sb("total", [P, BINS])
        slots_i = sb("slots_i", [P, BINS], I32)
        slots = sb("slots", [P, BINS])
        upto = sb("upto", [P, BINS])
        start_h = sb("start_h", [1, BINS], F16)
        junk = sb("junk", [P, 4, BINS], F16)
        bin_f = sb("bin_f", [P, 20])
        bin_i = sb("bin_i", [P, 20], I32)
        ea4 = sb("ea4", [P, 2, TPC, 4])
        ea12 = sb("ea12", [P, 2, TPC, 12])
        ea16 = sb("ea16", [P, 2, TPC, 16])
        ea32 = sb("ea32", [P, 2, TPC, 32])
        row_d = sb("row_d", [P, 2, TPC, WORDS_D])
        row_s = sb("row_s", [P, 2, TPC, WORDS_S])
        pos = sb("pos", [P, 2, 2, TPC])
        pos_i = sb("pos_i", [P, 2, 2, TPC], I32)
        zero_h = sb("zero_h", [P, BINS], F16)
        hist = ctx.enter_context(nc.psum_tensor("hist", [P, 512], F32))
        rank = ctx.enter_context(nc.psum_tensor("rank", [P, 4, 512], F32))
        RS, RD = slice(0, ALL_S), slice(ALL_S, BINS)

        keys_in, keys_padded, keys_ready, dve_steps = sem("keys_in"), sem("keys_padded"), sem("keys_ready"), sem("dve_steps")
        hist_hot, hist_added, hist_done = sem("hist_hot"), sem("hist_added"), sem("hist_done")
        bins_out = sem("bins_out")
        with nc.Block() as block:
            @block.sync
            def _(sp):
                sp.wait_ge(keys_padded, 2)
                for name, tile in (("src", src), ("dst", dst)):
                    a = A[name]
                    sp.dma_start(tile[:, 0:NCH - 1, :], a[0:(NCH - 1) * CHUNK].rearrange("(c p t) -> p c t", p=P, t=TPC)).then_inc(keys_in, 16)
                    at = (NCH - 1) * CHUNK
                    sp.dma_start(tile[0:TAIL_P, NCH - 1, :], a[at:at + TAIL_P * TPC].rearrange("(p t) -> p t", t=TPC)).then_inc(keys_in, 16)
                    sp.dma_start(tile[TAIL_P:TAIL_P + 1, NCH - 1, 0:TAIL_R], a[at + TAIL_P * TPC:E].rearrange("(p t) -> p t", p=1)).then_inc(keys_in, 16)
                sp.wait_ge(bins_out, 32)

            @block.vector
            def _(dve):
                v = Steps(dve, dve_steps)
                nc.vector.memset(src[:, NCH - 1, :], BINS_S * G).then_inc(keys_padded, 1)
                nc.vector.memset(dst[:, NCH - 1, :], BINS_D * P).then_inc(keys_padded, 1)
                v.done(nc.vector.memset(zero_h[:, :], 0.0))
                v.done(nc.vector.memset(before[:, 0, :], 0.0))
                dve.wait_ge(keys_in, 96)
                flat = lambda t: t[:, :, :].rearrange("p c t -> p (c t)")
                sG, sP = G.bit_length() - 1, P.bit_length() - 1
                v.done(nc.vector.tensor_scalar(key_i[:, :], flat(src), sG, None, ALU.arith_shift_right))
                v.done(nc.vector.tensor_scalar(loc_i[:, :], flat(src), G - 1, None, ALU.bitwise_and))
                v.after()
                v.done(nc.vector.tensor_copy(key_s[:, :], key_i[:, :]))
                v.done(nc.vector.tensor_scalar(loc_s[:, :], loc_i[:, :], 1.0, None, ALU.add))
                v.after()
                v.done(nc.vector.scalar_tensor_tensor(loc_s[:, :], key_s[:, :], float(BINS_S), loc_s[:, :], ALU.is_lt, ALU.mult))
                v.done(nc.vector.tensor_scalar(key_i[:, :], flat(dst), sP, None, ALU.arith_shift_right))
                v.done(nc.vector.tensor_scalar(loc_i[:, :], flat(dst), P - 1, None, ALU.bitwise_and))
                v.after()
                v.done(nc.vector.tensor_copy(key_d[:, :], key_i[:, :]))
                v.done(nc.vector.tensor_scalar(loc_d[:, :], loc_i[:, :], 1.0, None, ALU.add))
                v.after()
                v.done(nc.vector.scalar_tensor_tensor(loc_d[:, :], key_d[:, :], float(BINS_D), loc_d[:, :], ALU.is_lt, ALU.mult))
                v.done(nc.vector.tensor_scalar(flat(dst), flat(dst), float(NP - 1), None, ALU.min))
                v.after()
                nc.vector.memset(junk[:, 2, 0:1], 0.0).then_inc(keys_ready, 1)
                with dve.Fori(0, NT // 4) as i:
                    for k in range(4):
                        dve.wait_ge(hist_added, 4 * i + k + 1)
                        t = 4 * i + k
                        nc.vector.tensor_scalar(onehot[:, k, RS], K["iota_h"][:, 0:ALL_S], key_s[:, bass.ds(t, 1)], None, ALU.is_equal)
                        nc.vector.tensor_scalar(onehot[:, k, RD], K["iota_h"][:, 0:ALL_D], key_d[:, bass.ds(t, 1)], None, ALU.is_equal).then_inc(hist_hot, 1)
                dve.wait_ge(hist_done, 1)
                sQ = (QUAD * P).bit_length() - 1
                v.done(nc.vector.tensor_scalar(slots_i[:, RS], hist[:, RS], float(P - 1), None, ALU.add))
                v.link(nc.vector.tensor_scalar(slots_i[:, RD], hist[:, RD], float(QUAD * P - 1), None, ALU.add))
                v.done(nc.vector.tensor_scalar(slots_i[:, RS], slots_i[:, RS], sP, None, ALU.arith_shift_right))
                v.link(nc.vector.tensor_scalar(slots_i[:, RD], slots_i[:, RD], sQ, None, ALU.arith_shift_right))
                v.link(nc.vector.tensor_copy(slots[:, :], slots_i[:, :]))
                v.link(nc.vector.tensor_scalar(slots[:, RD], slots[:, RD], float(QUAD), None, ALU.mult))
                v.done(nc.vector.memset(total[:, :], 0.0))
                v.after()
                v.done(nc.vector.tensor_tensor_scan(upto[:, RS], slots[:, RS], total[:, RS], 0.0, ALU.add, ALU.add))
                v.link(nc.vector.tensor_tensor_scan(upto[:, RD], slots[:, RD], total[:, RD], 0.0, ALU.add, ALU.add))
                v.done(nc.vector.tensor_tensor(start_h[0:1, :], upto[0:1, :], slots[0:1, :], ALU.subtract))
                for c in range(10):
                    v.link(nc.vector.tensor_scalar(junk[:, 0, 0:BINS_S], upto[:, 0:BINS_S], K["slot_f"][:, c:c + 1], None, ALU.is_le, ALU.add, accum_out=bin_f[:, c:c + 1]))
                    v.link(nc.vector.tensor_scalar(junk[:, 1, 0:BINS_D], upto[:, ALL_S:ALL_S + BINS_D], K["slot_f"][:, c:c + 1], None, ALU.is_le, ALU.add, accum_out=bin_f[:, 10 + c:11 + c]))
                v.done(nc.vector.tensor_scalar(bin_i[:, 0:10], bin_f[:, 0:10], float(BINS_S - 1), float(G), ALU.min, ALU.mult))
                v.done(nc.vector.tensor_scalar(bin_i[:, 10:20], bin_f[:, 10:20], float(BINS_D - 1), None, ALU.min))
                v.after()
                nc.vector.memset(junk[:, 2, 0:1], 0.0).then_inc(keys_ready, 1)

            @block.tensor
            def _(pe):
                pe.wait_ge(keys_ready, 1)
                nc.tensor.matmul(hist[:, 0:BINS], zero_h[:, 0:P], zero_h[:, :], start=True, stop=False, skip_group_check=True).then_inc(hist_added, 4)
                with pe.Fori(0, NT // 4) as i:
                    for k in range(4):
                        pe.wait_ge(hist_hot, 4 * i + k + 1)
                        nc.tensor.matmul(hist[:, 0:BINS], K["ones_h"][:, :], onehot[:, k, :], start=False, stop=False, skip_group_check=True).then_inc(hist_added, 1)
                nc.tensor.matmul(hist[:, 0:BINS], zero_h[:, 0:P], zero_h[:, :], start=False, stop=True, skip_group_check=True).then_inc(hist_done, 1)

            @block.scalar
            def _(act):
                act.wait_ge(keys_ready, 2)
                act.dma_start(K["bins_s"].rearrange("(c p) -> p c", p=P), bin_i[:, 0:10], allow_slow_non_contiguous=True).then_inc(bins_out, 16)
                act.dma_start(K["bins_d"].rearrange("(c p) -> p c", p=P), bin_i[:, 10:20], allow_slow_non_contiguous=True).then_inc(bins_out, 16)

        with ExitStack() as ctx2:
            sem2 = ctx2.enter_context(Semaphores(nc))
            attr_in = [sem2(f"attr_in{k}") for k in range(2)]
            rows_sent = [sem2(f"rows_sent{k}") for k in range(2)]
            rows_built, hot, ranked, placed, pos_ready, pool_seen, sent = (
                sem2("rows_built"), sem2("hot"), sem2("ranked"), sem2("placed"), sem2("pos_ready"), sem2("pool_seen"), sem2("sent"))
            attrs = (("edge_attr_4", ea4, 4), ("edge_attr_12", ea12, 12), ("edge_attr_16", ea16, 16), ("edge_attr_32", ea32, 32))
            PAIRS = (NCH - 1) // 2
            SENT = 16 * 2 * TPC
            assert NCH == 2 * PAIRS + 1
            with nc.Block() as block:
                @block.sync
                def _(sp):
                    with sp.Fori(0, PAIRS) as i:
                        for k in range(2):
                            sp.wait_ge(rows_built, 2 * i + (k + 1))
                            for name, tile, w in attrs:
                                a = A[name].rearrange("e w -> (e w)")
                                sp.dma_start(tile[:, k, :, :].rearrange("p t w -> p (t w)"),
                                             a[bass.ds((2 * i + k) * (CHUNK * w), CHUNK * w)].rearrange("(p f) -> p f", p=P)).then_inc(attr_in[k], 16)
                    sp.wait_ge(rows_built, NCH)
                    for name, tile, w in attrs:
                        a = A[name].rearrange("e w -> (e w)")
                        at = (NCH - 1) * CHUNK * w
                        mid = at + TAIL_P * TPC * w
                        sp.dma_start(tile[0:TAIL_P, 0, :, :].rearrange("p t w -> p (t w)"), a[at:mid].rearrange("(p f) -> p f", p=TAIL_P)).then_inc(attr_in[0], 16)
                        sp.dma_start(tile[TAIL_P:TAIL_P + 1, 0, 0:TAIL_R, :].rearrange("p t w -> p (t w)"), a[mid:E * w].rearrange("(p f) -> p f", p=1)).then_inc(attr_in[0], 16)

                @block.scalar
                def _(act):
                    act.sem_inc(rows_built, 2)

                    def rows(c, k, loaded):
                        act.wait_ge(sent, c + 1)
                        act.wait_ge(attr_in[k], loaded)
                        cols = bass.ds(c * TPC, TPC)
                        d, s = row_d[:, k], row_s[:, k]
                        of = lambda t: t[:, bass.ds(c, 1), :].rearrange("p c t -> p (c t)")
                        nc.scalar.copy(d[:, :, D_SRC].bitcast(I32), of(src))
                        nc.scalar.copy(d[:, :, D_LOC], loc_d[:, cols])
                        nc.scalar.copy(d[:, :, D_E4:D_E4 + 4], ea4[:, k])
                        nc.scalar.copy(d[:, :, D_AGAIN:D_AGAIN + 2], ea4[:, k, :, 1:3])
                        nc.scalar.copy(d[:, :, D_E12:D_E12 + 12], ea12[:, k])
                        nc.scalar.copy(d[:, :, D_E16:D_E16 + 16], ea16[:, k])
                        nc.scalar.copy(s[:, :, S_DST].bitcast(I32), of(dst))
                        nc.scalar.copy(s[:, :, S_LOC], loc_s[:, cols])
                        nc.scalar.copy(s[:, :, S_E4:S_E4 + 4], ea4[:, k])
                        nc.scalar.copy(s[:, :, S_E32:S_E32 + 32], ea32[:, k]).then_inc(rows_built, 1)

                    with act.Fori(0, PAIRS) as i:
                        for k in range(2):
                            rows(2 * i + k, k, 64 * i + 64)
                    rows(NCH - 1, 0, 64 * PAIRS + 128)

                @block.vector
                def _(dve):
                    dve.sem_inc(placed, 4)

                    def chunk(c, k):
                        for t in range(TPC + 2):
                            if t < TPC:
                                b, tile = t % 4, c * TPC + t
                                nc.vector.tensor_scalar(onehot[:, b, RS], K["iota_h"][:, 0:ALL_S], key_s[:, bass.ds(tile, 1)], None, ALU.is_equal)
                                nc.vector.tensor_scalar(onehot[:, b, RD], K["iota_h"][:, 0:ALL_D], key_d[:, bass.ds(tile, 1)], None, ALU.is_equal).then_inc(hot, 1)
                                dve.wait_ge(hot, c * TPC + (t + 1))
                                nc.vector.tensor_tensor(before[:, (t + 1) % 4, :], before[:, b, :], onehot[:, b, :], ALU.add)
                            if t >= 2:
                                r = t - 2
                                b = r % 4
                                dve.wait_ge(ranked, c * TPC + (r + 1))
                                nc.vector.tensor_tensor_reduce(junk[:, b, RS], rank[:, b, RS], onehot[:, b, RS], 1.0, 0.0, ALU.mult, ALU.add, pos[:, k, 0, r:r + 1])
                                nc.vector.tensor_tensor_reduce(junk[:, b, RD], rank[:, b, RD], onehot[:, b, RD], 1.0, 0.0, ALU.mult, ALU.add, pos[:, k, 1, r:r + 1]).then_inc(placed, 1)
                        dve.wait_ge(sent, c + 1)
                        dve.wait_ge(placed, c * TPC + (TPC + 4))
                        nc.vector.tensor_copy(pos_i[:, k, :, :], pos[:, k, :, :]).then_inc(pos_ready, 1)

                    with dve.Fori(0, PAIRS) as i:
                        for k in range(2):
                            chunk(2 * i + k, k)
                    chunk(NCH - 1, 0)

                @block.tensor
                def _(pe):
                    with pe.Fori(0, NT // 4) as i:
                        for b in range(4):
                            pe.wait_ge(hot, 4 * i + b + 1)
                            pe.wait_ge(placed, 4 * i + b + 1)
                            nc.tensor.matmul(rank[:, b, 0:BINS], K["lower_h"][:, :], onehot[:, b, :], start=True, stop=False)
                            nc.tensor.matmul(rank[:, b, 0:BINS], K["ones_h"][:, :], before[:, b, :], start=False, stop=False)
                            nc.tensor.matmul(rank[:, b, 0:BINS], K["slotsize_h"][0:1, :], start_h[0:1, :], start=False, stop=True).then_inc(ranked, 1)

                @block.gpsimd
                def _(pool):
                    def scatter(c, k, before):
                        pool.wait_ge(pos_ready, c + 1)
                        pool.sem_inc(pool_seen, 1)
                        pool.wait_ge(rows_built, c + 3)
                        pool.sem_inc(pool_seen, 1)
                        for t in range(TPC):
                            for o, rows_, tile in ((0, K["rows_s"], row_s), (1, K["rows_d"], row_d)):
                                pool.indirect_dma_start(rows_, bass.IndirectOffsetOnAxis(ap=pos_i[:, k, o, t:t + 1].bitcast(U32), axis=0),
                                                        tile[:, k, t, :], None).then_inc(rows_sent[k], 16)
                            if t == 3 and before is not None:
                                pool.wait_ge(rows_sent[1 - k], before)
                                pool.sem_inc(sent, 1)

                    pool.sem_inc(sent, 2)
                    scatter(0, 0, None)
                    with pool.Fori(0, PAIRS) as i:
                        scatter(2 * i + 1, 1, SENT * i + SENT)
                        scatter(2 * i + 2, 0, SENT * i + SENT)
                    pool.wait_ge(rows_sent[0], SENT * (PAIRS + 1))


def consts(nc, ctx, A):
    sb = lambda n, s, d=F32: ctx.enter_context(nc.sbuf_tensor(n, s, d))
    K = {
        "X": sb("x_nodes", [P, NB, D]), "z": sb("node_attr", [P, NB]), "ident": sb("ident", [P, P]),
        "iota_i": sb("iota_i", [P, 512], I32), "iota_f": sb("iota_f", [P, 512]), "iota_h": sb("iota_h", [P, 512], F16),
        "part_i": sb("part_i", [P, 1], I32), "part_f": sb("part_f", [P, 1]), "part1_f": sb("part1_f", [P, 1]),
        "slot_i": sb("slot_i", [P, 10], I32), "slot_f": sb("slot_f", [P, 10]),
        "lower_h": sb("lower_h", [P, P], F16), "ones_h": sb("ones_h", [P, P], F16), "slotsize_h": sb("slotsize_h", [1, P], F16),
        "rows_d": nc.dram_tensor("rows_by_dst", [ROWS_D, WORDS_D], F32).ap(),
        "rows_s": nc.dram_tensor("rows_by_src", [ROWS_S, WORDS_S], F32).ap(),
        "table0": nc.dram_tensor("node_table0", [NP, D], F32).ap(),
        "table1": nc.dram_tensor("node_table1", [NP, D + 1], F32).ap(),
        "table2": nc.dram_tensor("node_table2", [NP, D + 1], F32).ap(),
        "h_turned": nc.dram_tensor("h_turned_l2", [D, NP], F32).ap(),
        "a_turned": nc.dram_tensor("sums_turned_l2", [D, NP], F32).ap(),
        "bins_s": nc.dram_tensor("bin_of_slot_s", [10 * P], I32).ap(),
        "bins_d": nc.dram_tensor("bin_of_slot_d", [10 * P], I32).ap(),
    }
    return K


def stage_norm(nc, K, H, tag):
    with ExitStack() as ctx:
        sb = lambda n, s, d=F32: ctx.enter_context(nc.sbuf_tensor(tag + "_" + n, s, d))
        sem = ctx.enter_context(Semaphores(nc))
        centred, square = sb("centred", [P, NB, D]), sb("square", [P, NB, D])
        mean, var, std, rstd, eps = (sb(n, [P, NB]) for n in ("ln_mean", "ln_var", "ln_std", "ln_rstd", "ln_eps"))
        steps, var_ready, std_ready = sem("norm_steps"), sem("var_ready"), sem("std_ready")
        over = lambda t: free(t[:, :], [1, NB], [0, D])
        with nc.Block() as block:
            @block.vector
            def _(dve):
                v = Steps(dve, steps)
                v.done(nc.vector.memset(eps[:, :], LN_EPS))
                v.link(nc.vector.tensor_reduce(mean[:, :], K["X"][:, :, :], AX.X, ALU.add))
                v.link(nc.vector.tensor_scalar(mean[:, :], mean[:, :], 1.0 / D, None, ALU.mult))
                v.link(nc.vector.tensor_tensor(centred[:, :, :], K["X"][:, :, :], over(mean), ALU.subtract))
                v.link(nc.vector.tensor_tensor(square[:, :, :], centred[:, :, :], centred[:, :, :], ALU.mult))
                nc.vector.tensor_reduce(var[:, :], square[:, :, :], AX.X, ALU.add).then_inc(var_ready, 1)
                dve.wait_ge(std_ready, 1)
                v.link(nc.vector.reciprocal(rstd[:, :], std[:, :]))
                v.link(nc.vector.tensor_tensor(square[:, :, :], centred[:, :, :], over(rstd), ALU.mult))
                v.link(nc.vector.tensor_scalar(H[:, :, :], square[:, :, :], 0.0, None, ALU.max))

            @block.scalar
            def _(act):
                act.wait_ge(var_ready, 1)
                nc.scalar.activation(std[:, :], var[:, :], ACT.Sqrt, bias=eps[:, 0:1], scale=1.0 / D).then_inc(std_ready, 1)


def stage_project(nc, K, H, W1, W2, scale, first, second, tag):
    dests = (first,) if second is None else (first, second)
    with ExitStack() as ctx:
        sb = lambda n, s, d=F32: ctx.enter_context(nc.sbuf_tensor(tag + "_" + n, s, d))
        sem = ctx.enter_context(Semaphores(nc))
        hb, ht1, ht2 = sb("h_block", [P, D]), sb("h_turned1", [P, P]), sb("h_turned2", [D - P, P])
        turn = ctx.enter_context(nc.psum_tensor(tag + "_" + "turn", [P, 512], F32))
        out = ctx.enter_context(nc.psum_tensor(tag + "_" + "proj", [P, 512], F32))
        taken, turned, copied, projected, stored = (sem(n) for n in ("taken", "turned", "copied", "projected", "stored"))
        with nc.Block() as block:
            @block.vector
            def _(dve):
                dve.sem_inc(stored, 1)
                with dve.Fori(0, NB) as b:
                    dve.wait_ge(turned, b + 1)
                    nc.vector.tensor_copy(hb[:, :], H[:, bass.ds(b, 1), :].rearrange("p o f -> p (o f)")).then_inc(taken, 1)
                    dve.wait_ge(projected, b + 2)
                    for n, dest in enumerate(dests):
                        to = dest[:, bass.ds(b, 1), :].rearrange("p o f -> p (o f)")
                        if scale is None:
                            ins = nc.vector.tensor_copy(to, out[:, n * D:(n + 1) * D])
                        else:
                            ins = nc.vector.tensor_scalar(to, out[:, n * D:(n + 1) * D], scale[:, bass.ds(b, 1)], None, ALU.mult)
                    ins.then_inc(stored, 1)

            @block.tensor
            def _(pe):
                pe.sem_inc(turned, 1)
                pe.sem_inc(projected, 1)
                with pe.Fori(0, NB) as b:
                    pe.wait_ge(taken, b + 1)
                    nc.tensor.transpose(turn[:, 0:P], hb[:, 0:P], K["ident"][:, :])
                    nc.tensor.transpose(turn[0:D - P, P:2 * P], hb[:, P:D], K["ident"][:, :]).then_inc(turned, 1)
                    pe.wait_ge(copied, b + 1)
                    pe.wait_ge(stored, b + 1)
                    nc.tensor.matmul(out[:, 0:len(dests) * D], ht1[:, :], W1[:, :], start=True, stop=False)
                    nc.tensor.matmul(out[:, 0:len(dests) * D], ht2[:, :], W2[:, :], start=False, stop=True).then_inc(projected, 1)

            @block.scalar
            def _(act):
                with act.Fori(0, NB) as b:
                    act.wait_ge(turned, b + 2)
                    act.wait_ge(projected, b + 1)
                    nc.scalar.copy(ht1[:, :], turn[:, 0:P])
                    nc.scalar.copy(ht2[:, :], turn[0:D - P, P:2 * P]).then_inc(copied, 1)


def stage_layer0(nc, A, K):
    SIN, COS = float(np.sin(np.pi / 8)), float(np.cos(np.pi / 8))
    RN, NEF = A["L0_gnn_W_fc1"].shape[1], A["L0_gnn_W_fc1"].shape[0]
    WN = 2 * CS + 2 * CV
    MS = CS + CV
    MW = 4 * MS
    QUADS = QUADS_D
    with ExitStack() as ctx:
        sb = lambda n, s, d=F32: ctx.enter_context(nc.sbuf_tensor("l0_" + n, s, d))
        sem = ctx.enter_context(Semaphores(nc))
        fc1, fc2 = sb("fc1", [PW, PAIR, RN]), sb("fc2", [RN, WN])
        l2_0, l2_1 = sb("l2_0", [MS, CS]), sb("l2_1", [MS, CV])
        bins = sb("bins", [1, 10 * P], I32)
        with ExitStack() as inner:
            sbi = lambda n, s, d=F32: inner.enter_context(nc.sbuf_tensor("l0_" + n, s, d))
            H = sbi("h0", [P, NB, D])
            stage_norm(nc, K, H, "l0n")
            W1, W2 = sbi("proj_w1", [P, 2 * D]), sbi("proj_w2", [CV, 2 * D])
            own, table = sbi("own", [P, NB, D]), sbi("table", [P, NB, D])
            w_in, w_clear, w_steps = sem("w_in"), sem("w_clear"), sem("w_steps")
            with nc.Block() as block:
                @block.sync
                def _(sp):
                    sp.wait_ge(w_clear, 1)
                    loads = 0

                    def load(to, name, rows=slice(None)):
                        sp.dma_start(to, A[name][rows, :]).then_inc(w_in, 16)

                    for half, (ws, wv) in enumerate((("L0_gnn_W_sc0", "L0_gnn_W_sc1"), ("L0_gnn_W_l1_0", "L0_gnn_W_l1_1"))):
                        c = half * D
                        load(W1[0:CS, c:c + CS], ws)
                        load(W1[CS:CS + CV, c + CS:c + CS + CV], wv)
                        load(W1[CS + CV:P, c + CS + CV:c + P], wv)
                        load(W2[:, c + P:c + D], wv)
                    for s in range(PAIR):
                        at = s * WORDS_D + D_E12
                        load(fc1[at:at + NEF, s, :], "L0_gnn_W_fc1")
                    load(fc2[:, :], "L0_gnn_W_fc2")
                    load(l2_0[:, :], "L0_gnn_W_l2_0")
                    load(l2_1[:, :], "L0_gnn_W_l2_1")
                    sp.dma_start(bins[0:1, :], K["bins_d"].rearrange("(o n) -> o n", o=1)).then_inc(w_in, 16)

                @block.vector
                def _(dve):
                    v = Steps(dve, w_steps)
                    nc.vector.memset(W1[:, :], 0.0)
                    nc.vector.memset(W2[:, :], 0.0)
                    nc.vector.memset(fc1[:, :, :], 0.0).then_inc(w_clear, 1)
                    dve.wait_ge(w_in, 16 * 14)
                    s, vv = 1.0 / CS ** 0.5, 1.0 / CV ** 0.5
                    scaled = lambda ap, f: v.done(nc.vector.tensor_scalar(ap, ap, float(f), None, ALU.mult))
                    for half, f in enumerate((SIN, 1.0)):
                        c = half * D
                        scaled(W1[0:CS, c:c + D], s * f)
                        scaled(W1[CS:P, c:c + D], vv * f)
                        scaled(W2[:, c:c + D], vv * f)
                    scaled(fc2[:, :], RN ** -0.5)
                    o = COS * 8.0 ** -0.5 * MS ** -0.5
                    scaled(l2_0[0:CS, :], o)
                    scaled(l2_0[CS:MS, :], o * 3.0 ** -0.5)
                    scaled(l2_1[:, :], o)
                    v.after()
            stage_project(nc, K, H, W1, W2, K["z"], own, table, "l0p")
            tab_out, own_added = sem("tab_out"), sem("own_added")
            with nc.Block() as block:
                @block.sync
                def _(sp):
                    sp.dma_start(K["table0"].rearrange("(b p) f -> p b f", p=P), table[:, :, :]).then_inc(tab_out, 16)
                    sp.wait_ge(tab_out, 16)

                @block.vector
                def _(dve):
                    nc.vector.tensor_tensor(K["X"][:, :, :], K["X"][:, :, :], own[:, :, :], ALU.add).then_inc(own_added, 1)
                    dve.wait_ge(own_added, 1)

        acc = sb("message_sums", [P, NB, MW])
        pay = [sb(f"edge_rows{k}", [P, QUAD, WORDS_D]) for k in range(2)]
        xg = [sb(f"source_rows{k}", [P, QUAD, D]) for k in range(2)]
        pay_t, hid = sb("edge_rows_turned", [PW, QUAD // PAIR, P]), sb("hidden", [RN, QUAD * P])
        u01 = sb("w_times_scalars", [P, QUAD, 2, CS])
        u23 = sb("w_times_vectors", [P, QUAD, 3, 2, CV])
        dots = sb("dot_parts", [P, QUAD, 3, CV])
        msg = [sb(f"messages{k}", [P, QUAD, MW]) for k in range(2)]
        hot = [sb(f"node_onehot{k}", [P, QUAD, P]) for k in range(2)]
        with ExitStack() as inner:
            ps = lambda n, s: inner.enter_context(nc.psum_tensor("l0_" + n, s, F32))
            semi = inner.enter_context(Semaphores(nc))
            p_turn, p_hid, p_w, p_sum = ps("p_turn", [P, 512]), ps("p_hid", [P, 512]), ps("p_w", [P, QUAD, 256]), ps("p_sum", [P, 2, 512])
            pay_in = [semi(f"pay_in{k}") for k in range(2)]
            xg_in = [semi(f"xg_in{k}") for k in range(2)]
            turned, turn_copied, hid_done, silu_done, w_done, msgs, summed, added, chain, pool_seen, pe_seen = (
                semi(n) for n in ("turned", "turn_copied", "hid_done", "silu_done", "w_done", "msgs", "summed", "added", "msg_steps", "pool_seen", "pe_seen"))
            ITERS = QUADS // 2
            with nc.Block() as block:
                @block.sync
                def _(sp):
                    with sp.Fori(0, ITERS + 1) as it:
                        for k in range(2):
                            sp.wait_ge(msgs, 2 * it + (k + 1))
                            at = (2 * it + k) * (QUAD * P)
                            sp.dma_start(pay[k][:, :, :], K["rows_d"][bass.ds(at, QUAD * P), :].rearrange("(s p) w -> p s w", p=P)).then_inc(pay_in[k], 16)

                @block.gpsimd
                def _(pool):
                    with pool.Fori(0, ITERS + 1) as it:
                        for k in range(2):
                            pool.wait_ge(pay_in[k], 16 * it + 16)
                            pool.sem_inc(pool_seen, 1)
                            for s in range(QUAD):
                                pool.indirect_dma_start(xg[k][:, s, :], None, K["table0"],
                                                        bass.IndirectOffsetOnAxis(ap=pay[k][:, s, D_SRC:D_SRC + 1].bitcast(U32), axis=0)).then_inc(xg_in[k], 16)
                    for k in range(2):
                        pool.wait_ge(xg_in[k], 16 * QUAD * (ITERS + 1))

                @block.scalar
                def _(act):
                    def quad(q):
                        act.wait_ge(turned, q + 1)
                        nc.scalar.copy(pay_t[:, :, :].rearrange("p h e -> p (h e)"), p_turn[0:PW, 0:QUAD // PAIR * P]).then_inc(turn_copied, 1)
                        act.wait_ge(hid_done, q + 1)
                        nc.scalar.activation(hid[:, :], p_hid[0:RN, :], ACT.Silu, scale=NEF ** -0.5).then_inc(silu_done, 1)

                    with act.Fori(0, QUADS + 1) as q:
                        quad(q)

                @block.tensor
                def _(pe):
                    def weights(q, k, loaded):
                        pe.wait_ge(pay_in[k], loaded)
                        pe.sem_inc(pe_seen, 1)
                        for h in range(QUAD // PAIR):
                            ins = nc.tensor.transpose(p_turn[0:PW, h * P:(h + 1) * P], pay[k][:, PAIR * h:PAIR * (h + 1), :].rearrange("p s w -> p (s w)"), K["ident"][:, :])
                        ins.then_inc(turned, 1)
                        pe.wait_ge(turn_copied, q + 1)
                        for s in range(QUAD):
                            ins = nc.tensor.matmul(p_hid[0:RN, s * P:(s + 1) * P], fc1[:, s % PAIR, :], pay_t[:, s // PAIR, :], start=True, stop=True)
                        ins.then_inc(hid_done, 1)
                        pe.wait_ge(silu_done, q + 1)
                        pe.wait_ge(msgs, q + 2)
                        for s in range(QUAD):
                            ins = nc.tensor.matmul(p_w[:, s, 0:WN], hid[:, s * P:(s + 1) * P], fc2[:, :], start=True, stop=True)
                        ins.then_inc(w_done, 1)

                    def sums(q, k):
                        pe.wait_ge(msgs, q + 3)
                        pe.wait_ge(added, q + 1)
                        for s in range(QUAD):
                            ins = nc.tensor.matmul(p_sum[:, k, 0:MW], hot[k][:, s, :], msg[k][:, s, :], start=s == 0, stop=s == QUAD - 1)
                        ins.then_inc(summed, 1)

                    weights(0, 0, 16)
                    with pe.Fori(0, ITERS) as it:
                        weights(2 * it + 1, 1, 16 * it + 16)
                        sums(2 * it, 0)
                        weights(2 * it + 2, 0, 16 * it + 32)
                        sums(2 * it + 1, 1)

                @block.vector
                def _(dve):
                    v = Steps(dve, chain, per=8)
                    bin_reg = dve.alloc_register("l0_bin")

                    def messages(q, k, loaded):
                        v.begin(q)
                        e0 = xg[k][:, :, 0:CS]
                        y0, y1 = pay[k][:, :, D_E4:D_E4 + 1], pay[k][:, :, D_E4 + 1:D_E4 + 4]
                        py, px = QUAD * WORDS_D, QUAD * D
                        dve.wait_ge(xg_in[k], loaded)
                        v.done(nc.vector.tensor_tensor(hot[k][:, :, :], free(K["iota_f"][:, 1:2], [0, QUAD], [1, P]),
                                                       free(pay[k][:, 0, D_LOC:D_LOC + 1], [WORDS_D, QUAD], [0, P]), ALU.is_equal))
                        dve.wait_ge(w_done, q + 1)
                        v.done(nc.vector.tensor_tensor(u01[:, :, :, :], p_w[:, :, 0:2 * CS].rearrange("p s (a c) -> p s a c", a=2),
                                                       free(e0, [D, QUAD], [0, 2], [1, CS]), ALU.mult))
                        for i in range(3):
                            e1 = xg[k][:, 0, CS + CV * i:CS + CV * i + CV]
                            ins = nc.vector.tensor_tensor(u23[:, :, i, :, :], p_w[:, :, 2 * CS:WN].rearrange("p s (a c) -> p s a c", a=2),
                                                          free(e1, [D, QUAD], [0, 2], [1, CV]), ALU.mult)
                        u23_done = v.done(ins)
                        v.after(u23_done - 1)
                        m = msg[k]
                        v.done(nc.vector.tensor_tensor(m[:, :, 0:CS], u01[:, :, 0, :], free(y0, [WORDS_D, QUAD], [0, CS]), ALU.mult))
                        v.done(nc.vector.tensor_tensor(free(m[:, 0, MS:MS + CS], [MW, QUAD], [MS, 3], [1, CS]),
                                                       free(u01[:, 0, 1, :], [2 * CS, QUAD], [0, 3], [1, CS]),
                                                       free(y1, [WORDS_D, QUAD], [1, 3], [0, CS]), ALU.mult))
                        v.after(u23_done)
                        v.done(nc.vector.tensor_tensor(dots[:, :, :, :], u23[:, :, :, 1, :], free(y1, [WORDS_D, QUAD], [1, 3], [0, CV]), ALU.mult))
                        d_done = v.k
                        v.done(nc.vector.tensor_tensor(free(m[:, 0, MS + CS:MS + MS], [MW, QUAD], [MS, 3], [1, CV]),
                                                       u23[:, :, :, 0, :], free(y0, [WORDS_D, QUAD], [0, 3], [0, CV]), ALU.mult))
                        v.after(d_done)
                        v.done(nc.vector.tensor_tensor(dots[:, :, 0, :], dots[:, :, 0, :], dots[:, :, 1, :], ALU.add))
                        v.after()
                        nc.vector.tensor_tensor(m[:, :, CS:MS], dots[:, :, 0, :], dots[:, :, 2, :], ALU.add).then_inc(msgs, 1)
                        v.end()

                    def add(q, k):
                        dve.reg_load([bin_reg], bins[0:1, bass.ds(q * QUAD, 1)])
                        b = dve.snap(bin_reg, min_val=0, max_val=NB - 1)
                        dve.wait_ge(summed, q + 1)
                        dve.wait_ge(added, q + 2)
                        to = acc[:, bass.ds(b, 1), :].rearrange("p o f -> p (o f)")
                        nc.vector.tensor_tensor(to, to, p_sum[:, k, 0:MW], ALU.add).then_inc(added, 1)

                    nc.vector.memset(acc[:, :, :], 0.0).then_inc(added, 2)
                    dve.sem_inc(msgs, 2)
                    messages(0, 0, 64)
                    with dve.Fori(0, ITERS) as it:
                        messages(2 * it + 1, 1, 64 * it + 64)
                        add(2 * it, 0)
                        messages(2 * it + 2, 0, 64 * it + 128)
                        add(2 * it + 1, 1)

        with ExitStack() as inner:
            sbi = lambda n, s, d=F32: inner.enter_context(nc.sbuf_tensor("l0_" + n, s, d))
            ps = lambda n, s: inner.enter_context(nc.psum_tensor("l0_" + n, s, F32))
            semi = inner.enter_context(Semaphores(nc))
            ab, at_ = sbi("sums_block", [P, MW]), sbi("sums_turned", [MS, 4 * P])
            p_t, p_o = ps("p_t", [P, 512]), ps("p_o", [P, 512])
            taken, turned, copied, mapped, x_done = (semi(n) for n in ("taken", "turned", "copied", "mapped", "x_done"))
            with nc.Block() as block:
                @block.vector
                def _(dve):
                    dve.sem_inc(x_done, 1)
                    with dve.Fori(0, NB) as b:
                        nc.vector.tensor_copy(ab[:, :], acc[:, bass.ds(b, 1), :].rearrange("p o f -> p (o f)")).then_inc(taken, 1)
                        dve.wait_ge(mapped, b + 1)
                        xb = K["X"][:, bass.ds(b, 1), :].rearrange("p o f -> p (o f)")
                        nc.vector.scalar_tensor_tensor(xb, p_o[:, 0:D], K["z"][:, bass.ds(b, 1)], xb, ALU.mult, ALU.add).then_inc(x_done, 1)

                @block.tensor
                def _(pe):
                    with pe.Fori(0, NB) as b:
                        pe.wait_ge(taken, b + 1)
                        for j in range(4):
                            ins = nc.tensor.transpose(p_t[0:MS, j * P:(j + 1) * P], ab[:, j * MS:(j + 1) * MS], K["ident"][:, :])
                        ins.then_inc(turned, 1)
                        pe.wait_ge(copied, b + 1)
                        pe.wait_ge(x_done, b + 1)
                        nc.tensor.matmul(p_o[:, 0:CS], at_[:, 0:P], l2_0[:, :], start=True, stop=True)
                        for i in range(3):
                            ins = nc.tensor.matmul(p_o[:, CS + CV * i:CS + CV * (i + 1)], at_[:, (i + 1) * P:(i + 2) * P], l2_1[:, :], start=True, stop=True)
                        ins.then_inc(mapped, 1)

                @block.scalar
                def _(act):
                    with act.Fori(0, NB) as b:
                        act.wait_ge(turned, b + 1)
                        nc.scalar.copy(at_[:, :], p_t[0:MS, :]).then_inc(copied, 1)


def stage_finish(nc, A, K, out):
    with ExitStack() as ctx:
        raw = ctx.enter_context(nc.sbuf_tensor("x_out", [P, NB, D], F32))
        sem = ctx.enter_context(Semaphores(nc))
        ready, written = sem("x_ready"), sem("x_written")
        last = N - (NB - 1) * P
        with nc.Block() as block:
            @block.vector
            def _(dve):
                nc.vector.tensor_copy(raw[:, :, 0:CS], K["X"][:, :, 0:CS])
                for i in range(3):
                    ins = nc.vector.tensor_copy(by_part(raw, i), K["X"][:, :, CS + CV * i:CS + CV * (i + 1)])
                ins.then_inc(ready, 1)

            @block.sync
            def _(sp):
                sp.wait_ge(ready, 1)
                sp.dma_start(out[0:(NB - 1) * P, :].rearrange("(b p) f -> p b f", p=P), raw[:, 0:NB - 1, :]).then_inc(written, 16)
                sp.dma_start(out[(NB - 1) * P:N, :], raw[0:last, NB - 1, :]).then_inc(written, 16)
                sp.wait_ge(written, 32)

NC_W = 400


def stage_turn(nc, K, H, ht1, ht2, table, tag):
    with ExitStack() as ctx:
        sb = lambda n, s, d=F32: ctx.enter_context(nc.sbuf_tensor(tag + "_" + n, s, d))
        sem = ctx.enter_context(Semaphores(nc))
        hb = sb("h_block", [P, D])
        one = sb("h_with_one", [P, NB, D + 1])
        turn = ctx.enter_context(nc.psum_tensor(tag + "_" + "turn", [P, 512], F32))
        taken, turned, copied, with_one, written = (sem(n) for n in ("taken", "turned", "copied", "with_one", "written"))
        with nc.Block() as block:
            @block.vector
            def _(dve):
                nc.vector.tensor_copy(one[:, :, 0:D], H[:, :, :])
                nc.vector.memset(one[:, :, D:D + 1], 1.0).then_inc(with_one, 1)
                with dve.Fori(0, NB) as b:
                    dve.wait_ge(turned, b + 1)
                    nc.vector.tensor_copy(hb[:, :], H[:, bass.ds(b, 1), :].rearrange("p o f -> p (o f)")).then_inc(taken, 1)

            @block.sync
            def _(sp):
                sp.wait_ge(with_one, 1)
                sp.dma_start(table.rearrange("(b p) f -> p b f", p=P), one[:, :, :]).then_inc(written, 16)
                sp.wait_ge(written, 16)

            @block.tensor
            def _(pe):
                pe.sem_inc(turned, 1)
                with pe.Fori(0, NB) as b:
                    pe.wait_ge(taken, b + 1)
                    pe.wait_ge(copied, b + 1)
                    nc.tensor.transpose(turn[:, 0:P], hb[:, 0:P], K["ident"][:, :])
                    nc.tensor.transpose(turn[0:D - P, P:2 * P], hb[:, P:D], K["ident"][:, :]).then_inc(turned, 1)

            @block.scalar
            def _(act):
                act.sem_inc(copied, 1)
                with act.Fori(0, NB) as b:
                    act.wait_ge(turned, b + 2)
                    nc.scalar.copy(ht1[:, bass.ds(b * P, P)], turn[:, 0:P])
                    nc.scalar.copy(ht2[:, bass.ds(b * P, P)], turn[0:D - P, P:2 * P]).then_inc(copied, 1)


def stage_back(nc, K, H, parts, tag):
    with ExitStack() as ctx:
        sb = lambda n, s, d=F32: ctx.enter_context(nc.sbuf_tensor(tag + "_" + n, s, d))
        sem = ctx.enter_context(Semaphores(nc))
        ub = [sb(f"u_block{j}", [rows, P]) for j, (_, rows, _) in enumerate(parts)]
        turn = ctx.enter_context(nc.psum_tensor(tag + "_" + "turn", [P, 512], F32))
        taken, turned, x_done = (sem(n) for n in ("taken", "turned", "x_done"))
        with nc.Block() as block:
            @block.scalar
            def _(act):
                with act.Fori(0, NB) as b:
                    act.wait_ge(turned, b + 1)
                    for j, (tile, rows, _) in enumerate(parts):
                        ins = nc.scalar.copy(ub[j][:, :], tile[0:rows, bass.ds(b * P, P)])
                    ins.then_inc(taken, 1)

            @block.tensor
            def _(pe):
                pe.sem_inc(turned, 1)
                with pe.Fori(0, NB) as b:
                    pe.wait_ge(taken, b + 1)
                    pe.wait_ge(x_done, b + 1)
                    for j, (_, rows, col) in enumerate(parts):
                        ins = nc.tensor.transpose(turn[:, col:col + rows], ub[j][:, :], K["ident"][0:rows, 0:rows])
                    ins.then_inc(turned, 1)

            @block.vector
            def _(dve):
                nc.vector.tensor_tensor(K["X"][:, :, :], K["X"][:, :, :], H[:, :, :], ALU.add).then_inc(x_done, 1)
                with dve.Fori(0, NB) as b:
                    dve.wait_ge(turned, b + 2)
                    dve.wait_ge(x_done, b + 1)
                    xb = K["X"][:, bass.ds(b, 1), :].rearrange("p o f -> p (o f)")
                    nc.vector.tensor_tensor(xb, turn[:, 0:D], xb, ALU.add).then_inc(x_done, 1)


def stage_node_sums(nc, K, table, bins, acc1, acc2, edge_col, channels, products, counts, tag):
    CH = channels + 1
    ITERS = SLOTS_S // BATCH_S
    QB = BATCH_S // QUAD
    X2 = D + 1 - P
    X2_OUT = X2 if counts else CV
    with ExitStack() as ctx:
        sb = lambda n, s, d=F32: ctx.enter_context(nc.sbuf_tensor(tag + "_" + n, s, d))
        ps = lambda n, s: ctx.enter_context(nc.psum_tensor(tag + "_" + n, s, F32))
        sem = ctx.enter_context(Semaphores(nc))
        pay = [sb(f"edge_rows{q}", [P, QUAD, WORDS_S]) for q in range(QB)]
        xg = [sb(f"node_rows{q}", [P, QUAD, D + 1]) for q in range(QB)]
        eh = [sb(f"edge_by_node{q}", [P, QUAD, CH, G]) for q in range(QB)]
        z1, z2 = sb("outer1", [P, CH, BATCH_S, G]), sb("outer2", [X2, CH, BATCH_S, G])
        p1, p2 = ps("p_outer1", [P, 2, 512]), ps("p_outer2", [P, 2, 512])
        c1, c2 = ps("p_sums1", [P, 512]), ps("p_sums2", [P, 512])
        pay_in = [sem(f"pay_in{q}") for q in range(QB)]
        xg_in = [sem(f"xg_in{q}") for q in range(QB)]
        built, outer, evacuated, contracted, added, pool_seen, hot_done, pe_seen, sp_seen = (
            sem(n) for n in ("built", "outer", "evacuated", "contracted", "added", "pool_seen", "hot_done", "pe_seen", "sp_seen"))
        with nc.Block() as block:
            @block.sync
            def _(sp):
                with sp.Fori(0, ITERS + 1) as it:
                    for q in range(QB):
                        sp.wait_ge(built, it * QB + (q + 1))
                        sp.sem_inc(sp_seen, 1)
                        sp.wait_ge(outer, it * BATCH_S + QUAD * (q + 1))
                        sp.sem_inc(sp_seen, 1)
                        at = (it * QB + q) * (QUAD * P)
                        sp.dma_start(pay[q][:, :, :], K["rows_s"][bass.ds(at, QUAD * P), :].rearrange("(s p) w -> p s w", p=P)).then_inc(pay_in[q], 16)

            @block.gpsimd
            def _(pool):
                with pool.Fori(0, ITERS + 1) as it:
                    for q in range(QB):
                        pool.wait_ge(pay_in[q], it * 16 + 16)
                        pool.sem_inc(pool_seen, 1)
                        pool.wait_ge(outer, it * BATCH_S + QUAD * (q + 1))
                        pool.sem_inc(pool_seen, 1)
                        for s in range(QUAD):
                            pool.indirect_dma_start(xg[q][:, s, :], None, table,
                                                    bass.IndirectOffsetOnAxis(ap=pay[q][:, s, S_DST:S_DST + 1].bitcast(U32), axis=0)).then_inc(xg_in[q], 16)
                for q in range(QB):
                    pool.wait_ge(xg_in[q], 16 * QUAD * (ITERS + 1))

            @block.vector
            def _(dve):
                regs = [dve.alloc_register(f"s_bin{channels}_{s}") for s in range(BATCH_S)]

                def build(it, q):
                    dve.wait_ge(pay_in[q], it * 16 + 16)
                    dve.wait_ge(outer, it * BATCH_S + QUAD * (q + 1))
                    hot = eh[q][:, :, channels, :]
                    nc.vector.tensor_tensor(hot, free(K["iota_f"][:, 1:2], [0, QUAD], [1, G]),
                                            free(pay[q][:, 0, S_LOC:S_LOC + 1], [WORDS_S, QUAD], [0, G]), ALU.is_equal).then_inc(hot_done, 1)
                    dve.wait_ge(hot_done, it * QB + (q + 1))
                    nc.vector.tensor_tensor(eh[q][:, :, 0:channels, :],
                                            free(pay[q][:, 0, edge_col:edge_col + 1], [WORDS_S, QUAD], [1, channels], [0, G]),
                                            free(hot, [CH * G, QUAD], [0, channels], [1, G]), ALU.mult).then_inc(built, 1)

                nc.vector.memset(acc1[:, :], 0.0)
                nc.vector.memset(acc2[:, :], 0.0).then_inc(added, 1)
                dve.sem_inc(built, QB)
                for q in range(QB):
                    build(0, q)
                with dve.Fori(0, ITERS) as it:
                    for q in range(QB):
                        build(it + 1, q)
                    dve.wait_ge(contracted, it + 1)
                    for half in range(2):
                        dve.reg_load(regs[half * 8:half * 8 + 8], bins[0:1, bass.ds(it * BATCH_S + half * 8, 8)])
                    for s in range(BATCH_S):
                        at = dve.snap(regs[s], min_val=0, max_val=(BINS_S - 1) * G)
                        dve.wait_ge(added, it * BATCH_S + (s + 1))
                        o1, o2 = acc1[:, bass.ds(at, G)], acc2[0:X2_OUT, bass.ds(at, G)]
                        nc.vector.tensor_tensor(o1, o1, c1[:, s * G:(s + 1) * G], ALU.add)
                        nc.vector.tensor_tensor(o2, o2, c2[0:X2_OUT, s * G:(s + 1) * G], ALU.add).then_inc(added, 1)

            @block.tensor
            def _(pe):
                pe.sem_inc(outer, BATCH_S)
                with pe.Fori(0, ITERS) as it:
                    for q in range(QB):
                        pe.wait_ge(built, it * QB + (QB + q + 1))
                        pe.sem_inc(pe_seen, 1)
                        pe.wait_ge(xg_in[q], it * (16 * QUAD) + 16 * QUAD)
                        pe.sem_inc(pe_seen, 1)
                        for s in range(QUAD):
                            j = q * QUAD + s
                            pe.wait_ge(evacuated, it * BATCH_S + (j + 1))
                            e = eh[q][:, s, :, :].rearrange("p c n -> p (c n)")
                            nc.tensor.matmul(p1[:, j % 2, 0:CH * G], xg[q][:, s, 0:P], e, start=True, stop=True)
                            nc.tensor.matmul(p2[0:X2, j % 2, 0:CH * G], xg[q][:, s, P:D + 1], e, start=True, stop=True).then_inc(outer, 1)
                    pe.wait_ge(evacuated, it * BATCH_S + (BATCH_S + 2))
                    pe.sem_inc(pe_seen, 1)
                    pe.wait_ge(added, it * BATCH_S + 1)
                    pe.sem_inc(pe_seen, 1)
                    first, last = {}, {}
                    for n, (to, rows, *_) in enumerate(products):
                        first.setdefault(to, n)
                        last[to] = n
                    for n, (to, rows, lhs, of, krows, ch) in enumerate(products):
                        z = (z1, z2)[of][0:krows, ch, :, :].rearrange("p s n -> p (s n)")
                        ins = nc.tensor.matmul((c1, c2)[to][0:rows, 0:BATCH_S * G], lhs, z, start=n == first[to], stop=n == last[to], skip_group_check=True)
                    ins.then_inc(contracted, 1)

            @block.scalar
            def _(act):
                act.sem_inc(evacuated, 2)
                with act.Fori(0, ITERS) as it:
                    for j in range(BATCH_S):
                        act.wait_ge(outer, it * BATCH_S + (BATCH_S + j + 1))
                        nc.scalar.copy(z1[:, :, j, :], p1[:, j % 2, 0:CH * G].rearrange("p (c n) -> p c n", n=G))
                        nc.scalar.copy(z2[:, :, j, :], p2[0:X2, j % 2, 0:CH * G].rearrange("p (c n) -> p c n", n=G)).then_inc(evacuated, 1)


def stage_layer1(nc, A, K):
    NS = 8
    R2, RT = 2.0 ** -0.5, 3.0 ** -0.5
    with ExitStack() as ctx:
        sb = lambda n, s, d=F32: ctx.enter_context(nc.sbuf_tensor("l1_" + n, s, d))
        sem = ctx.enter_context(Semaphores(nc))
        H = sb("h1", [P, NB, D])
        ht1, ht2 = sb("h_by_feature1", [P, NP]), sb("h_by_feature2", [CV, NP])
        stage_norm(nc, K, H, "l1n")
        stage_turn(nc, K, H, ht1, ht2, K["table1"], "l1t")
        acc1, acc2 = sb("sums1", [P, NP]), sb("sums2", [CV + 1, NP])
        wm1, wm2 = sb("wm1", [P, D]), sb("wm2", [CV + 1, D])
        raw = [sb("wu_h1", [P, D]), sb("wu_h2", [CV, D]), sb("wu_a1", [P, D]), sb("wu_a2", [CV, D])]
        wu = [sb("wu_h1p", [P, D]), sb("wu_h2p", [CV, D]), sb("wu_a1p", [P, D]), sb("wu_a2p", [CV, D])]
        bu1, bu2 = sb("bu1", [P, 1]), sb("bu2", [CV, 1])
        with ExitStack() as inner:
            sbi = lambda n, s, d=F32: inner.enter_context(nc.sbuf_tensor("l1_" + n, s, d))
            ws, ws2 = sbi("w_scalar", [P, NS, P]), sbi("w_scalar2", [CV, NS, CV])
            wv = [sbi(f"w_vector{i}", [P, NS, P]) for i in range(2)]
            wv2 = sbi("w_vector2", [CV, NS, CS])
            one = sbi("keep_count", [CV + 1, CV + 1])
            bins = sbi("bins", [1, 10 * P], I32)
            w_in, w_clear, w_steps = sem("w_in"), sem("w_clear"), sem("w_steps")
            S0, V0, V1 = slice(0, CS), slice(CS, CS + CV), slice(CS + CV, P)
            with nc.Block() as block:
                @block.sync
                def _(sp):
                    sp.wait_ge(w_clear, 1)

                    def load(to, of, **kw):
                        sp.dma_start(to, of, **kw).then_inc(w_in, 16)

                    W1, W2, W3, W4 = (A[f"L1_gnn_W{n}"] for n in (1, 2, 3, 4))
                    load(ws[S0, :, S0], W1)
                    load(ws[V0, :, V0], W4)
                    load(ws[V1, :, V1], W4)
                    load(ws2[:, :, :], W4)
                    for i, V in enumerate((V0, V1)):
                        load(wv[i][S0, :, V], W3)
                        load(wv[i][V, :, S0], W2)
                    load(wv2[:, :, :], W2)
                    load(bins[0:1, :], K["bins_s"].rearrange("(o n) -> o n", o=1))
                    Wm, Wu, bm, bu = A["L1_gnn_Wm"], A["L1_gnn_Wu"], A["L1_gnn_bm"], A["L1_gnn_bu"]
                    for w, t1, t2 in ((Wm, wm1, wm2), (Wu, raw[0], raw[1])):
                        load(t1[S0, :], w[0:CS, :])
                        for i, to in enumerate((t1[V0, :], t1[V1, :], t2[0:CV, :])):
                            load(to, w[CS + i:D:3, :])
                    load(wm2[CV:CV + 1, :], bm.rearrange("(o f) -> o f", o=1))
                    load(raw[2][:, :], Wu[D:D + P, :])
                    load(raw[3][:, :], Wu[D + P:2 * D, :])
                    bcol = bu.rearrange("(f o) -> f o", o=1)
                    load(bu1[S0, :], bcol[0:CS, :], allow_slow_non_contiguous=True)
                    for i, to in enumerate((bu1[V0, :], bu1[V1, :], bu2[:, :])):
                        load(to, bcol[CS + i:D:3, :], allow_slow_non_contiguous=True)

                @block.vector
                def _(dve):
                    v = Steps(dve, w_steps)
                    nc.vector.memset(ws[:, :, :], 0.0)
                    nc.vector.memset(one[:, :], 0.0)
                    for i in range(2):
                        ins = nc.vector.memset(wv[i][:, :, :], 0.0)
                    ins.then_inc(w_clear, 1)
                    dve.wait_ge(w_clear, 1)
                    v.done(nc.vector.memset(one[CV:CV + 1, CV:CV + 1], 1.0))
                    dve.wait_ge(w_in, 16 * 25)
                    scaled = lambda ap, f: v.done(nc.vector.tensor_scalar(ap, ap, float(f), None, ALU.mult))
                    f1, f2, f4 = R2 * (CS * NS) ** -0.5, R2 * RT * (CV * NS) ** -0.5, R2 * (CV * NS) ** -0.5
                    scaled(ws[S0, :, :], f1)
                    scaled(ws[CS:P, :, :], f4)
                    scaled(ws2[:, :, :], f4)
                    for i in range(2):
                        scaled(wv[i][S0, :, :], f1)
                        scaled(wv[i][CS:P, :, :], f2)
                    scaled(wv2[:, :, :], f2)
                    for a, b in zip(raw, wu):
                        v.done(nc.vector.tensor_copy(b[:, 0:CS], a[:, 0:CS]))
                        for i in range(3):
                            v.done(nc.vector.tensor_copy(b[:, CS + CV * i:CS + CV * (i + 1)], a[:, CS + i:D:3]))
                    v.after()
            products = [(1, CV + 1, one[:, :], 1, CV + 1, 4 * NS)]
            for b in range(NS):
                products += [(0, P, ws[:, b, :], 0, P, b), (1, CV, ws2[:, b, :], 1, CV, b)]
                for i in range(2):
                    products.append((0, P, wv[i][:, b, :], 0, P, NS + 3 * b + i))
                products += [(1, CV, wv[0][S0, b, V0], 0, CS, NS + 3 * b + 2), (0, CS, wv2[:, b, :], 1, CV, NS + 3 * b + 2)]
            stage_node_sums(nc, K, K["table1"], bins, acc1, acc2, S_E32, 4 * NS, products, True, "l1s")

        ut1, ut2 = sb("update1", [P, NP]), sb("update2", [CV, NP])
        with ExitStack() as inner:
            sbi = lambda n, s, d=F32: inner.enter_context(nc.sbuf_tensor("l1_" + n, s, d))
            ps = lambda n: inner.enter_context(nc.psum_tensor("l1_" + n, [P, 512], F32))
            semi = inner.enter_context(Semaphores(nc))
            ag1, ag2 = sbi("agg1", [P, NC_W]), sbi("agg2", [CV, NC_W])
            whole = (ht1, ht2, acc1, acc2)
            part = [sbi(f"nodes{j}", [t.shape[0], NC_W]) for j, t in enumerate(whole)]
            h1, h2, s1, s2 = part
            pa1, pa2, pu1, pu2 = ps("p_agg1"), ps("p_agg2"), ps("p_upd1"), ps("p_upd2")
            taken, agg, agg_copied, upd, upd_copied = (semi(n) for n in ("taken", "agg", "agg_copied", "upd", "upd_copied"))
            with nc.Block() as block:
                @block.vector
                def _(dve):
                    with dve.Fori(0, NP // NC_W) as c:
                        dve.wait_ge(upd, c + 1)
                        for t, of in zip(part, whole):
                            ins = nc.vector.tensor_copy(t[:, :], of[:, bass.ds(c * NC_W, NC_W)])
                        ins.then_inc(taken, 1)

                @block.tensor
                def _(pe):
                    pe.sem_inc(upd, 1)
                    with pe.Fori(0, NP // NC_W) as c:
                        pe.wait_ge(taken, c + 1)
                        for to, cols, rows in ((pa1, slice(0, P), P), (pa2, slice(P, D), CV)):
                            nc.tensor.matmul(to[0:rows, 0:NC_W], wm1[:, cols], s1[:, :], start=True, stop=False)
                            ins = nc.tensor.matmul(to[0:rows, 0:NC_W], wm2[:, cols], s2[:, :], start=False, stop=True)
                        ins.then_inc(agg, 1)
                        pe.wait_ge(agg_copied, c + 1)
                        pe.wait_ge(upd_copied, c + 1)
                        for to, cols, rows in ((pu1, slice(0, P), P), (pu2, slice(P, D), CV)):
                            o = to[0:rows, 0:NC_W]
                            nc.tensor.matmul(o, wu[0][:, cols], h1[:, :], start=True, stop=False)
                            nc.tensor.matmul(o, wu[1][:, cols], h2[:, :], start=False, stop=False)
                            nc.tensor.matmul(o, wu[2][:, cols], ag1[:, :], start=False, stop=False)
                            ins = nc.tensor.matmul(o, wu[3][:, cols], ag2[:, :], start=False, stop=True)
                        ins.then_inc(upd, 1)

                @block.scalar
                def _(act):
                    act.sem_inc(upd_copied, 1)
                    with act.Fori(0, NP // NC_W) as c:
                        n = bass.ds(c * NC_W, NC_W)
                        act.wait_ge(agg, c + 1)
                        nc.scalar.copy(ag1[:, :], pa1[:, 0:NC_W])
                        nc.scalar.copy(ag2[:, :], pa2[0:CV, 0:NC_W]).then_inc(agg_copied, 1)
                        act.wait_ge(upd, c + 2)
                        nc.scalar.activation(ut1[:, n], pu1[:, 0:NC_W], ACT.Identity, bias=bu1[:, 0:1])
                        nc.scalar.activation(ut2[:, n], pu2[0:CV, 0:NC_W], ACT.Identity, bias=bu2[:, 0:1]).then_inc(upd_copied, 1)
        stage_back(nc, K, H, [(ut1, P, 0), (ut2, CV, P)], "l1b")


def stage_layer2(nc, A, K):
    R3, R8, R32 = 3.0 ** -0.5, CS ** -0.5, CV ** -0.5
    with ExitStack() as ctx:
        sb = lambda n, s, d=F32: ctx.enter_context(nc.sbuf_tensor("l2_" + n, s, d))
        sem = ctx.enter_context(Semaphores(nc))
        H = sb("h2", [P, NB, D])
        with ExitStack() as inner:
            sbi = lambda n, s, d=F32: inner.enter_context(nc.sbuf_tensor("l2_" + n, s, d))
            ht1, ht2 = sbi("h_by_feature1", [P, NP]), sbi("h_by_feature2", [CV, NP])
            stage_norm(nc, K, H, "l2n")
            stage_turn(nc, K, H, ht1, ht2, K["table2"], "l2t")
            acc1, acc2 = sbi("sums1", [P, NP]), sbi("sums2", [CV + 1, NP])
            ws, ws2 = sbi("w_scalar", [P, 2, P]), sbi("w_scalar2", [CV, 2, CV])
            wv = [sbi(f"w_vector{i}", [P, P]) for i in range(2)]
            wv2 = sbi("w_vector2", [CV, CS])
            bins = sbi("bins", [1, 10 * P], I32)
            w_in, w_clear, w_steps = sem("w_in"), sem("w_clear"), sem("w_steps")
            S0, V0, V1 = slice(0, CS), slice(CS, CS + CV), slice(CS + CV, P)
            with nc.Block() as block:
                @block.sync
                def _(sp):
                    sp.wait_ge(w_clear, 1)

                    def load(to, of):
                        sp.dma_start(to, of).then_inc(w_in, 16)

                    for k, (s, v) in enumerate((("Wm_ss", "Wm_vs"), ("Lm_s", "Lm_v"))):
                        load(ws[S0, k, S0], A["L2_gnn_" + s])
                        for to in (ws[V0, k, V0], ws[V1, k, V1], ws2[:, k, :]):
                            load(to, A["L2_gnn_" + v])
                    for i, V in enumerate((V0, V1)):
                        load(wv[i][S0, V], A["L2_gnn_Wm_sv"])
                        load(wv[i][V, S0], A["L2_gnn_Wm_vv"])
                    load(wv2[:, :], A["L2_gnn_Wm_vv"])
                    load(bins[0:1, :], K["bins_s"].rearrange("(o n) -> o n", o=1))
                    sp.dma_start(K["h_turned"][0:P, :], ht1[:, :]).then_inc(w_in, 16)
                    sp.dma_start(K["h_turned"][P:D, :], ht2[:, :]).then_inc(w_in, 16)

                @block.vector
                def _(dve):
                    v = Steps(dve, w_steps)
                    nc.vector.memset(ws[:, :, :], 0.0)
                    for i in range(2):
                        ins = nc.vector.memset(wv[i][:, :], 0.0)
                    ins.then_inc(w_clear, 1)
                    dve.wait_ge(w_in, 16 * 16)
                    scaled = lambda ap, f: v.done(nc.vector.tensor_scalar(ap, ap, float(f), None, ALU.mult))
                    scaled(ws[S0, :, :], R8)
                    scaled(ws[CS:P, :, :], R32)
                    scaled(ws2[:, :, :], R32)
                    for i in range(2):
                        scaled(wv[i][S0, :], R8)
                        scaled(wv[i][CS:P, :], R3 * R32)
                    scaled(wv2[:, :], R3 * R32)
                    v.after()
            DIST, ONE = 3, 4
            products = []
            for k, ch in enumerate((DIST, ONE)):
                products += [(0, P, ws[:, k, :], 0, P, ch), (1, CV, ws2[:, k, :], 1, CV, ch)]
            for i in range(2):
                products.append((0, P, wv[i][:, :], 0, P, i))
            products += [(1, CV, wv[0][S0, V0], 0, CS, 2), (0, CS, wv2[:, :], 1, CV, 2)]
            stage_node_sums(nc, K, K["table2"], bins, acc1, acc2, S_E4, 4, products, False, "l2s")
            a_out = sem("a_out")
            with nc.Block() as block:
                @block.sync
                def _(sp):
                    sp.dma_start(K["a_turned"][0:P, :], acc1[:, :]).then_inc(a_out, 16)
                    sp.dma_start(K["a_turned"][P:D, :], acc2[0:CV, :]).then_inc(a_out, 16)
                    sp.wait_ge(a_out, 32)

        U = sb("update", [P, NB, D])
        with ExitStack() as inner:
            sbi = lambda n, s, d=F32: inner.enter_context(nc.sbuf_tensor("l2_" + n, s, d))
            semi = inner.enter_context(Semaphores(nc))
            KB = 8
            SPAN = P // 4
            w_ss = [sbi(f"w_ss{h}", [P, 16, CS]) for h in range(2)]
            w_vv, w_sv, w_vs = sbi("w_vv", [P, 8, CS]), sbi("w_sv", [P, 16, CV]), sbi("w_vs", [P, 16, CV])
            l_s, l_v = sbi("l_s", [CS, CS]), sbi("l_v", [CV, CV])
            xs4, a04 = sbi("xs_by32", [P, 16, P]), sbi("a0_by32", [P, 16, P])
            xv4 = sbi("xv_by32", [P, 3, 8, P])
            a0, a1, xv = sbi("a0_four_times", [P, 2, P]), sbi("a1_four_times", [P, 3, P]), sbi("xv_four_times", [P, 3, P])
            hs, hv = sbi("h_scalars", [CS, P]), sbi("h_vectors", [CV, 3, P])
            p_u = inner.enter_context(nc.psum_tensor("l2_p_upd", [P, 512], F32))
            w_in, w_steps = semi("w_in2"), semi("w_steps2")
            hT, aT = K["h_turned"], K["a_turned"]
            S = slice(0, CS)
            V = [slice(CS + CV * i, CS + CV * (i + 1)) for i in range(3)]
            steps = []
            for i in range(3):
                steps.append(("xv4", xv4[:, i, :, :], ("a1", a1[:, i, :]), [w_vv[:, j, :] for j in range(KB)], S))
            for i in range(3):
                for k in range(0, 16, KB):
                    steps.append(("xs4", xs4[:, k:k + KB, :], ("a1", a1[:, i, :]), [w_sv[:, k + j, :] for j in range(KB)], V[i]))
            for h in range(2):
                for k in range(0, 16, KB):
                    steps.append(("xs4", xs4[:, k:k + KB, :], ("a0", a0[:, h, :]), [w_ss[h][:, k + j, :] for j in range(KB)], S))
            for i in range(3):
                for k in range(0, 16, KB):
                    steps.append(("a04", a04[:, k:k + KB, :], ("xv", xv[:, i, :]), [w_vs[:, k + j, :] for j in range(KB)], V[i]))
            STEPS = len(steps)
            prod = [sbi(f"outer{m}", [P, KB, P]) for m in range(STEPS)]
            names = ("xv4", "a1", "xs4", "a0", "a04", "xv")
            last_use = {g: max(m for m, s in enumerate(steps) if g in (s[0], s[2][0])) + 1 for g in names}
            loads = {"xv4": 12, "a1": 4, "xs4": 4, "a0": 4, "a04": 4, "xv": 4, "lin": 2}
            arrived = {g: semi(f"{g}_in") for g in loads}
            made, used, seen, upd, upd_copied = (semi(n) for n in ("made", "used", "seen", "upd", "upd_copied"))
            with nc.Block() as block:
                @block.scalar
                def _(act):
                    def load(to, of):
                        act.dma_start(to, of).then_inc(w_in, 16)

                    for j in range(4):
                        rows = slice(j * SPAN, (j + 1) * SPAN)
                        for h in range(2):
                            load(w_ss[h][rows, :, :], A["L2_gnn_Wu_ss"][j:CS:4, h * SPAN:(h + 1) * SPAN, :].rearrange("k v w -> v k w"))
                        load(w_vv[rows, :, :], A["L2_gnn_Wu_vv"][j:CV:4, :, :].rearrange("k v w -> v k w"))
                        load(w_sv[rows, :, :], A["L2_gnn_Wu_sv"][j:CS:4, :, :].rearrange("k v w -> v k w"))
                        load(w_vs[rows, :, :], A["L2_gnn_Wu_vs"][:, j:CS:4, :])
                    load(l_s[:, :], A["L2_gnn_Lu_s"])
                    load(l_v[:, :], A["L2_gnn_Lu_v"])
                    act.sem_inc(upd_copied, 1)
                    with act.Fori(0, NB) as t:
                        act.wait_ge(upd, t + 1)
                        nc.scalar.copy(U[:, bass.ds(t, 1), :].rearrange("p o f -> p (o f)"), p_u[:, 0:D]).then_inc(upd_copied, 1)

                @block.sync
                def _(sp):
                    def spread(group, to, of, first, rows, n):
                        for j in range(4):
                            v = of[first + j:first + rows:4, n]
                            v = bass.AP(v.tensor, v.offset, [[0, SPAN]] + [list(d) for d in v.ap])
                            sp.dma_start(to[j * SPAN:(j + 1) * SPAN, :, :], v).then_inc(arrived[group], 16)

                    def free_to_load(group, t):
                        sp.wait_ge(made, t * STEPS + last_use[group])
                        sp.sem_inc(seen, 1)

                    with sp.Fori(0, NB) as t:
                        n = bass.ds(t * P, P)
                        vectors = lambda of: of[CS:D, n].rearrange("(i c) n -> c i n", i=3)
                        sp.wait_ge(used, t * STEPS + 1)
                        sp.sem_inc(seen, 1)
                        sp.dma_start(hs[:, :], hT[0:CS, n]).then_inc(arrived["lin"], 16)
                        sp.dma_start(hv[:, :, :], vectors(hT)).then_inc(arrived["lin"], 16)
                        free_to_load("xv4", t)
                        for i in range(3):
                            spread("xv4", xv4[:, i, :, :], hT, CS + CV * i, CV, n)
                        free_to_load("a1", t)
                        for j in range(4):
                            sp.dma_start(a1[j * SPAN:(j + 1) * SPAN, :, :], vectors(aT)).then_inc(arrived["a1"], 16)
                        free_to_load("xs4", t)
                        spread("xs4", xs4, hT, 0, CS, n)
                        free_to_load("a0", t)
                        for j in range(4):
                            sp.dma_start(a0[j * SPAN:(j + 1) * SPAN, :, :], aT[0:CS, n].rearrange("(h v) n -> v h n", h=2)).then_inc(arrived["a0"], 16)
                        free_to_load("a04", t)
                        spread("a04", a04, aT, 0, CS, n)
                        free_to_load("xv", t)
                        for j in range(4):
                            sp.dma_start(xv[j * SPAN:(j + 1) * SPAN, :, :], vectors(hT)).then_inc(arrived["xv"], 16)

                @block.vector
                def _(dve):
                    v = Steps(dve, w_steps)
                    dve.wait_ge(w_in, 16 * 22)
                    scaled = lambda ap, f: v.done(nc.vector.tensor_scalar(ap, ap, float(f), None, ALU.mult))
                    for h in range(2):
                        scaled(w_ss[h][:, :, :], 1.0 / CS)
                    scaled(w_vv[:, :, :], R3 / CV)
                    scaled(w_sv[:, :, :], (CS * CV) ** -0.5)
                    scaled(w_vs[:, :, :], (CS * CV) ** -0.5)
                    scaled(l_s[:, :], R8)
                    scaled(l_v[:, :], R32)
                    v.after()
                    dve.sem_inc(made, STEPS)
                    with dve.Fori(0, NB) as t:
                        waited = set()
                        for m, (g, x, (g2, a), _, _) in enumerate(steps):
                            for name in (g, g2):
                                if name not in waited:
                                    dve.wait_ge(arrived[name], t * (16 * loads[name]) + 16 * loads[name])
                                    waited.add(name)
                            dve.wait_ge(used, t * STEPS + (m + 1))
                            nc.vector.tensor_tensor(prod[m][:, :, :], x, free(a, [0, KB], [1, P]), ALU.mult).then_inc(made, 1)

                @block.tensor
                def _(pe):
                    pe.sem_inc(used, STEPS)
                    with pe.Fori(0, NB) as t:
                        pe.wait_ge(upd_copied, t + 1)
                        pe.sem_inc(seen, 1)
                        pe.wait_ge(made, t * STEPS + (STEPS + 1))
                        pe.sem_inc(seen, 1)
                        pe.wait_ge(arrived["lin"], t * 32 + 32)
                        pe.sem_inc(seen, 1)
                        nc.tensor.matmul(p_u[:, S], hs[:, :], l_s[:, :], start=True, stop=False, skip_group_check=True)
                        for i in range(3):
                            nc.tensor.matmul(p_u[:, V[i]], hv[:, i, :], l_v[:, :], start=False, stop=False, skip_group_check=True)
                        last = {}
                        for m, s in enumerate(steps):
                            last[s[4].start] = m
                        for m, (_, _, _, weights, cols) in enumerate(steps):
                            pe.wait_ge(made, t * STEPS + (STEPS + m + 1))
                            pe.sem_inc(seen, 1)
                            for j, w in enumerate(weights):
                                ins = nc.tensor.matmul(p_u[:, cols], prod[m][:, j, :], w, start=False, stop=m == last[cols.start] and j == KB - 1, skip_group_check=True)
                            ins.then_inc(used, 1)
                        pe.wait_ge(used, t * STEPS + 2 * STEPS)
                        pe.sem_inc(upd, 1)
            with nc.Block() as block:
                @block.vector
                def _(dve):
                    v = Steps(dve, w_steps, base=7)
                    for t in (H, U):
                        v.link(nc.vector.tensor_tensor(K["X"][:, :, :], K["X"][:, :, :], t[:, :, :], ALU.add))

BF16 = mybir.dt.bfloat16
HEADS, AS, AV = 4, 16, 8
HW = AS + 3 * AV + 1
NEVER = 1e30


def stage_equivariant_norm(nc, K, H, S, gs, bs, gv):
    with ExitStack() as ctx:
        sb = lambda n, s, d=F32: ctx.enter_context(nc.sbuf_tensor("l3e_" + n, s, d))
        sem = ctx.enter_context(Semaphores(nc))
        square = sb("square", [P, NB, D])
        mean, var, rms, rstd, rrms, eps = (sb(n, [P, NB]) for n in ("mean", "var", "rms", "rstd", "rrms", "eps"))
        steps, squares_ready, roots_ready = sem("norm_steps"), sem("squares_ready"), sem("roots_ready")
        over = lambda t, n: free(t[:, :], [1, NB], [0, n])
        gain = lambda t, n: free(t[:, :], [0, NB], [1, n])
        s, v3 = S[:, :, 0:CS], S[:, :, CS:D]
        vec = lambda t: free(t[:, 0, CS:CS + 1], [D, NB], [CV, 3], [1, CV])
        with nc.Block() as block:
            @block.vector
            def _(dve):
                v = Steps(dve, steps)
                v.done(nc.vector.memset(eps[:, :], LN_EPS))
                v.link(nc.vector.tensor_reduce(mean[:, :], H[:, :, 0:CS], AX.X, ALU.add))
                v.link(nc.vector.tensor_scalar(mean[:, :], mean[:, :], 1.0 / CS, None, ALU.mult))
                v.link(nc.vector.tensor_tensor(s, H[:, :, 0:CS], over(mean, CS), ALU.subtract))
                v.done(nc.vector.tensor_tensor(square[:, :, 0:CS], s, s, ALU.mult))
                v.link(nc.vector.tensor_tensor(square[:, :, CS:D], H[:, :, CS:D], H[:, :, CS:D], ALU.mult))
                v.done(nc.vector.tensor_reduce(var[:, :], square[:, :, 0:CS], AX.X, ALU.add))
                nc.vector.tensor_reduce(rms[:, :], square[:, :, CS:D], AX.X, ALU.add).then_inc(squares_ready, 1)
                dve.wait_ge(roots_ready, 1)
                v.done(nc.vector.reciprocal(rstd[:, :], var[:, :]))
                v.link(nc.vector.reciprocal(rrms[:, :], rms[:, :]))
                v.link(nc.vector.tensor_tensor(s, s, over(rstd, CS), ALU.mult))
                v.link(nc.vector.tensor_tensor(s, s, gain(gs, CS), ALU.mult))
                v.done(nc.vector.tensor_tensor(s, s, gain(bs, CS), ALU.add))
                v.link(nc.vector.tensor_tensor(v3, H[:, :, CS:D], over(rrms, 3 * CV), ALU.mult))
                for i in range(3):
                    vi = S[:, :, CS + CV * i:CS + CV * (i + 1)]
                    v.done(nc.vector.tensor_tensor(vi, vi, gain(gv, CV), ALU.mult))
                v.after()

            @block.scalar
            def _(act):
                act.wait_ge(squares_ready, 1)
                nc.scalar.activation(var[:, :], var[:, :], ACT.Sqrt, bias=eps[:, 0:1], scale=1.0 / CS)
                nc.scalar.activation(rms[:, :], rms[:, :], ACT.Sqrt, bias=eps[:, 0:1], scale=1.0 / CV).then_inc(roots_ready, 1)


def stage_layer3(nc, A, K):
    W3 = lambda n: A["L3_gnn_" + n]
    PAIRS = SLOTS_D // PAIR
    TURN = 4
    TURNS = -(-(PAIRS + 3) // TURN) * TURN
    MS, FW, WN = CS + CV, 4 * P, 2 * CS + 3 * CV
    LEAD = 3 * PAIR
    with ExitStack() as ctx:
        sb = lambda n, s, d=F32: ctx.enter_context(nc.sbuf_tensor("l3_" + n, s, d))
        sem = ctx.enter_context(Semaphores(nc))
        H = sb("h", [P, NB, D])
        stage_norm(nc, K, H, "l3n")
        w_rbf = sb("w_rbf", [PW, PAIR, WN])
        w_a, w_v = sb("w_a", [P, D]), sb("w_v", [P, CV])
        w_hs, w_hv = sb("w_hs", [P, CS]), sb("w_hv", [P, CV])
        alpha_dot = sb("alpha_dot", [P, CS])
        bins = sb("bins", [1, LEAD + 10 * P], I32)
        sel, apart = sb("sel", [3 * HEADS, HEADS, P], BF16), sb("apart", [P, P], BF16)
        wp1, wp2 = sb("wp1", [P, D]), sb("wp2", [CV, D])
        ident_b = sb("ident_b", [P, P], BF16)
        tab_d = sb("table_dst", [P, NB, D])
        with ExitStack() as inner:
            sbi = lambda n, s, d=F32: inner.enter_context(nc.sbuf_tensor("l3_" + n, s, d))
            psi = lambda n: inner.enter_context(nc.psum_tensor("l3_" + n, [P, 512], F32))
            S, tab_s = sbi("normed", [P, NB, D]), sbi("table_src", [P, NB, D])
            wq1, wq2 = sbi("wq1", [P, 2 * D]), sbi("wq2", [CV, 2 * D])
            gs, bs, gv = sbi("gamma_s", [P, CS]), sbi("beta_s", [P, CS]), sbi("gamma_v", [P, CV])
            wg, val_t = sbi("w_gate", [CS, CV]), sbi("w_val_turned", [CS, MS])
            p_seen, head_rows = sbi("loads_seen", [1, 1]), sbi("head_rows", [3 * HEADS, HEADS])
            w2s, w2v = sbi("w2_s", [P, 1]), sbi("w2_v", [P, 1])
            p_t, p_g = psi("p_w_turned"), psi("p_w_gate")
            w_in, w_clear, w_steps, w_loaded, w_turned, w_copied, gated = (
                sem(n) for n in ("w_in", "w_clear", "w_steps", "w_loaded", "w_turned", "w_copied", "gated"))
            V = [slice(CS + CV * i, CS + CV * (i + 1)) for i in range(3)]
            n_loads, LOADS = [], 30
            with nc.Block() as block:
                @block.sync
                def _(sp):
                    sp.wait_ge(w_clear, 1)

                    def load(to, of, **kw):
                        n_loads.append(1)
                        sp.dma_start(to, of, **kw).then_inc(w_in, 16)

                    over_parts = lambda v, n: bass.AP(v.tensor, v.offset, [[0, P], [1, n]])
                    load(gs[:, :], over_parts(W3("gamma_s"), CS))
                    load(bs[:, :], over_parts(W3("beta_s"), CS))
                    load(gv[:, :], over_parts(W3("gamma_v"), CV))
                    load(alpha_dot[:, :], over_parts(W3("alpha_dot"), CS))
                    for w1, w2, c, ws, wv in ((wq1, wq2, 0, "Ws_src", "Wv_src"), (wq1, wq2, D, "Ws_dst", "Wv_dst"), (wp1, wp2, 0, "Wps", "Wpv")):
                        load(w1[0:CS, c:c + CS], W3(ws))
                        for i in range(2):
                            load(w1[V[i], c + V[i].start:c + V[i].stop], W3(wv))
                        load(w2[:, c + V[2].start:c + V[2].stop], W3(wv))
                    for s in range(PAIR):
                        at = s * WORDS_D + D_E16
                        load(w_rbf[at:at + 16, s, :], W3("W_rbf"))
                    load(w_a[0:MS, 0:CS], W3("W_alpha"))
                    load(w_a[0:MS, CS:2 * CS], W3("Ws_val"))
                    load(w_v[:, :], W3("Wv_val"))
                    load(wg[:, :], W3("Wg"))
                    load(w_hs[0:MS, :], W3("Ws_vlin"))
                    load(w_hv[:, :], W3("Wv_vlin"))
                    col = lambda n: W3(n).rearrange("(f o) -> f o", o=1)
                    for to, at, n in ((w2s, 0, "w2_ss"), (w2s, CS, "w2_vv0"), (w2v, 0, "w2_sv"), (w2v, CS, "w2_vs"), (w2v, MS, "w2_vv1")):
                        f = CS if at == 0 else CV
                        load(to[at:at + f, :], col(n), allow_slow_non_contiguous=True)
                    load(bins[0:1, LEAD:], K["bins_d"].rearrange("(o n) -> o n", o=1))

                @block.vector
                def _(dve):
                    v = Steps(dve, w_steps)
                    for t in (wq1, wq2, wp1, wp2, w_a, w_hs, w2s):
                        nc.vector.memset(t[:, :], 0.0)
                    nc.vector.memset(bins[0:1, 0:LEAD], 0)
                    nc.vector.memset(w_rbf[:, :, :], 0.0).then_inc(w_clear, 1)
                    i12 = K["ident"][0:3 * HEADS, :]

                    v.link(nc.vector.tensor_tensor(head_rows[:, :], i12[:, 0:HEADS], i12[:, HEADS:2 * HEADS], ALU.add))
                    v.link(nc.vector.tensor_tensor(head_rows[:, :], head_rows[:, :], i12[:, 2 * HEADS:3 * HEADS], ALU.add))
                    v.done(nc.vector.tensor_copy(sel[:, :, :], free(head_rows[:, :], [1, HEADS], [0, P])))
                    v.done(nc.vector.tensor_copy(ident_b[:, :], K["ident"][:, :]))
                    v.done(nc.vector.tensor_scalar(apart[:, :], K["ident"][:, :], 1.0, NEVER, ALU.subtract, ALU.mult))
                    dve.wait_ge(w_in, 16 * LOADS)
                    nc.vector.memset(p_seen[:, :], 0.0).then_inc(w_loaded, 1)
                    scaled = lambda ap, f: v.done(nc.vector.tensor_scalar(ap, ap, f, None, ALU.mult))
                    r2, r3 = 2.0 ** -0.5, 3.0 ** -0.5
                    scaled(w_rbf[:, :, 2 * CS + CV:2 * CS + 2 * CV], r3)
                    scaled(w_rbf[:, :, 2 * CS + 2 * CV:WN], r2)
                    v.after()
                    scaled(w_hs[:, :], w2s[:, 0:1])
                    scaled(w_hv[:, :], w2v[:, 0:1])
                    v.after()
                    scaled(w_hs[0:CS, :], 0.5)
                    scaled(w_hs[CS:MS, :], 0.5 * r3)
                    scaled(w_hv[0:MS, :], 0.5)
                    scaled(w_hv[MS:P, :], 0.5 * r2)
                    dve.wait_ge(gated, 1)
                    v.done(nc.vector.tensor_copy(w_a[0:MS, 2 * CS:D], p_g[0:MS, 0:CV]))
                    v.after()

                @block.tensor
                def _(pe):
                    pe.wait_ge(w_loaded, 1)
                    nc.tensor.transpose(p_t[0:CS, 0:MS], w_a[0:MS, CS:2 * CS], K["ident"][0:MS, 0:MS]).then_inc(w_turned, 1)
                    pe.wait_ge(w_copied, 1)
                    nc.tensor.matmul(p_g[0:MS, 0:CV], val_t[:, :], wg[:, :], start=True, stop=True).then_inc(gated, 1)

                @block.scalar
                def _(act):
                    act.wait_ge(w_turned, 1)
                    nc.scalar.copy(val_t[:, :], p_t[0:CS, 0:MS]).then_inc(w_copied, 1)
            assert len(n_loads) == LOADS, len(n_loads)
            stage_equivariant_norm(nc, K, H, S, gs, bs, gv)
            stage_project(nc, K, S, wq1, wq2, None, tab_s, tab_d, "l3p")
            tab_out = sem("tab_out")
            with nc.Block() as block:
                @block.sync
                def _(sp):
                    sp.dma_start(K["table0"].rearrange("(b p) f -> p b f", p=P), tab_s[:, :, :]).then_inc(tab_out, 16)
                    sp.wait_ge(tab_out, 16)

        acc, top = sb("sums", [P, NB, HEADS, HW]), sb("maxima", [P, NB, HEADS])
        with ExitStack() as inner:
            sbi = lambda n, s, d=F32: inner.enter_context(nc.sbuf_tensor("l3_" + n, s, d))
            ps = lambda n, s, d=F32: inner.enter_context(nc.psum_tensor("l3_" + n, s, d))
            semi = inner.enter_context(Semaphores(nc))
            four = lambda n, s, d=F32: [sbi(f"{n}{u}", s, d) for u in range(4)]
            two = lambda n, s, d=F32: [sbi(f"{n}{u}", s, d) for u in range(2)]
            pay, xg = four("edge_rows", [P, PAIR, WORDS_D]), four("source_rows", [P, PAIR, D])
            hot = four("node_onehot", [P, PAIR, P])
            hot_t, hot_tb = four("onehot_turned", [P, PAIR * P]), four("onehot_turned_b", [P, PAIR * P], BF16)
            pay_t = sbi("edge_rows_turned", [PW, P])
            msg = sbi("message", [P, PAIR, D])
            us, uv = sbi("weighted_s", [P, PAIR, 2, CS]), sbi("weighted_v", [P, PAIR, 3, 3, CV])
            F, G_ = two("product1", [P, PAIR, 4, P]), two("product2", [P, PAIR, 4, P])
            f_t, g_t = two("product1_turned", [P, 4 * P]), two("product2_turned", [P, 4 * P])
            dots, crossed, cross2 = (sbi(n, [P, PAIR, 3, CV]) for n in ("dot_parts", "crossed", "crossed_back"))
            th, sg, val_v = sbi("half_tanh", [P, PAIR, MS]), sbi("twice_sigmoid", [P, PAIR, MS]), sbi("val_v", [P, PAIR, 3, CV])
            slope, leaky, lsum = sbi("slope", [P, PAIR, CS]), sbi("leaky", [P, PAIR, CS]), sbi("logits", [P, PAIR, HEADS])
            none = sbi("empty_row", [P, PAIR])
            logit = two("logits_kept", [P, PAIR, HEADS])
            rest = sbi("rest", [P, PAIR, 2, HEADS])
            a3, a3_t = sbi("logit_parts", [P, PAIR, 3, HEADS], BF16), sbi("logit_parts_turned", [3 * HEADS, PAIR * P], BF16)
            qm, mn, drop, shrink = (sbi(n, [P, HEADS]) for n in ("pair_max", "new_max", "max_step", "shrink"))
            ea, Z = sbi("weight_logits", [P, PAIR, HEADS]), sbi("weighted", [P, PAIR, HEADS, HW])

            p_f = ps("p_front", [P, 512])
            p_a3 = p_f[0:3 * HEADS, 3 * P:4 * P].bitcast(BF16)
            p_w, p_d = ps("p_weights", [P, PAIR, 256]), ps("p_dst", [P, 512])
            p_t = [ps(f"p_turn{u}", [P, 512]) for u in range(2)]
            p_a, p_h, p_m = ps("p_logits_values", [P, PAIR, 256]), ps("p_heads", [P, 512]), ps("p_max", [P, 2, PAIR * P])
            heads = lambda s: p_h[:, s * D:(s + 1) * D].rearrange("p (h c) -> p h c", h=HEADS)
            MG, SUM = 2 * D, 2 * D + PAIR * HEADS

            pay_in = [semi(f"pay_in{u}") for u in range(4)]
            xg_in = [semi(f"xg_in{u}") for u in range(4)]
            names = ("rows_used", "hot_made", "front_turned", "front_copied", "front_done", "a_done", "f_turned", "f_copied", "logits_done",
                     "tanh_done", "g_turned", "g_copied", "heads_done", "a3_made", "a3_turned", "a3_copied", "masked", "max_taken", "max_made", "max_gathered",
                     "shrink_done", "ea_made", "ex_done", "b_done", "z_made", "summed", "acc_done", "cleared", "steps", "pe_seen", "pool_seen", "sp_seen", "dve_seen")
            m = {n: semi(n) for n in names}
            at = lambda it, u, off=0, per=1, k=None: it * (TURN * per) + ((u + off + 1) * per + (per if k is None else k))
            twice = ("f_turned", "f_copied", "g_turned", "g_copied", "masked", "max_taken")
            once = ("hot_made", "front_turned", "front_copied", "front_done", "a_done", "logits_done", "tanh_done", "heads_done",
                    "a3_made", "a3_turned", "a3_copied", "max_made", "max_gathered", "shrink_done", "ea_made", "ex_done", "b_done",
                    "z_made", "summed", "acc_done")
            PT = 4 * P
            with nc.Block() as block:
                @block.sync
                def _(sp):
                    sp.wait_ge(m["cleared"], 1)
                    def load(turn, u):
                        sp.wait_ge(m["rows_used"], turn + 1)
                        sp.sem_inc(m["sp_seen"], 1)
                        sp.dma_start(pay[u][:, :, :], K["rows_d"][bass.ds(turn * (PAIR * P), PAIR * P), :].rearrange("(s p) w -> p s w", p=P)).then_inc(pay_in[u], 16)

                    with sp.Fori(0, TURNS // TURN) as it:
                        for u in range(TURN):
                            load(it * TURN + u, u)
                    load(TURNS, 0)

                @block.gpsimd
                def _(pool):
                    pool.wait_ge(m["cleared"], 1)
                    with pool.Fori(0, TURNS // TURN) as it:
                        for u in range(TURN):
                            pool.wait_ge(pay_in[u], it * 16 + 16)
                            pool.sem_inc(m["pool_seen"], 1)
                            for s in range(PAIR):
                                pool.indirect_dma_start(xg[u][:, s, :], None, K["table0"],
                                                        bass.IndirectOffsetOnAxis(ap=pay[u][:, s, D_SRC:D_SRC + 1].bitcast(U32), axis=0)).then_inc(xg_in[u], 16)

                @block.tensor
                def _(pe):
                    bin_reg = pe.alloc_register("l3_pe_bin")

                    def wait(n, v):
                        pe.wait_ge(m[n], v)
                        pe.sem_inc(m["pe_seen"], 1)

                    wait("cleared", 1)
                    with pe.Fori(0, TURNS // TURN) as it:
                        for u in range(TURN):
                            t = lambda off=0, per=1, k=None: at(it, u, off, per, k)
                            prev, prev2, prev3 = (u - 1) % 4, (u - 2) % 4, (u - 3) % 4
                            wait("hot_made", t())
                            wait("a3_copied", t(-1))
                            for s in range(PAIR):
                                nc.tensor.transpose(p_f[:, s * P:(s + 1) * P], hot[u][:, s, :], K["ident"][:, :])
                            nc.tensor.transpose(p_f[0:PW, 2 * P:3 * P], pay[u][:, :, :].rearrange("p s w -> p (s w)"), K["ident"][:, :]).then_inc(m["front_turned"], 1)
                            wait("front_copied", t())
                            wait("a_done", t(-1))
                            pe.reg_load([bin_reg], bins[0:1, bass.ds((it * TURN + u) * PAIR + LEAD, 1)])
                            b = pe.snap(bin_reg, min_val=0, max_val=NB - 1)
                            for s in range(PAIR):
                                nc.tensor.matmul(p_w[:, s, 0:WN], pay_t[:, :], w_rbf[:, s, :], start=True, stop=True)
                            for s in range(PAIR):
                                ins = nc.tensor.matmul(p_d[:, s * D:(s + 1) * D], hot_t[u][:, s * P:(s + 1) * P], tab_d[:, bass.ds(b, 1), :].rearrange("p o f -> p (o f)"), start=True, stop=True)
                            ins.then_inc(m["front_done"], 1)
                            wait("a3_made", t(-1))
                            for s in range(PAIR):
                                ins = nc.tensor.transpose(p_a3[:, s * P:(s + 1) * P], a3[:, s, :, :].rearrange("p k h -> p (k h)"), ident_b[:, :])
                            ins.then_inc(m["a3_turned"], 1)

                            def masked(half):
                                for j in range(2):
                                    nc.tensor.matmul(p_m[:, j, :], sel[:, 2 * half + j, :], a3_t[:, :], start=True, stop=False)
                                    ins = nc.tensor.matmul(p_m[:, j, :], apart[:, :], hot_tb[prev2][:, :], start=False, stop=True)
                                ins.then_inc(m["masked"], 1)

                            wait("a3_copied", t())
                            wait("max_taken", t(-1, 2))
                            masked(0)
                            wait("z_made", t(-1))
                            wait("acc_done", t(-1))
                            for s in range(PAIR):
                                ins = nc.tensor.matmul(p_h[:, SUM:SUM + HEADS * HW], hot[prev3][:, s, :], Z[:, s, :, :].rearrange("p h c -> p (h c)"), start=s == 0, stop=s == PAIR - 1)
                            ins.then_inc(m["summed"], 1)
                            wait("g_copied", t(-1, 2))
                            for s in range(PAIR):
                                for c in range(4):
                                    ins = nc.tensor.transpose(p_t[s][:, c * P:(c + 1) * P], F[prev % 2][:, s, c, :], K["ident"][:, :])
                                ins.then_inc(m["f_turned"], 1)
                            wait("b_done", t(-1))
                            for s in range(PAIR):
                                wait("f_copied", t(0, 2, s + 1))
                                nc.tensor.matmul(p_a[:, s, 0:D], f_t[s][:, 0:P], w_a[:, :], start=True, stop=True)
                                for i in range(3):
                                    ins = nc.tensor.matmul(p_a[:, s, D + CV * i:D + CV * (i + 1)], f_t[s][:, (i + 1) * P:(i + 2) * P], w_v[:, :], start=True, stop=True)
                            ins.then_inc(m["logits_done"], 1)
                            wait("acc_done", t())
                            for s in range(PAIR):
                                for c in range(4):
                                    ins = nc.tensor.transpose(p_t[s][:, c * P:(c + 1) * P], G_[prev2 % 2][:, s, c, :], K["ident"][:, :])
                                ins.then_inc(m["g_turned"], 1)
                            for s in range(PAIR):
                                wait("g_copied", t(0, 2, s + 1))
                                split = lambda w, n: w.rearrange("p (h c) -> p h c", c=n)
                                nc.tensor.matmul(heads(s)[:, :, 0:AS], g_t[s][:, 0:P], split(w_hs[:, :], AS), start=True, stop=True)
                                for i in range(3):
                                    ins = nc.tensor.matmul(heads(s)[:, :, AS + AV * i:AS + AV * (i + 1)], g_t[s][:, (i + 1) * P:(i + 2) * P], split(w_hv[:, :], AV), start=True, stop=True)
                            ins.then_inc(m["heads_done"], 1)
                            wait("max_taken", t(0, 2, 1))
                            masked(1)
                            wait("max_made", t())
                            for s in range(PAIR):
                                ins = nc.tensor.matmul(p_h[:, MG + s * HEADS:MG + (s + 1) * HEADS], hot_t[prev2][:, s * P:(s + 1) * P], mn[:, :], start=True, stop=True)
                            ins.then_inc(m["max_gathered"], 1)

                @block.scalar
                def _(act):
                    act.wait_ge(m["cleared"], 1)
                    with act.Fori(0, TURNS // TURN) as it:
                        for u in range(TURN):
                            t = lambda off=0, per=1, k=None: at(it, u, off, per, k)
                            act.wait_ge(m["front_turned"], t())
                            act.wait_ge(m["front_done"], t(-1))
                            nc.scalar.copy(hot_t[u][:, :], p_f[:, 0:2 * P])
                            nc.scalar.copy(hot_tb[u][:, :], p_f[:, 0:2 * P])
                            nc.scalar.copy(pay_t[:, :], p_f[0:PW, 2 * P:3 * P]).then_inc(m["front_copied"], 1)
                            act.wait_ge(m["a3_turned"], t())
                            act.wait_ge(m["masked"], t(-1, 2))
                            nc.scalar.copy(a3_t[:, :], p_a3).then_inc(m["a3_copied"], 1)
                            act.wait_ge(m["logits_done"], t(-1))
                            for s in range(PAIR):
                                act.wait_ge(m["f_turned"], t(0, 2, s + 1))
                                nc.scalar.copy(f_t[s][:, :], p_t[s][:, :]).then_inc(m["f_copied"], 1)
                            act.wait_ge(m["logits_done"], t())
                            act.wait_ge(m["b_done"], t(-1))
                            nc.scalar.activation(slope[:, :, :], p_a[:, :, 0:CS], ACT.Copy, scale=0.2)
                            nc.scalar.activation(th[:, :, :], p_a[:, :, CS:D], ACT.Tanh, scale=0.5).then_inc(m["tanh_done"], 1)
                            act.wait_ge(m["heads_done"], t(-1))
                            for s in range(PAIR):
                                act.wait_ge(m["g_turned"], t(0, 2, s + 1))
                                nc.scalar.copy(g_t[s][:, :], p_t[s][:, :]).then_inc(m["g_copied"], 1)
                            act.wait_ge(m["max_made"], t())
                            nc.scalar.activation(shrink[:, :], drop[:, :], ACT.Exp).then_inc(m["shrink_done"], 1)
                            act.wait_ge(m["ea_made"], t())
                            act.wait_ge(m["summed"], t())
                            nc.scalar.activation(Z[:, :, :, HW - 1], ea[:, :, :], ACT.Exp).then_inc(m["ex_done"], 1)

                @block.vector
                def _(dve):
                    v = Steps(dve, m["steps"])
                    for w in (pay, xg, hot, hot_t, hot_tb, F, G_):
                        for t_ in w:
                            nc.vector.memset(t_[...], 0.0)
                    for t_ in (a3, Z, acc, shrink, mn, ea, logit[0], logit[1], drop):
                        nc.vector.memset(t_[...], 0.0)
                    v.done(nc.vector.memset(top[:, :, :], -NEVER))
                    v.after()
                    dve.sem_inc(m["rows_used"], 3)
                    for n in once:
                        dve.sem_inc(m[n], 1)
                    for n in twice:
                        dve.sem_inc(m[n], 2)
                    dve.sem_inc(m["cleared"], 1)
                    bin_c, bin_e = dve.alloc_register("l3_bin_c"), dve.alloc_register("l3_bin_e")
                    TT = nc.vector.tensor_tensor

                    def product(v, s_, sv, vs, vv0, vv1, pay_, out):
                        y0 = lambda *d: free(pay_[:, 0, D_E4:D_E4 + 1], [WORDS_D, PAIR], *d)
                        y1 = lambda i, *d: free(pay_[:, 0, D_E4 + 1 + i:D_E4 + 2 + i], [WORDS_D, PAIR], *d)
                        parts = lambda c, n: free(out[:, 0, 1, c:c + 1], [PT, PAIR], [P, 3], [1, n])
                        s_(out[:, :, 0, 0:CS], y0([0, CS]))
                        sv(parts(0, CS), y1(0, [1, 3], [0, CS]))
                        v.done(TT(dots[:, :, :, :], vv0(0, 3), y1(0, [1, 3], [0, CV]), ALU.mult))
                        d0 = v.k
                        v.done(TT(crossed[:, :, 0:2, :], vv1(1, 2), y1(2, [1, 2], [0, CV]), ALU.mult))
                        v.done(TT(crossed[:, :, 2, :], vv1(0, 1)[:, :, 0, :], y1(1, [0, CV]), ALU.mult))
                        v.done(TT(cross2[:, :, 0, :], vv1(2, 1)[:, :, 0, :], y1(1, [0, CV]), ALU.mult))
                        v.done(TT(cross2[:, :, 1:3, :], vv1(0, 2), y1(2, [1, 2], [0, CV]), ALU.mult))
                        c0 = v.k
                        v.after(d0)
                        v.done(TT(dots[:, :, 0, :], dots[:, :, 0, :], dots[:, :, 1, :], ALU.add))
                        d0 = v.k
                        v.done(TT(parts(CS, CV), vs(0, 3), y0([0, 3], [0, CV]), ALU.mult))
                        v.after(c0)
                        v.done(TT(parts(MS, CV), crossed[:, :, :, :], cross2[:, :, :, :], ALU.subtract))
                        v.after(d0)
                        return TT(out[:, :, 0, CS:MS], dots[:, :, 0, :], dots[:, :, 2, :], ALU.add)

                    def onehot(u, loaded):
                        dve.wait_ge(pay_in[u], loaded)
                        TT(hot[u][:, :, :], free(K["iota_f"][:, 1:2], [0, PAIR], [1, P]),
                           free(pay[u][:, 0, D_LOC:D_LOC + 1], [WORDS_D, PAIR], [0, P]), ALU.is_equal).then_inc(m["hot_made"], 1)

                    onehot(0, 16)
                    w = Steps(dve, m["steps"], per=TURN * 39, base=v.k)
                    with dve.Fori(0, TURNS // TURN) as it:
                        w.begin(it)
                        for u in range(TURN):
                            t = lambda off=0, per=1, k=None: at(it, u, off, per, k)
                            now, prev = u % 4, (u - 1) % 4
                            dve.reg_load([bin_e], bins[0:1, bass.ds((it * TURN + u) * PAIR, 1)])
                            dve.reg_load([bin_c], bins[0:1, bass.ds((it * TURN + u) * PAIR + PAIR, 1)])
                            be, bc = dve.snap(bin_e, min_val=0, max_val=NB - 1), dve.snap(bin_c, min_val=0, max_val=NB - 1)
                            dve.wait_ge(m["masked"], t(0, 2, 1))
                            nc.vector.tensor_reduce(qm[:, 0:2], p_m[:, :, :], AX.X, ALU.max).then_inc(m["max_taken"], 1)
                            dve.wait_ge(m["shrink_done"], t(-1))
                            dve.wait_ge(m["acc_done"], t(-1))
                            acc_b = acc[:, bass.ds(be, 1), :, :].rearrange("p o h c -> p (o h) c")
                            w.done(TT(acc_b, acc_b, free(shrink[:, :], [1, HEADS], [0, HW]), ALU.mult))
                            dve.wait_ge(m["summed"], t())
                            w.after()
                            TT(acc_b, acc_b, p_h[:, SUM:SUM + HEADS * HW].rearrange("p (h c) -> p h c", h=HEADS), ALU.add).then_inc(m["acc_done"], 1)
                            dve.wait_ge(m["front_done"], t())
                            dve.wait_ge(xg_in[u], it * (16 * PAIR) + 16 * PAIR)
                            w.done(TT(msg[:, :, :], p_d[:, 0:2 * D].rearrange("p (s f) -> p s f", s=PAIR), xg[u][:, :, :], ALU.add))
                            w.after()
                            w.done(TT(us[:, :, :, :], p_w[:, :, 0:2 * CS].rearrange("p s (a c) -> p s a c", a=2), free(msg[:, :, 0:1], [D, PAIR], [0, 2], [1, CS]), ALU.mult))
                            for i in range(3):
                                w.done(TT(uv[:, :, i, :, :], p_w[:, :, 2 * CS:WN].rearrange("p s (a c) -> p s a c", a=3),
                                          free(msg[:, 0, CS + CV * i:CS + CV * i + 1], [D, PAIR], [0, 3], [1, CV]), ALU.mult))
                            dve.wait_ge(m["f_turned"], t(-1, 2))
                            w.after()
                            v_of = lambda a: lambda i, n: uv[:, :, i:i + n, a, :]
                            product(w, lambda o, y: w.done(TT(o, us[:, :, 0, :], y, ALU.mult)),
                                    lambda o, y: w.done(TT(o, free(us[:, 0, 1, 0:1], [2 * CS, PAIR], [0, 3], [1, CS]), y, ALU.mult)),
                                    v_of(0), v_of(1), v_of(2), pay[u], F[u % 2]).then_inc(m["a_done"], 1)
                            dve.wait_ge(m["masked"], t(0, 2, 2))
                            nc.vector.tensor_reduce(qm[:, 2:4], p_m[:, :, :], AX.X, ALU.max).then_inc(m["max_taken"], 1)
                            dve.wait_ge(m["max_taken"], t(0, 2, 2))
                            top_b = top[:, bass.ds(bc, 1), :].rearrange("p o h -> p (o h)")
                            w.done(TT(mn[:, :], top_b, qm[:, :], ALU.max))
                            w.after()
                            w.done(TT(drop[:, :], top_b, mn[:, :], ALU.subtract))
                            w.after()
                            dve.sem_inc(m["dve_seen"], 1)
                            nc.vector.tensor_copy(top_b, mn[:, :]).then_inc(m["max_made"], 1)
                            dve.wait_ge(m["tanh_done"], t())
                            w.done(TT(leaky[:, :, :], p_a[:, :, 0:CS], slope[:, :, :], ALU.max))
                            w.done(nc.vector.tensor_scalar(none[:, :], pay[prev][:, :, D_LOC], 0.5, -NEVER, ALU.is_lt, ALU.mult))
                            w.after()
                            w.done(TT(leaky[:, :, :], leaky[:, :, :], free(alpha_dot[:, :], [0, PAIR], [1, CS]), ALU.mult))
                            w.after()
                            w.done(nc.vector.tensor_reduce(lsum[:, :, :], leaky[:, :, :].rearrange("p s (h c) -> p s h c", h=HEADS), AX.X, ALU.add))
                            w.after()
                            lk = logit[prev % 2]
                            w.done(TT(lk[:, :, :], lsum[:, :, :], free(none[:, :], [1, PAIR], [0, HEADS]), ALU.add))
                            dve.wait_ge(m["a3_turned"], t())
                            w.after()
                            w.done(nc.vector.tensor_copy(a3[:, :, 0, :], lk[:, :, :]))
                            w.after()
                            w.done(TT(rest[:, :, 0, :], lk[:, :, :], a3[:, :, 0, :], ALU.subtract))
                            w.after()
                            w.done(nc.vector.tensor_copy(a3[:, :, 1, :], rest[:, :, 0, :]))
                            w.after()
                            w.done(TT(rest[:, :, 1, :], rest[:, :, 0, :], a3[:, :, 1, :], ALU.subtract))
                            w.after()
                            nc.vector.tensor_copy(a3[:, :, 2, :], rest[:, :, 1, :]).then_inc(m["a3_made"], 1)
                            dve.wait_ge(m["max_gathered"], t())
                            dve.wait_ge(m["ex_done"], t(-1))
                            TT(ea[:, :, :], logit[(u - 2) % 2][:, :, :], p_h[:, MG:SUM].rearrange("p (s h) -> p s h", s=PAIR), ALU.subtract).then_inc(m["ea_made"], 1)
                            dve.wait_ge(m["g_turned"], t(-1, 2))
                            w.done(nc.vector.tensor_scalar(sg[:, :, :], th[:, :, :], 1.0, None, ALU.add))
                            w.after()
                            w.done(TT(val_v[:, :, :, :], free(sg[:, 0, CS:CS + 1], [MS, PAIR], [0, 3], [1, CV]),
                                      p_a[:, :, D:256].rearrange("p s (i c) -> p s i c", i=3), ALU.mult))
                            w.after()
                            vv = lambda i, n: val_v[:, :, i:i + n, :]
                            product(w, lambda o, y: w.done(TT(o, sg[:, :, 0:CS], y, ALU.mult)),
                                    lambda o, y: w.done(TT(o, free(sg[:, 0, 0:1], [MS, PAIR], [0, 3], [1, CS]), y, ALU.mult)),
                                    vv, vv, vv, pay[prev], G_[prev % 2]).then_inc(m["b_done"], 1)
                            onehot((u + 1) % 4, it * 16 + 16 * ((u + 1) // 4 + 1))
                            dve.wait_ge(m["ex_done"], t())
                            dve.wait_ge(m["heads_done"], t())
                            for s, done in ((0, "rows_used"), (1, "z_made")):
                                TT(Z[:, s, :, 0:HW - 1], heads(s), free(Z[:, s, 0, HW - 1:HW], [HW, HEADS], [0, HW - 1]), ALU.mult).then_inc(m[done], 1)
                        w.end()

        with ExitStack() as inner:
            sbi = lambda n, s, d=F32: inner.enter_context(nc.sbuf_tensor("l3_" + n, s, d))
            semi = inner.enter_context(Semaphores(nc))
            den, agg, upd = sbi("weight_sums", [P, NB, HEADS]), sbi("head_means", [P, NB, D]), sbi("update", [P, NB, D])
            steps, x_done = semi("steps"), semi("x_done")
            with nc.Block() as block:
                @block.vector
                def _(dve):
                    v = Steps(dve, steps)
                    v.link(nc.vector.tensor_scalar(den[:, :, :], acc[:, :, :, HW - 1], 1e-16, None, ALU.add))
                    v.link(nc.vector.reciprocal(den[:, :, :], den[:, :, :]))
                    for h in range(HEADS):
                        over = lambda n: free(den[:, 0, h:h + 1], [HEADS, NB], [0, n])
                        v.done(nc.vector.tensor_tensor(agg[:, :, h * AS:(h + 1) * AS], acc[:, :, h, 0:AS], over(AS), ALU.mult))
                        for i in range(3):
                            c = CS + CV * i + h * AV
                            v.done(nc.vector.tensor_tensor(agg[:, :, c:c + AV], acc[:, :, h, AS + AV * i:AS + AV * (i + 1)], over(AV), ALU.mult))
                    v.after()
            stage_project(nc, K, agg, wp1, wp2, None, upd, None, "l3q")
            with nc.Block() as block:
                @block.vector
                def _(dve):
                    v = Steps(dve, x_done)
                    for t_ in (H, upd):
                        v.link(nc.vector.tensor_tensor(K["X"][:, :, :], K["X"][:, :, :], t_[:, :, :], ALU.add))


def build(nc, A, out):
    with ExitStack() as ctx:
        K = consts(nc, ctx, A)
        stage_setup(nc, A, K)
        stage_sort(nc, A, K)
        stage_layer0(nc, A, K)
        stage_layer1(nc, A, K)
        stage_layer2(nc, A, K)
        stage_layer3(nc, A, K)
        stage_finish(nc, A, K, out)


def kernel(**inputs):
    import concourse.bacc as bacc
    from concourse.bass_utils import run_bass_kernel_spmd

    nc = bacc.Bacc("TRN2", target_bir_lowering=False, num_devices=1)
    arrays, A = {}, {}
    for name, value in inputs.items():
        a = np.ascontiguousarray(value)
        arrays["in_" + name] = a
        A[name] = nc.dram_tensor("in_" + name, a.shape, mybir.dt.from_np(a.dtype), kind="ExternalInput").ap()
    out = nc.dram_tensor("out_x", (N, D), F32, kind="ExternalOutput").ap()
    build(nc, A, out)
    r = run_bass_kernel_spmd(nc, [arrays], core_ids=[0])
    return r.results[0]["out_x"]
```

```python
import itertools
from contextlib import ExitStack

import numpy as np

import concourse.bass as bass
from concourse import mybir

ALU = mybir.AluOpType
ACT = mybir.ActivationFunctionType
AX = mybir.AxisListType
F32 = mybir.dt.float32
F16 = mybir.dt.float16
I32 = mybir.dt.int32
U32 = mybir.dt.uint32

P = 128
N = 3125
E = 103125
D = 160
CS, CV = 64, 32
NB = -(-N // P)
NP = NB * P
LN_EPS = 1e-5

TPC = 28
CHUNK = P * TPC
NCH = -(-E // CHUNK)
NT = NCH * TPC
TAIL = E - (NCH - 1) * CHUNK
TAIL_P, TAIL_R = divmod(TAIL, TPC)

G = 8
BINS_D = NB
BINS_S = -(-N // G)
ALL_D = BINS_D + 1
ALL_S = BINS_S + 1
BINS = ALL_S + ALL_D
QUAD = 4
QUADS_D = -(-((E + BINS_D * (QUAD * P - 1)) // (QUAD * P)) // 2) * 2
SLOTS_D = QUADS_D * QUAD
BATCH_S = 16
SLOTS_S = -(-((E + BINS_S * (P - 1)) // P) // BATCH_S) * BATCH_S
PADS = -(-(NT * P - E) // P) + 1
ROWS_D = (SLOTS_D + max(PADS, 6 * QUAD)) * P
ROWS_S = (SLOTS_S + max(PADS, BATCH_S)) * P

D_SRC, D_LOC, D_E4, D_AGAIN, D_E12, D_E16 = 0, 1, 2, 6, 8, 20
WORDS_D = 36
PAIR = 2
PW = PAIR * WORDS_D
S_DST, S_LOC, S_E4, S_E32 = 0, 1, 2, 6
WORDS_S = 38


class Semaphores:

    stages = itertools.count()

    def __init__(self, nc):
        self.nc, self.handles, self.stage = nc, [], next(self.stages)

    def __enter__(self):
        return self

    def __call__(self, name):
        self.handles.append(self.nc.alloc_semaphore(name=f"{name}_{self.stage}"))
        return self.handles[-1]

    def __exit__(self, *error):
        if error[0] is None:
            self.nc.clear_and_free_semaphores(self.handles)
            self.nc.all_engine_barrier()


class Steps:

    def __init__(self, eng, sem, per=0, base=0):
        self.eng, self.sem, self.per, self.base, self.turn, self.k = eng, sem, per, base, None, 0

    def begin(self, turn):
        self.turn, self.k = turn, 0

    def done(self, ins):
        ins.then_inc(self.sem, 1)
        self.k += 1
        return self.k

    def value(self, k):
        return self.base + k if self.turn is None else self.turn * self.per + (self.base + k)

    def after(self, k=None):
        self.eng.wait_ge(self.sem, self.value(self.k if k is None else k))

    def link(self, ins):
        self.done(ins)
        self.after()

    def end(self):
        assert self.turn is None or self.k == self.per, (self.k, self.per)


def free(ap, *dims):
    return bass.AP(ap.tensor, ap.offset, [list(ap.ap[0])] + [list(d) for d in dims])


def by_part(v, axis_i):
    return v[..., CS + axis_i:D:3]


def stage_setup(nc, A, K):
    with ExitStack() as ctx:
        sb = lambda n, s, d=F32: ctx.enter_context(nc.sbuf_tensor(n, s, d))
        sem = ctx.enter_context(Semaphores(nc))
        raw = sb("x_raw", [P, NB, D])
        x_in, x_padded, dve_steps, iota_done = sem("x_in"), sem("x_padded"), sem("dve_steps"), sem("iota_done")
        last = N - (NB - 1) * P
        with nc.Block() as block:
            @block.sync
            def _(sp):
                sp.wait_ge(x_padded, 1)
                sp.dma_start(raw[:, 0:NB - 1, :], A["x"][0:(NB - 1) * P, :].rearrange("(b p) f -> p b f", p=P)).then_inc(x_in, 16)
                sp.dma_start(raw[0:last, NB - 1, :], A["x"][(NB - 1) * P:N, :]).then_inc(x_in, 16)
                sp.dma_start(K["z"][:, 0:NB - 1], A["node_vec1"][0:(NB - 1) * P, :].rearrange("(b p) o -> p (b o)", p=P), allow_slow_non_contiguous=True).then_inc(x_in, 16)
                sp.dma_start(K["z"][0:last, NB - 1:NB], A["node_vec1"][(NB - 1) * P:N, :]).then_inc(x_in, 16)
                sp.wait_ge(x_in, 64)

            @block.gpsimd
            def _(pool):
                st = Steps(pool, iota_done)
                st.done(nc.gpsimd.iota(K["iota_i"][:, :], pattern=[[1, 512]], base=0, channel_multiplier=0))
                st.done(nc.gpsimd.iota(K["part_i"][:, :], pattern=[[0, 1]], base=0, channel_multiplier=1))
                st.done(nc.gpsimd.iota(K["slot_i"][:, :], pattern=[[P, 10]], base=0, channel_multiplier=1))

            @block.vector
            def _(dve):
                v = Steps(dve, dve_steps)
                nc.vector.memset(raw[:, NB - 1, :], 0.0)
                nc.vector.memset(K["z"][:, NB - 1:NB], 0.0).then_inc(x_padded, 1)
                dve.wait_ge(iota_done, 3)
                v.done(nc.vector.tensor_copy(K["iota_f"][:, :], K["iota_i"][:, :]))
                v.done(nc.vector.tensor_copy(K["part_f"][:, :], K["part_i"][:, :]))
                v.done(nc.vector.tensor_copy(K["slot_f"][:, :], K["slot_i"][:, :]))
                v.link(nc.vector.tensor_copy(K["iota_h"][:, :], K["iota_i"][:, :]))
                v.done(nc.vector.tensor_scalar(K["ident"][:, :], K["iota_f"][:, 0:P], K["part_f"][:, 0:1], None, ALU.is_equal))
                v.done(nc.vector.tensor_scalar(K["lower_h"][:, :], K["iota_f"][:, 0:P], K["part_f"][:, 0:1], None, ALU.is_gt))
                v.done(nc.vector.memset(K["ones_h"][:, :], 1.0))
                v.done(nc.vector.memset(K["slotsize_h"][:, :], float(P)))
                v.done(nc.vector.tensor_scalar(K["part1_f"][:, :], K["part_f"][:, :], 1.0, None, ALU.add))
                dve.wait_ge(x_in, 64)
                v.done(nc.vector.tensor_copy(K["X"][:, :, 0:CS], raw[:, :, 0:CS]))
                for i in range(3):
                    v.done(nc.vector.tensor_copy(K["X"][:, :, CS + CV * i:CS + CV * (i + 1)], by_part(raw, i)))
                v.after()


def stage_sort(nc, A, K):
    with ExitStack() as ctx:
        sb = lambda n, s, d=F32: ctx.enter_context(nc.sbuf_tensor(n, s, d))
        sem = ctx.enter_context(Semaphores(nc))
        src = sb("src_i", [P, NCH, TPC], I32)
        dst = sb("dst_i", [P, NCH, TPC], I32)
        key_i = sb("key_i", [P, NT], I32)
        key_s = sb("key_s", [P, NT])
        key_d = sb("key_d", [P, NT])
        loc_i = sb("loc_i", [P, NT], I32)
        loc_s = sb("loc_s", [P, NT])
        loc_d = sb("loc_d", [P, NT])
        onehot = sb("onehot", [P, 4, BINS], F16)
        before = sb("before", [P, 4, BINS], F16)
        total = sb("total", [P, BINS])
        slots_i = sb("slots_i", [P, BINS], I32)
        slots = sb("slots", [P, BINS])
        upto = sb("upto", [P, BINS])
        start_h = sb("start_h", [1, BINS], F16)
        junk = sb("junk", [P, 4, BINS], F16)
        bin_f = sb("bin_f", [P, 20])
        bin_i = sb("bin_i", [P, 20], I32)
        ea4 = sb("ea4", [P, 2, TPC, 4])
        ea12 = sb("ea12", [P, 2, TPC, 12])
        ea16 = sb("ea16", [P, 2, TPC, 16])
        ea32 = sb("ea32", [P, 2, TPC, 32])
        row_d = sb("row_d", [P, 2, TPC, WORDS_D])
        row_s = sb("row_s", [P, 2, TPC, WORDS_S])
        pos = sb("pos", [P, 2, 2, TPC])
        pos_i = sb("pos_i", [P, 2, 2, TPC], I32)
        LO = 32
        HI = -(-ALL_S // LO)
        ROW = LO + ALL_D
        zero_h = sb("zero_h", [P, ROW], F16)
        zero = sb("zero_rows", [P, 2048])
        hi_i, lo_i, key_hi, key_lo = sb("hi_i", [P, NT], I32), sb("lo_i", [P, NT], I32), sb("key_hi", [P, NT]), sb("key_lo", [P, NT])
        rows_hot = [sb(f"rows_onehot{k}", [P, TPC, HI + 1], F16) for k in range(2)]
        cols_hot = [sb(f"cols_onehot{k}", [P, TPC, ROW], F16) for k in range(2)]
        table, row_of = sb("hist_table", [HI + 1, ROW]), sb("hist_row_of", [HI + 1, HI + 1, P])
        counts = ctx.enter_context(nc.psum_tensor("hist_counts", [HI + 1, 512], F32))
        hist = ctx.enter_context(nc.psum_tensor("hist", [P, 512], F32))
        rank = ctx.enter_context(nc.psum_tensor("rank", [P, 4, 512], F32))
        RS, RD = slice(0, ALL_S), slice(ALL_S, BINS)

        keys_in, keys_padded, keys_ready, dve_steps = sem("keys_in"), sem("keys_padded"), sem("keys_ready"), sem("dve_steps")
        hist_hot, hist_added, hist_done = sem("hist_hot"), sem("hist_added"), sem("hist_done")
        hist_counted, hist_copied = sem("hist_counted"), sem("hist_copied")
        bins_out, cleared, zeros_written = sem("bins_out"), sem("cleared"), sem("zeros_written")
        with nc.Block() as block:
            @block.sync
            def _(sp):
                sp.wait_ge(keys_padded, 2)
                for name, tile in (("src", src), ("dst", dst)):
                    a = A[name]
                    sp.dma_start(tile[:, 0:NCH - 1, :], a[0:(NCH - 1) * CHUNK].rearrange("(c p t) -> p c t", p=P, t=TPC)).then_inc(keys_in, 16)
                    at = (NCH - 1) * CHUNK
                    sp.dma_start(tile[0:TAIL_P, NCH - 1, :], a[at:at + TAIL_P * TPC].rearrange("(p t) -> p t", t=TPC)).then_inc(keys_in, 16)
                    sp.dma_start(tile[TAIL_P:TAIL_P + 1, NCH - 1, 0:TAIL_R], a[at + TAIL_P * TPC:E].rearrange("(p t) -> p t", p=1)).then_inc(keys_in, 16)
                sp.wait_ge(keys_ready, 2)
                sp.dma_start(K["bins_s"].rearrange("(c p) -> p c", p=P), bin_i[:, 0:10], allow_slow_non_contiguous=True).then_inc(bins_out, 16)
                sp.dma_start(K["bins_d"].rearrange("(c p) -> p c", p=P), bin_i[:, 10:20], allow_slow_non_contiguous=True).then_inc(bins_out, 16)
                sp.wait_ge(bins_out, 32)

            @block.vector
            def _(dve):
                v = Steps(dve, dve_steps)
                nc.vector.memset(src[:, NCH - 1, :], BINS_S * G).then_inc(keys_padded, 1)
                nc.vector.memset(dst[:, NCH - 1, :], BINS_D * P).then_inc(keys_padded, 1)
                nc.vector.memset(zero[:, :], 0.0).then_inc(cleared, 1)
                v.done(nc.vector.memset(zero_h[:, :], 0.0))
                v.done(nc.vector.memset(before[:, 0, :], 0.0))
                dve.wait_ge(keys_in, 96)
                flat = lambda t: t[:, :, :].rearrange("p c t -> p (c t)")
                sG, sP = G.bit_length() - 1, P.bit_length() - 1
                v.done(nc.vector.tensor_scalar(key_i[:, :], flat(src), sG, None, ALU.arith_shift_right))
                v.done(nc.vector.tensor_scalar(loc_i[:, :], flat(src), G - 1, None, ALU.bitwise_and))
                v.after()
                v.done(nc.vector.tensor_copy(key_s[:, :], key_i[:, :]))
                v.done(nc.vector.tensor_scalar(hi_i[:, :], key_i[:, :], LO.bit_length() - 1, None, ALU.arith_shift_right))
                v.done(nc.vector.tensor_scalar(lo_i[:, :], key_i[:, :], LO - 1, None, ALU.bitwise_and))
                v.done(nc.vector.tensor_scalar(loc_s[:, :], loc_i[:, :], 1.0, None, ALU.add))
                v.after()
                v.done(nc.vector.tensor_copy(key_hi[:, :], hi_i[:, :]))
                v.done(nc.vector.tensor_copy(key_lo[:, :], lo_i[:, :]))
                v.done(nc.vector.scalar_tensor_tensor(loc_s[:, :], key_s[:, :], float(BINS_S), loc_s[:, :], ALU.is_lt, ALU.mult))
                v.done(nc.vector.tensor_scalar(key_i[:, :], flat(dst), sP, None, ALU.arith_shift_right))
                v.done(nc.vector.tensor_scalar(loc_i[:, :], flat(dst), P - 1, None, ALU.bitwise_and))
                v.after()
                v.done(nc.vector.tensor_copy(key_d[:, :], key_i[:, :]))
                v.done(nc.vector.tensor_scalar(loc_d[:, :], loc_i[:, :], 1.0, None, ALU.add))
                v.after()
                v.done(nc.vector.scalar_tensor_tensor(loc_d[:, :], key_d[:, :], float(BINS_D), loc_d[:, :], ALU.is_lt, ALU.mult))
                v.done(nc.vector.tensor_scalar(flat(dst), flat(dst), float(NP - 1), None, ALU.min))
                v.after()
                nc.vector.memset(junk[:, 2, 0:1], 0.0).then_inc(keys_ready, 1)
                for k in range(2):
                    v.done(nc.vector.memset(rows_hot[k][:, :, HI:HI + 1], 1.0))
                v.done(nc.vector.tensor_scalar(row_of[:, :, :], free(K["iota_f"][0:HI + 1, 0:1], [1, HI + 1], [0, P]), K["part_f"][0:HI + 1, 0:1], None, ALU.is_equal))
                v.after()

                def hot_of(c, k):
                    dve.wait_ge(hist_added, c + 1)
                    for ins_of, at, n, key in ((rows_hot, 0, HI, key_hi), (cols_hot, 0, LO, key_lo), (cols_hot, LO, ALL_D, key_d)):
                        ins = nc.vector.tensor_tensor(ins_of[k][:, :, at:at + n], free(K["iota_f"][:, 0:1], [0, TPC], [1, n]),
                                                      free(key[:, bass.ds(c * TPC, TPC)], [1, TPC], [0, n]), ALU.is_equal)
                    ins.then_inc(hist_hot, 1)

                with dve.Fori(0, NCH // 2) as i:
                    for k in range(2):
                        hot_of(2 * i + k, k)
                hot_of(NCH - 1, 0)
                dve.wait_ge(hist_counted, 1)
                nc.vector.tensor_copy(table[:, :], counts[:, 0:ROW]).then_inc(hist_copied, 1)
                dve.wait_ge(hist_done, 1)
                sQ = (QUAD * P).bit_length() - 1
                v.done(nc.vector.tensor_scalar(slots_i[:, RS], hist[:, RS], float(P - 1), None, ALU.add))
                v.link(nc.vector.tensor_scalar(slots_i[:, RD], hist[:, HI * LO:HI * LO + ALL_D], float(QUAD * P - 1), None, ALU.add))
                v.done(nc.vector.tensor_scalar(slots_i[:, RS], slots_i[:, RS], sP, None, ALU.arith_shift_right))
                v.link(nc.vector.tensor_scalar(slots_i[:, RD], slots_i[:, RD], sQ, None, ALU.arith_shift_right))
                v.link(nc.vector.tensor_copy(slots[:, :], slots_i[:, :]))
                v.link(nc.vector.tensor_scalar(slots[:, RD], slots[:, RD], float(QUAD), None, ALU.mult))
                v.done(nc.vector.memset(total[:, :], 0.0))
                v.after()
                v.done(nc.vector.tensor_tensor_scan(upto[:, RS], slots[:, RS], total[:, RS], 0.0, ALU.add, ALU.add))
                v.link(nc.vector.tensor_tensor_scan(upto[:, RD], slots[:, RD], total[:, RD], 0.0, ALU.add, ALU.add))
                v.done(nc.vector.tensor_tensor(start_h[0:1, :], upto[0:1, :], slots[0:1, :], ALU.subtract))
                for c in range(10):
                    v.link(nc.vector.tensor_scalar(junk[:, 0, 0:BINS_S], upto[:, 0:BINS_S], K["slot_f"][:, c:c + 1], None, ALU.is_le, ALU.add, accum_out=bin_f[:, c:c + 1]))
                    v.link(nc.vector.tensor_scalar(junk[:, 1, 0:BINS_D], upto[:, ALL_S:ALL_S + BINS_D], K["slot_f"][:, c:c + 1], None, ALU.is_le, ALU.add, accum_out=bin_f[:, 10 + c:11 + c]))
                v.done(nc.vector.tensor_scalar(bin_i[:, 0:10], bin_f[:, 0:10], float(BINS_S - 1), float(G), ALU.min, ALU.mult))
                v.done(nc.vector.tensor_scalar(bin_i[:, 10:20], bin_f[:, 10:20], float(BINS_D - 1), None, ALU.min))
                v.after()
                nc.vector.memset(junk[:, 2, 0:1], 0.0).then_inc(keys_ready, 1)

            @block.tensor
            def _(pe):
                pe.wait_ge(keys_ready, 1)
                nc.tensor.matmul(counts[:, 0:ROW], zero_h[:, 0:HI + 1], zero_h[:, :], start=True, stop=False, skip_group_check=True).then_inc(hist_added, 2)

                def add(c, k):
                    pe.wait_ge(hist_hot, c + 1)
                    for t in range(TPC):
                        ins = nc.tensor.matmul(counts[:, 0:ROW], rows_hot[k][:, t, :], cols_hot[k][:, t, :], start=False, stop=False, skip_group_check=True)
                    ins.then_inc(hist_added, 1)

                with pe.Fori(0, NCH // 2) as i:
                    for k in range(2):
                        add(2 * i + k, k)
                add(NCH - 1, 0)
                nc.tensor.matmul(counts[:, 0:ROW], zero_h[:, 0:HI + 1], zero_h[:, :], start=False, stop=True, skip_group_check=True).then_inc(hist_counted, 1)
                pe.wait_ge(hist_copied, 1)
                for r in range(HI):
                    nc.tensor.matmul(hist[:, r * LO:(r + 1) * LO], row_of[:, r, :], table[:, 0:LO], start=True, stop=True)
                nc.tensor.matmul(hist[:, HI * LO:HI * LO + ALL_D], row_of[:, HI, :], table[:, LO:ROW], start=True, stop=True).then_inc(hist_done, 1)

            @block.scalar
            def _(act):
                act.wait_ge(cleared, 1)
                n = 0
                for buf, words in ((K["rows_d"], WORDS_D), (K["rows_s"], WORDS_S)):
                    flat = buf.rearrange("(p r) w -> p (r w)", p=P)
                    total = flat.shape[1]
                    for at in range(0, total, 2048):
                        w = min(2048, total - at)
                        act.dma_start(flat[:, at:at + w], zero[:, 0:w]).then_inc(zeros_written, 16)
                        n += 16
                act.wait_ge(zeros_written, n)

        with ExitStack() as ctx2:
            sem2 = ctx2.enter_context(Semaphores(nc))
            attr_in = [sem2(f"attr_in{k}") for k in range(2)]
            rows_sent = [sem2(f"rows_sent{k}") for k in range(2)]
            rows_built, hot, ranked, placed, pos_ready, pool_seen, sent = (
                sem2("rows_built"), sem2("hot"), sem2("ranked"), sem2("placed"), sem2("pos_ready"), sem2("pool_seen"), sem2("sent"))
            attrs = (("edge_attr_4", ea4, 4), ("edge_attr_12", ea12, 12), ("edge_attr_16", ea16, 16), ("edge_attr_32", ea32, 32))
            PAIRS = (NCH - 1) // 2
            SENT = 16 * 2 * TPC
            assert NCH == 2 * PAIRS + 1
            with nc.Block() as block:
                @block.sync
                def _(sp):
                    with sp.Fori(0, PAIRS) as i:
                        for k in range(2):
                            sp.wait_ge(rows_built, 2 * i + (k + 1))
                            for name, tile, w in attrs:
                                a = A[name].rearrange("e w -> (e w)")
                                sp.dma_start(tile[:, k, :, :].rearrange("p t w -> p (t w)"),
                                             a[bass.ds((2 * i + k) * (CHUNK * w), CHUNK * w)].rearrange("(p f) -> p f", p=P)).then_inc(attr_in[k], 16)
                    sp.wait_ge(rows_built, NCH)
                    for name, tile, w in attrs:
                        a = A[name].rearrange("e w -> (e w)")
                        at = (NCH - 1) * CHUNK * w
                        mid = at + TAIL_P * TPC * w
                        sp.dma_start(tile[0:TAIL_P, 0, :, :].rearrange("p t w -> p (t w)"), a[at:mid].rearrange("(p f) -> p f", p=TAIL_P)).then_inc(attr_in[0], 16)
                        sp.dma_start(tile[TAIL_P:TAIL_P + 1, 0, 0:TAIL_R, :].rearrange("p t w -> p (t w)"), a[mid:E * w].rearrange("(p f) -> p f", p=1)).then_inc(attr_in[0], 16)

                @block.scalar
                def _(act):
                    act.sem_inc(rows_built, 2)

                    def rows(c, k, loaded):
                        act.wait_ge(sent, c + 1)
                        act.wait_ge(attr_in[k], loaded)
                        cols = bass.ds(c * TPC, TPC)
                        d, s = row_d[:, k], row_s[:, k]
                        of = lambda t: t[:, bass.ds(c, 1), :].rearrange("p c t -> p (c t)")
                        nc.scalar.copy(d[:, :, D_SRC].bitcast(I32), of(src))
                        nc.scalar.copy(d[:, :, D_LOC], loc_d[:, cols])
                        nc.scalar.copy(d[:, :, D_E4:D_E4 + 4], ea4[:, k])
                        nc.scalar.copy(d[:, :, D_AGAIN:D_AGAIN + 2], ea4[:, k, :, 1:3])
                        nc.scalar.copy(d[:, :, D_E12:D_E12 + 12], ea12[:, k])
                        nc.scalar.copy(d[:, :, D_E16:D_E16 + 16], ea16[:, k])
                        nc.scalar.copy(s[:, :, S_DST].bitcast(I32), of(dst))
                        nc.scalar.copy(s[:, :, S_LOC], loc_s[:, cols])
                        nc.scalar.copy(s[:, :, S_E4:S_E4 + 4], ea4[:, k])
                        nc.scalar.copy(s[:, :, S_E32:S_E32 + 32], ea32[:, k]).then_inc(rows_built, 1)

                    with act.Fori(0, PAIRS) as i:
                        for k in range(2):
                            rows(2 * i + k, k, 64 * i + 64)
                    rows(NCH - 1, 0, 64 * PAIRS + 128)

                @block.vector
                def _(dve):
                    dve.sem_inc(placed, 4)

                    def chunk(c, k):
                        for t in range(TPC + 2):
                            if t < TPC:
                                b, tile = t % 4, c * TPC + t
                                nc.vector.tensor_scalar(onehot[:, b, RS], K["iota_h"][:, 0:ALL_S], key_s[:, bass.ds(tile, 1)], None, ALU.is_equal)
                                nc.vector.tensor_scalar(onehot[:, b, RD], K["iota_h"][:, 0:ALL_D], key_d[:, bass.ds(tile, 1)], None, ALU.is_equal).then_inc(hot, 1)
                                dve.wait_ge(hot, c * TPC + (t + 1))
                                nc.vector.tensor_tensor(before[:, (t + 1) % 4, :], before[:, b, :], onehot[:, b, :], ALU.add)
                            if t >= 2:
                                r = t - 2
                                b = r % 4
                                dve.wait_ge(ranked, c * TPC + (r + 1))
                                nc.vector.tensor_tensor_reduce(junk[:, b, RS], rank[:, b, RS], onehot[:, b, RS], 1.0, 0.0, ALU.mult, ALU.add, pos[:, k, 0, r:r + 1])
                                nc.vector.tensor_tensor_reduce(junk[:, b, RD], rank[:, b, RD], onehot[:, b, RD], 1.0, 0.0, ALU.mult, ALU.add, pos[:, k, 1, r:r + 1]).then_inc(placed, 1)
                        dve.wait_ge(sent, c + 1)
                        dve.wait_ge(placed, c * TPC + (TPC + 4))
                        nc.vector.tensor_copy(pos_i[:, k, :, :], pos[:, k, :, :]).then_inc(pos_ready, 1)

                    with dve.Fori(0, PAIRS) as i:
                        for k in range(2):
                            chunk(2 * i + k, k)
                    chunk(NCH - 1, 0)

                @block.tensor
                def _(pe):
                    with pe.Fori(0, NT // 4) as i:
                        for b in range(4):
                            pe.wait_ge(hot, 4 * i + b + 1)
                            pe.wait_ge(placed, 4 * i + b + 1)
                            nc.tensor.matmul(rank[:, b, 0:BINS], K["lower_h"][:, :], onehot[:, b, :], start=True, stop=False)
                            nc.tensor.matmul(rank[:, b, 0:BINS], K["ones_h"][:, :], before[:, b, :], start=False, stop=False)
                            nc.tensor.matmul(rank[:, b, 0:BINS], K["slotsize_h"][0:1, :], start_h[0:1, :], start=False, stop=True).then_inc(ranked, 1)

                @block.gpsimd
                def _(pool):
                    def scatter(c, k, before):
                        pool.wait_ge(pos_ready, c + 1)
                        pool.sem_inc(pool_seen, 1)
                        pool.wait_ge(rows_built, c + 3)
                        pool.sem_inc(pool_seen, 1)
                        for t in range(TPC):
                            for o, rows_, tile in ((0, K["rows_s"], row_s), (1, K["rows_d"], row_d)):
                                pool.indirect_dma_start(rows_, bass.IndirectOffsetOnAxis(ap=pos_i[:, k, o, t:t + 1].bitcast(U32), axis=0),
                                                        tile[:, k, t, :], None).then_inc(rows_sent[k], 16)
                            if t == 3 and before is not None:
                                pool.wait_ge(rows_sent[1 - k], before)
                                pool.sem_inc(sent, 1)

                    pool.sem_inc(sent, 2)
                    scatter(0, 0, None)
                    with pool.Fori(0, PAIRS) as i:
                        scatter(2 * i + 1, 1, SENT * i + SENT)
                        scatter(2 * i + 2, 0, SENT * i + SENT)
                    pool.wait_ge(rows_sent[0], SENT * (PAIRS + 1))


def consts(nc, ctx, A):
    sb = lambda n, s, d=F32: ctx.enter_context(nc.sbuf_tensor(n, s, d))
    K = {
        "X": sb("x_nodes", [P, NB, D]), "z": sb("node_attr", [P, NB]), "ident": sb("ident", [P, P]),
        "iota_i": sb("iota_i", [P, 512], I32), "iota_f": sb("iota_f", [P, 512]), "iota_h": sb("iota_h", [P, 512], F16),
        "part_i": sb("part_i", [P, 1], I32), "part_f": sb("part_f", [P, 1]), "part1_f": sb("part1_f", [P, 1]),
        "slot_i": sb("slot_i", [P, 10], I32), "slot_f": sb("slot_f", [P, 10]),
        "lower_h": sb("lower_h", [P, P], F16), "ones_h": sb("ones_h", [P, P], F16), "slotsize_h": sb("slotsize_h", [1, P], F16),
        "rows_d": nc.dram_tensor("rows_by_dst", [ROWS_D, WORDS_D], F32).ap(),
        "rows_s": nc.dram_tensor("rows_by_src", [ROWS_S, WORDS_S], F32).ap(),
        "table0": nc.dram_tensor("node_table0", [NP, D], F32).ap(),
        "table1": nc.dram_tensor("node_table1", [NP, D + 1], F32).ap(),
        "table2": nc.dram_tensor("node_table2", [NP, D + 1], F32).ap(),
        "h_turned": nc.dram_tensor("h_turned_l2", [D, NP], F32).ap(),
        "a_turned": nc.dram_tensor("sums_turned_l2", [D, NP], F32).ap(),
        "bins_s": nc.dram_tensor("bin_of_slot_s", [10 * P], I32).ap(),
        "bins_d": nc.dram_tensor("bin_of_slot_d", [10 * P], I32).ap(),
    }
    return K


def stage_norm(nc, K, H, tag):
    with ExitStack() as ctx:
        sb = lambda n, s, d=F32: ctx.enter_context(nc.sbuf_tensor(tag + "_" + n, s, d))
        sem = ctx.enter_context(Semaphores(nc))
        centred, square = sb("centred", [P, NB, D]), sb("square", [P, NB, D])
        mean, var, std, rstd, eps = (sb(n, [P, NB]) for n in ("ln_mean", "ln_var", "ln_std", "ln_rstd", "ln_eps"))
        steps, var_ready, std_ready = sem("norm_steps"), sem("var_ready"), sem("std_ready")
        over = lambda t: free(t[:, :], [1, NB], [0, D])
        with nc.Block() as block:
            @block.vector
            def _(dve):
                v = Steps(dve, steps)
                v.done(nc.vector.memset(eps[:, :], LN_EPS))
                v.link(nc.vector.tensor_reduce(mean[:, :], K["X"][:, :, :], AX.X, ALU.add))
                v.link(nc.vector.tensor_scalar(mean[:, :], mean[:, :], 1.0 / D, None, ALU.mult))
                v.link(nc.vector.tensor_tensor(centred[:, :, :], K["X"][:, :, :], over(mean), ALU.subtract))
                v.link(nc.vector.tensor_tensor(square[:, :, :], centred[:, :, :], centred[:, :, :], ALU.mult))
                nc.vector.tensor_reduce(var[:, :], square[:, :, :], AX.X, ALU.add).then_inc(var_ready, 1)
                dve.wait_ge(std_ready, 1)
                v.link(nc.vector.reciprocal(rstd[:, :], std[:, :]))
                v.link(nc.vector.tensor_tensor(square[:, :, :], centred[:, :, :], over(rstd), ALU.mult))
                v.link(nc.vector.tensor_scalar(H[:, :, :], square[:, :, :], 0.0, None, ALU.max))

            @block.scalar
            def _(act):
                act.wait_ge(var_ready, 1)
                nc.scalar.activation(std[:, :], var[:, :], ACT.Sqrt, bias=eps[:, 0:1], scale=1.0 / D).then_inc(std_ready, 1)


def stage_project(nc, K, H, W1, W2, scale, first, second, tag):
    dests = (first,) if second is None else (first, second)
    with ExitStack() as ctx:
        sb = lambda n, s, d=F32: ctx.enter_context(nc.sbuf_tensor(tag + "_" + n, s, d))
        sem = ctx.enter_context(Semaphores(nc))
        two = lambda n, s: [sb(f"{n}_{k}", s) for k in range(2)]
        bank = lambda n: [ctx.enter_context(nc.psum_tensor(f"{tag}_{n}{k}", [P, 512], F32)) for k in range(2)]
        hb, ht1, ht2 = two("h_block", [P, D]), two("h_turned1", [P, P]), two("h_turned2", [D - P, P])
        turn, out = bank("turn"), bank("proj")
        W = len(dests) * D
        taken, turned, copied, projected, stored, pool_seen = (
            sem(n) for n in ("taken", "turned", "copied", "projected", "stored", "pool_seen"))
        FREE = 2
        assert NB % 2 == 1

        def blocks(eng, step):
            with eng.Fori(0, NB // 2) as i:
                for k in range(2):
                    step(2 * i + k, k)
            step(NB - 1, 0)

        with nc.Block() as block:
            @block.gpsimd
            def _(pool):
                pool.sem_inc(copied, FREE)

                def take(b, k):
                    pool.wait_ge(turned, b + 1)
                    pool.sem_inc(pool_seen, 1)
                    nc.gpsimd.tensor_copy(hb[k][:, :], H[:, bass.ds(b, 1), :].rearrange("p o f -> p (o f)")).then_inc(taken, 1)

                blocks(pool, take)

            @block.vector
            def _(dve):
                dve.sem_inc(stored, FREE)

                def store(b, k):
                    dve.wait_ge(projected, b + (1 + FREE))
                    for n, dest in enumerate(dests):
                        to = dest[:, bass.ds(b, 1), :].rearrange("p o f -> p (o f)")
                        if scale is None:
                            ins = nc.vector.tensor_copy(to, out[k][:, n * D:(n + 1) * D])
                        else:
                            ins = nc.vector.tensor_scalar(to, out[k][:, n * D:(n + 1) * D], scale[:, bass.ds(b, 1)], None, ALU.mult)
                    ins.then_inc(stored, 1)

                blocks(dve, store)

            @block.tensor
            def _(pe):
                pe.sem_inc(turned, FREE)
                pe.sem_inc(projected, FREE)

                def turn_block(b, k):
                    pe.wait_ge(taken, b + 1)
                    pe.wait_ge(copied, b + 1)
                    nc.tensor.transpose(turn[k][:, 0:P], hb[k][:, 0:P], K["ident"][:, :])
                    nc.tensor.transpose(turn[k][0:D - P, P:2 * P], hb[k][:, P:D], K["ident"][:, :]).then_inc(turned, 1)

                def project(b, k):
                    pe.wait_ge(copied, b + (1 + FREE))
                    pe.wait_ge(stored, b + 1)
                    nc.tensor.matmul(out[k][:, 0:W], ht1[k][:, :], W1[:, 0:W], start=True, stop=False)
                    nc.tensor.matmul(out[k][:, 0:W], ht2[k][:, :], W2[:, 0:W], start=False, stop=True).then_inc(projected, 1)

                turn_block(0, 0)
                with pe.Fori(0, NB // 2) as i:
                    for k in range(2):
                        turn_block(2 * i + (k + 1), 1 - k)
                        project(2 * i + k, k)
                project(NB - 1, 0)

            @block.scalar
            def _(act):
                def copy(b, k):
                    act.wait_ge(turned, b + (1 + FREE))
                    act.wait_ge(projected, b + 1)
                    nc.scalar.copy(ht1[k][:, :], turn[k][:, 0:P])
                    nc.scalar.copy(ht2[k][:, :], turn[k][0:D - P, P:2 * P]).then_inc(copied, 1)

                blocks(act, copy)


def stage_layer0(nc, A, K):
    SIN, COS = float(np.sin(np.pi / 8)), float(np.cos(np.pi / 8))
    RN, NEF = A["L0_gnn_W_fc1"].shape[1], A["L0_gnn_W_fc1"].shape[0]
    WN = 2 * CS + 2 * CV
    MS = CS + CV
    MW = 4 * MS
    AHEAD = 4
    QUADS = -(-QUADS_D // AHEAD) * AHEAD
    with ExitStack() as ctx:
        sb = lambda n, s, d=F32: ctx.enter_context(nc.sbuf_tensor("l0_" + n, s, d))
        sem = ctx.enter_context(Semaphores(nc))
        fc1, fc2 = sb("fc1", [PW, PAIR, RN]), sb("fc2", [RN, WN])
        l2_0, l2_1 = sb("l2_0", [MS, CS]), sb("l2_1", [MS, CV])
        bins = sb("bins", [1, 10 * P], I32)
        with ExitStack() as inner:
            sbi = lambda n, s, d=F32: inner.enter_context(nc.sbuf_tensor("l0_" + n, s, d))
            H = sbi("h0", [P, NB, D])
            stage_norm(nc, K, H, "l0n")
            W1, W2 = sbi("proj_w1", [P, 2 * D]), sbi("proj_w2", [CV, 2 * D])
            own, table = sbi("own", [P, NB, D]), sbi("table", [P, NB, D])
            w_in, w_clear, w_steps = sem("w_in"), sem("w_clear"), sem("w_steps")
            with nc.Block() as block:
                @block.sync
                def _(sp):
                    sp.wait_ge(w_clear, 1)
                    loads = 0

                    def load(to, name, rows=slice(None)):
                        sp.dma_start(to, A[name][rows, :]).then_inc(w_in, 16)

                    for half, (ws, wv) in enumerate((("L0_gnn_W_sc0", "L0_gnn_W_sc1"), ("L0_gnn_W_l1_0", "L0_gnn_W_l1_1"))):
                        c = half * D
                        load(W1[0:CS, c:c + CS], ws)
                        load(W1[CS:CS + CV, c + CS:c + CS + CV], wv)
                        load(W1[CS + CV:P, c + CS + CV:c + P], wv)
                        load(W2[:, c + P:c + D], wv)
                    for s in range(PAIR):
                        at = s * WORDS_D + D_E12
                        load(fc1[at:at + NEF, s, :], "L0_gnn_W_fc1")
                    load(fc2[:, :], "L0_gnn_W_fc2")
                    load(l2_0[:, :], "L0_gnn_W_l2_0")
                    load(l2_1[:, :], "L0_gnn_W_l2_1")
                    sp.dma_start(bins[0:1, :], K["bins_d"].rearrange("(o n) -> o n", o=1)).then_inc(w_in, 16)

                @block.vector
                def _(dve):
                    v = Steps(dve, w_steps)
                    nc.vector.memset(W1[:, :], 0.0)
                    nc.vector.memset(W2[:, :], 0.0)
                    nc.vector.memset(fc1[:, :, :], 0.0).then_inc(w_clear, 1)
                    dve.wait_ge(w_in, 16 * 14)
                    s, vv = 1.0 / CS ** 0.5, 1.0 / CV ** 0.5
                    scaled = lambda ap, f: v.done(nc.vector.tensor_scalar(ap, ap, float(f), None, ALU.mult))
                    for half, f in enumerate((SIN, 1.0)):
                        c = half * D
                        scaled(W1[0:CS, c:c + D], s * f)
                        scaled(W1[CS:P, c:c + D], vv * f)
                        scaled(W2[:, c:c + D], vv * f)
                    scaled(fc2[:, :], RN ** -0.5)
                    o = COS * 8.0 ** -0.5 * MS ** -0.5
                    scaled(l2_0[0:CS, :], o)
                    scaled(l2_0[CS:MS, :], o * 3.0 ** -0.5)
                    scaled(l2_1[:, :], o)
                    v.after()
            stage_project(nc, K, H, W1, W2, K["z"], own, table, "l0p")
            tab_out, own_added = sem("tab_out"), sem("own_added")
            with nc.Block() as block:
                @block.sync
                def _(sp):
                    sp.dma_start(K["table0"].rearrange("(b p) f -> p b f", p=P), table[:, :, :]).then_inc(tab_out, 16)
                    sp.wait_ge(tab_out, 16)

                @block.vector
                def _(dve):
                    nc.vector.tensor_tensor(K["X"][:, :, :], K["X"][:, :, :], own[:, :, :], ALU.add).then_inc(own_added, 1)
                    dve.wait_ge(own_added, 1)

        acc = sb("message_sums", [P, NB, MW])
        pay = [sb(f"edge_rows{k}", [P, QUAD, WORDS_D]) for k in range(AHEAD)]
        xg = [sb(f"source_rows{k}", [P, QUAD, D]) for k in range(AHEAD)]
        pay_t, hid = sb("edge_rows_turned", [PW, QUAD // PAIR, P]), sb("hidden", [RN, QUAD * P])
        u01 = sb("w_times_scalars", [P, QUAD, 2, CS])
        u23 = sb("w_times_vectors", [P, QUAD, 3, 2, CV])
        dots = sb("dot_parts", [P, QUAD, 3, CV])
        msg = [sb(f"messages{k}", [P, QUAD, MW]) for k in range(2)]
        hot = [sb(f"node_onehot{k}", [P, QUAD, P]) for k in range(2)]
        with ExitStack() as inner:
            ps = lambda n, s: inner.enter_context(nc.psum_tensor("l0_" + n, s, F32))
            semi = inner.enter_context(Semaphores(nc))
            p_turn, p_hid, p_w, p_sum = ps("p_turn", [P, 512]), ps("p_hid", [P, 512]), [ps(f"p_w{k}", [P, QUAD, 256]) for k in range(2)], ps("p_sum", [P, 2, 512])
            pay_in = [semi(f"pay_in{k}") for k in range(AHEAD)]
            xg_in = [semi(f"xg_in{k}") for k in range(AHEAD)]
            turned, turn_copied, hid_done, silu_done, w_done, msgs, summed, added, chain, pool_seen, pe_seen = (
                semi(n) for n in ("turned", "turn_copied", "hid_done", "silu_done", "w_done", "msgs", "summed", "added", "msg_steps", "pool_seen", "pe_seen"))
            ITERS = QUADS // AHEAD
            assert (QUADS + AHEAD) * QUAD * P <= ROWS_D
            with nc.Block() as block:
                @block.sync
                def _(sp):
                    with sp.Fori(0, ITERS + 1) as it:
                        for k in range(AHEAD):
                            sp.wait_ge(msgs, AHEAD * it + (k + 1))
                            at = (AHEAD * it + k) * (QUAD * P)
                            sp.dma_start(pay[k][:, :, :], K["rows_d"][bass.ds(at, QUAD * P), :].rearrange("(s p) w -> p s w", p=P)).then_inc(pay_in[k], 16)

                @block.gpsimd
                def _(pool):
                    with pool.Fori(0, ITERS + 1) as it:
                        for k in range(AHEAD):
                            pool.wait_ge(pay_in[k], 16 * it + 16)
                            pool.sem_inc(pool_seen, 1)
                            for s in range(QUAD):
                                pool.indirect_dma_start(xg[k][:, s, :], None, K["table0"],
                                                        bass.IndirectOffsetOnAxis(ap=pay[k][:, s, D_SRC:D_SRC + 1].bitcast(U32), axis=0)).then_inc(xg_in[k], 16)
                    for k in range(AHEAD):
                        pool.wait_ge(xg_in[k], 16 * QUAD * (ITERS + 1))

                @block.scalar
                def _(act):
                    def quad(q):
                        act.wait_ge(turned, q + 1)
                        nc.scalar.copy(pay_t[:, :, :].rearrange("p h e -> p (h e)"), p_turn[0:PW, 0:QUAD // PAIR * P]).then_inc(turn_copied, 1)
                        act.wait_ge(hid_done, q + 1)
                        nc.scalar.activation(hid[:, :], p_hid[0:RN, :], ACT.Silu, scale=NEF ** -0.5).then_inc(silu_done, 1)

                    with act.Fori(0, QUADS + 2) as q:
                        quad(q)

                @block.tensor
                def _(pe):
                    def turn_rows(q, u, loaded):
                        pe.wait_ge(pay_in[u], loaded)
                        pe.sem_inc(pe_seen, 1)
                        for h in range(QUAD // PAIR):
                            ins = nc.tensor.transpose(p_turn[0:PW, h * P:(h + 1) * P], pay[u][:, PAIR * h:PAIR * (h + 1), :].rearrange("p s w -> p (s w)"), K["ident"][:, :])
                        ins.then_inc(turned, 1)

                    def hidden(q):
                        pe.wait_ge(turn_copied, q + 1)
                        for s in range(QUAD):
                            ins = nc.tensor.matmul(p_hid[0:RN, s * P:(s + 1) * P], fc1[:, s % PAIR, :], pay_t[:, s // PAIR, :], start=True, stop=True)
                        ins.then_inc(hid_done, 1)

                    def weights(q, k):
                        pe.wait_ge(silu_done, q + 1)
                        for s in range(QUAD):
                            ins = nc.tensor.matmul(p_w[k][:, s, 0:WN], hid[:, s * P:(s + 1) * P], fc2[:, :], start=True, stop=True)
                        ins.then_inc(w_done, 1)

                    def sums(q, k):
                        pe.wait_ge(msgs, q + (1 + AHEAD))
                        pe.sem_inc(pe_seen, 1)
                        pe.wait_ge(added, q + 1)
                        for s in range(QUAD):
                            ins = nc.tensor.matmul(p_sum[:, k, 0:MW], hot[k][:, s, :], msg[k][:, s, :], start=s == 0, stop=s == QUAD - 1)
                        ins.then_inc(summed, 1)

                    turn_rows(0, 0, 16)
                    for q in range(2):
                        hidden(q)
                        turn_rows(q + 1, q + 1, 16)
                        weights(q, q)
                    with pe.Fori(0, ITERS) as it:
                        for u in range(AHEAD):
                            q, ahead = AHEAD * it + u, u + 3
                            hidden(q + 2)
                            turn_rows(q + 3, ahead % AHEAD, 16 * it + 16 * (ahead // AHEAD + 1))
                            sums(q, u % 2)
                            weights(q + 2, u % 2)

                @block.vector
                def _(dve):
                    v = Steps(dve, chain, per=8)
                    bin_reg = dve.alloc_register("l0_bin")

                    def messages(q, u, loaded):
                        v.begin(q)
                        k = u % 2
                        e0 = xg[u][:, :, 0:CS]
                        y0, y1 = pay[u][:, :, D_E4:D_E4 + 1], pay[u][:, :, D_E4 + 1:D_E4 + 4]
                        dve.wait_ge(xg_in[u], loaded)
                        v.done(nc.vector.tensor_tensor(hot[k][:, :, :], free(K["iota_f"][:, 1:2], [0, QUAD], [1, P]),
                                                       free(pay[u][:, 0, D_LOC:D_LOC + 1], [WORDS_D, QUAD], [0, P]), ALU.is_equal))
                        dve.wait_ge(w_done, q + 1)
                        v.done(nc.vector.tensor_tensor(u01[:, :, :, :], p_w[k][:, :, 0:2 * CS].rearrange("p s (a c) -> p s a c", a=2),
                                                       free(e0, [D, QUAD], [0, 2], [1, CS]), ALU.mult))
                        for i in range(3):
                            e1 = xg[u][:, 0, CS + CV * i:CS + CV * i + CV]
                            ins = nc.vector.tensor_tensor(u23[:, :, i, :, :], p_w[k][:, :, 2 * CS:WN].rearrange("p s (a c) -> p s a c", a=2),
                                                          free(e1, [D, QUAD], [0, 2], [1, CV]), ALU.mult)
                        u23_done = v.done(ins)
                        v.after(u23_done - 1)
                        m = msg[k]
                        v.done(nc.vector.tensor_tensor(m[:, :, 0:CS], u01[:, :, 0, :], free(y0, [WORDS_D, QUAD], [0, CS]), ALU.mult))
                        v.done(nc.vector.tensor_tensor(free(m[:, 0, MS:MS + CS], [MW, QUAD], [MS, 3], [1, CS]),
                                                       free(u01[:, 0, 1, :], [2 * CS, QUAD], [0, 3], [1, CS]),
                                                       free(y1, [WORDS_D, QUAD], [1, 3], [0, CS]), ALU.mult))
                        v.after(u23_done)
                        v.done(nc.vector.tensor_tensor(dots[:, :, :, :], u23[:, :, :, 1, :], free(y1, [WORDS_D, QUAD], [1, 3], [0, CV]), ALU.mult))
                        d_done = v.k
                        v.done(nc.vector.tensor_tensor(free(m[:, 0, MS + CS:MS + MS], [MW, QUAD], [MS, 3], [1, CV]),
                                                       u23[:, :, :, 0, :], free(y0, [WORDS_D, QUAD], [0, 3], [0, CV]), ALU.mult))
                        v.after(d_done)
                        v.done(nc.vector.tensor_tensor(dots[:, :, 0, :], dots[:, :, 0, :], dots[:, :, 1, :], ALU.add))
                        v.after()
                        nc.vector.tensor_tensor(m[:, :, CS:MS], dots[:, :, 0, :], dots[:, :, 2, :], ALU.add).then_inc(msgs, 1)
                        v.end()

                    def add(q, k):
                        dve.reg_load([bin_reg], bins[0:1, bass.ds(q * QUAD, 1)])
                        b = dve.snap(bin_reg, min_val=0, max_val=NB - 1)
                        dve.wait_ge(summed, q + 1)
                        dve.wait_ge(added, q + 2)
                        to = acc[:, bass.ds(b, 1), :].rearrange("p o f -> p (o f)")
                        nc.vector.tensor_tensor(to, to, p_sum[:, k, 0:MW], ALU.add).then_inc(added, 1)

                    nc.vector.memset(acc[:, :, :], 0.0).then_inc(added, 2)
                    dve.sem_inc(msgs, AHEAD)
                    messages(0, 0, 16 * QUAD)
                    with dve.Fori(0, ITERS) as it:
                        for u in range(AHEAD):
                            q, n = AHEAD * it + u, u + 1
                            messages(q + 1, n % AHEAD, 16 * QUAD * it + 16 * QUAD * (n // AHEAD + 1))
                            add(q, u % 2)

        with ExitStack() as inner:
            sbi = lambda n, s, d=F32: inner.enter_context(nc.sbuf_tensor("l0_" + n, s, d))
            ps = lambda n, s: inner.enter_context(nc.psum_tensor("l0_" + n, s, F32))
            semi = inner.enter_context(Semaphores(nc))
            ab = [sbi(f"sums_block{k}", [P, MW]) for k in range(2)]
            at_ = [sbi(f"sums_turned{k}", [MS, 4 * P]) for k in range(2)]
            p_t, p_o = [ps(f"p_t{k}", [P, 512]) for k in range(2)], [ps(f"p_o{k}", [P, 512]) for k in range(2)]
            taken, turned, copied, mapped, x_done, pool_seen = (semi(n) for n in ("taken", "turned", "copied", "mapped", "x_done", "pool_seen"))
            FREE = 2

            def blocks(eng, step):
                with eng.Fori(0, NB // 2) as i:
                    for k in range(2):
                        step(2 * i + k, k)
                step(NB - 1, 0)

            with nc.Block() as block:
                @block.gpsimd
                def _(pool):
                    pool.sem_inc(copied, FREE)

                    def take(b, k):
                        pool.wait_ge(turned, b + 1)
                        pool.sem_inc(pool_seen, 1)
                        nc.gpsimd.tensor_copy(ab[k][:, :], acc[:, bass.ds(b, 1), :].rearrange("p o f -> p (o f)")).then_inc(taken, 1)

                    blocks(pool, take)

                @block.vector
                def _(dve):
                    dve.sem_inc(x_done, FREE)

                    def update(b, k):
                        dve.wait_ge(mapped, b + (1 + FREE))
                        xb = K["X"][:, bass.ds(b, 1), :].rearrange("p o f -> p (o f)")
                        nc.vector.scalar_tensor_tensor(xb, p_o[k][:, 0:D], K["z"][:, bass.ds(b, 1)], xb, ALU.mult, ALU.add).then_inc(x_done, 1)

                    blocks(dve, update)

                @block.tensor
                def _(pe):
                    pe.sem_inc(turned, FREE)
                    pe.sem_inc(mapped, FREE)

                    def turn_block(b, k):
                        pe.wait_ge(taken, b + 1)
                        pe.wait_ge(copied, b + 1)
                        for j in range(4):
                            ins = nc.tensor.transpose(p_t[k][0:MS, j * P:(j + 1) * P], ab[k][:, j * MS:(j + 1) * MS], K["ident"][:, :])
                        ins.then_inc(turned, 1)

                    def map_block(b, k):
                        pe.wait_ge(copied, b + (1 + FREE))
                        pe.wait_ge(x_done, b + 1)
                        nc.tensor.matmul(p_o[k][:, 0:CS], at_[k][:, 0:P], l2_0[:, :], start=True, stop=True)
                        for i in range(3):
                            ins = nc.tensor.matmul(p_o[k][:, CS + CV * i:CS + CV * (i + 1)], at_[k][:, (i + 1) * P:(i + 2) * P], l2_1[:, :], start=True, stop=True)
                        ins.then_inc(mapped, 1)

                    turn_block(0, 0)
                    with pe.Fori(0, NB // 2) as i:
                        for k in range(2):
                            turn_block(2 * i + (k + 1), 1 - k)
                            map_block(2 * i + k, k)
                    map_block(NB - 1, 0)

                @block.scalar
                def _(act):
                    def copy(b, k):
                        act.wait_ge(turned, b + (1 + FREE))
                        act.wait_ge(mapped, b + 1)
                        nc.scalar.copy(at_[k][:, :], p_t[k][0:MS, :]).then_inc(copied, 1)

                    blocks(act, copy)


def stage_finish(nc, A, K, out):
    with ExitStack() as ctx:
        raw = ctx.enter_context(nc.sbuf_tensor("x_out", [P, NB, D], F32))
        sem = ctx.enter_context(Semaphores(nc))
        ready, written = sem("x_ready"), sem("x_written")
        last = N - (NB - 1) * P
        with nc.Block() as block:
            @block.vector
            def _(dve):
                nc.vector.tensor_copy(raw[:, :, 0:CS], K["X"][:, :, 0:CS])
                for i in range(3):
                    ins = nc.vector.tensor_copy(by_part(raw, i), K["X"][:, :, CS + CV * i:CS + CV * (i + 1)])
                ins.then_inc(ready, 1)

            @block.sync
            def _(sp):
                sp.wait_ge(ready, 1)
                sp.dma_start(out[0:(NB - 1) * P, :].rearrange("(b p) f -> p b f", p=P), raw[:, 0:NB - 1, :]).then_inc(written, 16)
                sp.dma_start(out[(NB - 1) * P:N, :], raw[0:last, NB - 1, :]).then_inc(written, 16)
                sp.wait_ge(written, 32)

NC_W = 400


def stage_turn(nc, K, H, ht1, ht2, table, tag):
    with ExitStack() as ctx:
        sb = lambda n, s, d=F32: ctx.enter_context(nc.sbuf_tensor(tag + "_" + n, s, d))
        sem = ctx.enter_context(Semaphores(nc))
        hb = sb("h_block", [P, D])
        one = sb("h_with_one", [P, NB, D + 1])
        turn = ctx.enter_context(nc.psum_tensor(tag + "_" + "turn", [P, 512], F32))
        taken, turned, copied, with_one, written = (sem(n) for n in ("taken", "turned", "copied", "with_one", "written"))
        with nc.Block() as block:
            @block.vector
            def _(dve):
                nc.vector.tensor_copy(one[:, :, 0:D], H[:, :, :])
                nc.vector.memset(one[:, :, D:D + 1], 1.0).then_inc(with_one, 1)
                with dve.Fori(0, NB) as b:
                    dve.wait_ge(turned, b + 1)
                    nc.vector.tensor_copy(hb[:, :], H[:, bass.ds(b, 1), :].rearrange("p o f -> p (o f)")).then_inc(taken, 1)

            @block.sync
            def _(sp):
                sp.wait_ge(with_one, 1)
                sp.dma_start(table.rearrange("(b p) f -> p b f", p=P), one[:, :, :]).then_inc(written, 16)
                sp.wait_ge(written, 16)

            @block.tensor
            def _(pe):
                pe.sem_inc(turned, 1)
                with pe.Fori(0, NB) as b:
                    pe.wait_ge(taken, b + 1)
                    pe.wait_ge(copied, b + 1)
                    nc.tensor.transpose(turn[:, 0:P], hb[:, 0:P], K["ident"][:, :])
                    nc.tensor.transpose(turn[0:D - P, P:2 * P], hb[:, P:D], K["ident"][:, :]).then_inc(turned, 1)

            @block.scalar
            def _(act):
                act.sem_inc(copied, 1)
                with act.Fori(0, NB) as b:
                    act.wait_ge(turned, b + 2)
                    nc.scalar.copy(ht1[:, bass.ds(b * P, P)], turn[:, 0:P])
                    nc.scalar.copy(ht2[:, bass.ds(b * P, P)], turn[0:D - P, P:2 * P]).then_inc(copied, 1)


def stage_back(nc, K, H, parts, tag):
    with ExitStack() as ctx:
        sb = lambda n, s, d=F32: ctx.enter_context(nc.sbuf_tensor(tag + "_" + n, s, d))
        sem = ctx.enter_context(Semaphores(nc))
        ub = [sb(f"u_block{j}", [rows, P]) for j, (_, rows, _) in enumerate(parts)]
        turn = ctx.enter_context(nc.psum_tensor(tag + "_" + "turn", [P, 512], F32))
        taken, turned, x_done, pe_seen = (sem(n) for n in ("taken", "turned", "x_done", "pe_seen"))
        with nc.Block() as block:
            @block.scalar
            def _(act):
                with act.Fori(0, NB) as b:
                    act.wait_ge(turned, b + 1)
                    for j, (tile, rows, _) in enumerate(parts):
                        ins = nc.scalar.copy(ub[j][:, :], tile[0:rows, bass.ds(b * P, P)])
                    ins.then_inc(taken, 1)

            @block.tensor
            def _(pe):
                pe.sem_inc(turned, 1)
                with pe.Fori(0, NB) as b:
                    pe.wait_ge(taken, b + 1)
                    pe.wait_ge(x_done, b + 1)
                    pe.sem_inc(pe_seen, 1)
                    for j, (_, rows, col) in enumerate(parts):
                        ins = nc.tensor.transpose(turn[:, col:col + rows], ub[j][:, :], K["ident"][0:rows, 0:rows])
                    ins.then_inc(turned, 1)

            @block.vector
            def _(dve):
                nc.vector.tensor_tensor(K["X"][:, :, :], K["X"][:, :, :], H[:, :, :], ALU.add).then_inc(x_done, 1)
                with dve.Fori(0, NB) as b:
                    dve.wait_ge(turned, b + 2)
                    dve.wait_ge(x_done, b + 1)
                    xb = K["X"][:, bass.ds(b, 1), :].rearrange("p o f -> p (o f)")
                    nc.vector.tensor_tensor(xb, turn[:, 0:D], xb, ALU.add).then_inc(x_done, 1)


def stage_node_sums(nc, K, table, bins, acc1, acc2, edge_col, channels, products, counts, tag):
    CH = channels + 1
    ITERS = SLOTS_S // BATCH_S
    QB = BATCH_S // QUAD
    X2 = D + 1 - P
    X2_OUT = X2 if counts else CV
    with ExitStack() as ctx:
        sb = lambda n, s, d=F32: ctx.enter_context(nc.sbuf_tensor(tag + "_" + n, s, d))
        ps = lambda n, s: ctx.enter_context(nc.psum_tensor(tag + "_" + n, s, F32))
        sem = ctx.enter_context(Semaphores(nc))
        pay = [sb(f"edge_rows{q}", [P, QUAD, WORDS_S]) for q in range(QB)]
        xg = [sb(f"node_rows{q}", [P, QUAD, D + 1]) for q in range(QB)]
        eh = [sb(f"edge_by_node{q}", [P, QUAD, CH, G]) for q in range(QB)]
        z1, z2 = sb("outer1", [P, CH, BATCH_S, G]), sb("outer2", [X2, CH, BATCH_S, G])
        p1, p2 = ps("p_outer1", [P, 2, 512]), ps("p_outer2", [P, 2, 512])
        c1, c2 = ps("p_sums1", [P, 512]), ps("p_sums2", [P, 512])
        pay_in = [sem(f"pay_in{q}") for q in range(QB)]
        xg_in = [sem(f"xg_in{q}") for q in range(QB)]
        built, outer, evacuated, contracted, added, pool_seen, hot_done, pe_seen, sp_seen = (
            sem(n) for n in ("built", "outer", "evacuated", "contracted", "added", "pool_seen", "hot_done", "pe_seen", "sp_seen"))
        with nc.Block() as block:
            @block.sync
            def _(sp):
                with sp.Fori(0, ITERS + 1) as it:
                    for q in range(QB):
                        sp.wait_ge(built, it * QB + (q + 1))
                        sp.sem_inc(sp_seen, 1)
                        sp.wait_ge(outer, it * BATCH_S + QUAD * (q + 1))
                        sp.sem_inc(sp_seen, 1)
                        at = (it * QB + q) * (QUAD * P)
                        sp.dma_start(pay[q][:, :, :], K["rows_s"][bass.ds(at, QUAD * P), :].rearrange("(s p) w -> p s w", p=P)).then_inc(pay_in[q], 16)

            @block.gpsimd
            def _(pool):
                with pool.Fori(0, ITERS + 1) as it:
                    for q in range(QB):
                        pool.wait_ge(pay_in[q], it * 16 + 16)
                        pool.sem_inc(pool_seen, 1)
                        pool.wait_ge(outer, it * BATCH_S + QUAD * (q + 1))
                        pool.sem_inc(pool_seen, 1)
                        for s in range(QUAD):
                            pool.indirect_dma_start(xg[q][:, s, :], None, table,
                                                    bass.IndirectOffsetOnAxis(ap=pay[q][:, s, S_DST:S_DST + 1].bitcast(U32), axis=0)).then_inc(xg_in[q], 16)
                for q in range(QB):
                    pool.wait_ge(xg_in[q], 16 * QUAD * (ITERS + 1))

            @block.vector
            def _(dve):
                regs = [dve.alloc_register(f"s_bin{channels}_{s}") for s in range(BATCH_S)]

                def build(it, q):
                    dve.wait_ge(pay_in[q], it * 16 + 16)
                    dve.wait_ge(outer, it * BATCH_S + QUAD * (q + 1))
                    hot = eh[q][:, :, channels, :]
                    nc.vector.tensor_tensor(hot, free(K["iota_f"][:, 1:2], [0, QUAD], [1, G]),
                                            free(pay[q][:, 0, S_LOC:S_LOC + 1], [WORDS_S, QUAD], [0, G]), ALU.is_equal).then_inc(hot_done, 1)
                    dve.wait_ge(hot_done, it * QB + (q + 1))
                    nc.vector.tensor_tensor(eh[q][:, :, 0:channels, :],
                                            free(pay[q][:, 0, edge_col:edge_col + 1], [WORDS_S, QUAD], [1, channels], [0, G]),
                                            free(hot, [CH * G, QUAD], [0, channels], [1, G]), ALU.mult).then_inc(built, 1)

                nc.vector.memset(acc1[:, :], 0.0)
                nc.vector.memset(acc2[:, :], 0.0).then_inc(added, 1)
                dve.sem_inc(built, QB)
                for q in range(QB):
                    build(0, q)
                with dve.Fori(0, ITERS) as it:
                    for q in range(QB):
                        build(it + 1, q)
                    dve.wait_ge(contracted, it + 1)
                    for half in range(2):
                        dve.reg_load(regs[half * 8:half * 8 + 8], bins[0:1, bass.ds(it * BATCH_S + half * 8, 8)])
                    for s in range(BATCH_S):
                        at = dve.snap(regs[s], min_val=0, max_val=(BINS_S - 1) * G)
                        dve.wait_ge(added, it * BATCH_S + (s + 1))
                        o1, o2 = acc1[:, bass.ds(at, G)], acc2[0:X2_OUT, bass.ds(at, G)]
                        nc.vector.tensor_tensor(o1, o1, c1[:, s * G:(s + 1) * G], ALU.add)
                        nc.vector.tensor_tensor(o2, o2, c2[0:X2_OUT, s * G:(s + 1) * G], ALU.add).then_inc(added, 1)

            @block.tensor
            def _(pe):
                pe.sem_inc(outer, BATCH_S)
                with pe.Fori(0, ITERS) as it:
                    for q in range(QB):
                        pe.wait_ge(built, it * QB + (QB + q + 1))
                        pe.sem_inc(pe_seen, 1)
                        pe.wait_ge(xg_in[q], it * (16 * QUAD) + 16 * QUAD)
                        pe.sem_inc(pe_seen, 1)
                        for s in range(QUAD):
                            j = q * QUAD + s
                            pe.wait_ge(evacuated, it * BATCH_S + (j + 1))
                            e = eh[q][:, s, :, :].rearrange("p c n -> p (c n)")
                            nc.tensor.matmul(p1[:, j % 2, 0:CH * G], xg[q][:, s, 0:P], e, start=True, stop=True)
                            nc.tensor.matmul(p2[0:X2, j % 2, 0:CH * G], xg[q][:, s, P:D + 1], e, start=True, stop=True).then_inc(outer, 1)
                    pe.wait_ge(evacuated, it * BATCH_S + (BATCH_S + 2))
                    pe.sem_inc(pe_seen, 1)
                    pe.wait_ge(added, it * BATCH_S + 1)
                    pe.sem_inc(pe_seen, 1)
                    first, last = {}, {}
                    for n, (to, rows, *_) in enumerate(products):
                        first.setdefault(to, n)
                        last[to] = n
                    for n, (to, rows, lhs, of, krows, ch) in enumerate(products):
                        z = (z1, z2)[of][0:krows, ch, :, :].rearrange("p s n -> p (s n)")
                        ins = nc.tensor.matmul((c1, c2)[to][0:rows, 0:BATCH_S * G], lhs, z, start=n == first[to], stop=n == last[to], skip_group_check=True)
                    ins.then_inc(contracted, 1)

            @block.scalar
            def _(act):
                act.sem_inc(evacuated, 2)
                with act.Fori(0, ITERS) as it:
                    for j in range(BATCH_S):
                        act.wait_ge(outer, it * BATCH_S + (BATCH_S + j + 1))
                        nc.scalar.copy(z1[:, :, j, :], p1[:, j % 2, 0:CH * G].rearrange("p (c n) -> p c n", n=G))
                        nc.scalar.copy(z2[:, :, j, :], p2[0:X2, j % 2, 0:CH * G].rearrange("p (c n) -> p c n", n=G)).then_inc(evacuated, 1)


def stage_layer1(nc, A, K):
    NS = 8
    R2, RT = 2.0 ** -0.5, 3.0 ** -0.5
    with ExitStack() as ctx:
        sb = lambda n, s, d=F32: ctx.enter_context(nc.sbuf_tensor("l1_" + n, s, d))
        sem = ctx.enter_context(Semaphores(nc))
        H = sb("h1", [P, NB, D])
        ht1, ht2 = sb("h_by_feature1", [P, NP]), sb("h_by_feature2", [CV, NP])
        stage_norm(nc, K, H, "l1n")
        stage_turn(nc, K, H, ht1, ht2, K["table1"], "l1t")
        acc1, acc2 = sb("sums1", [P, NP]), sb("sums2", [CV + 1, NP])
        wm1, wm2 = sb("wm1", [P, D]), sb("wm2", [CV + 1, D])
        raw = [sb("wu_h1", [P, D]), sb("wu_h2", [CV, D]), sb("wu_a1", [P, D]), sb("wu_a2", [CV, D])]
        wu = [sb("wu_h1p", [P, D]), sb("wu_h2p", [CV, D]), sb("wu_a1p", [P, D]), sb("wu_a2p", [CV, D])]
        bu1, bu2 = sb("bu1", [P, 1]), sb("bu2", [CV, 1])
        with ExitStack() as inner:
            sbi = lambda n, s, d=F32: inner.enter_context(nc.sbuf_tensor("l1_" + n, s, d))
            ws, ws2 = sbi("w_scalar", [P, NS, P]), sbi("w_scalar2", [CV, NS, CV])
            wv = [sbi(f"w_vector{i}", [P, NS, P]) for i in range(2)]
            wv2 = sbi("w_vector2", [CV, NS, CS])
            one = sbi("keep_count", [CV + 1, CV + 1])
            bins = sbi("bins", [1, 10 * P], I32)
            w_in, w_clear, w_steps = sem("w_in"), sem("w_clear"), sem("w_steps")
            S0, V0, V1 = slice(0, CS), slice(CS, CS + CV), slice(CS + CV, P)
            with nc.Block() as block:
                @block.sync
                def _(sp):
                    sp.wait_ge(w_clear, 1)

                    def load(to, of, **kw):
                        sp.dma_start(to, of, **kw).then_inc(w_in, 16)

                    W1, W2, W3, W4 = (A[f"L1_gnn_W{n}"] for n in (1, 2, 3, 4))
                    load(ws[S0, :, S0], W1)
                    load(ws[V0, :, V0], W4)
                    load(ws[V1, :, V1], W4)
                    load(ws2[:, :, :], W4)
                    for i, V in enumerate((V0, V1)):
                        load(wv[i][S0, :, V], W3)
                        load(wv[i][V, :, S0], W2)
                    load(wv2[:, :, :], W2)
                    load(bins[0:1, :], K["bins_s"].rearrange("(o n) -> o n", o=1))
                    Wm, Wu, bm, bu = A["L1_gnn_Wm"], A["L1_gnn_Wu"], A["L1_gnn_bm"], A["L1_gnn_bu"]
                    for w, t1, t2 in ((Wm, wm1, wm2), (Wu, raw[0], raw[1])):
                        load(t1[S0, :], w[0:CS, :])
                        for i, to in enumerate((t1[V0, :], t1[V1, :], t2[0:CV, :])):
                            load(to, w[CS + i:D:3, :])
                    load(wm2[CV:CV + 1, :], bm.rearrange("(o f) -> o f", o=1))
                    load(raw[2][:, :], Wu[D:D + P, :])
                    load(raw[3][:, :], Wu[D + P:2 * D, :])
                    bcol = bu.rearrange("(f o) -> f o", o=1)
                    load(bu1[S0, :], bcol[0:CS, :], allow_slow_non_contiguous=True)
                    for i, to in enumerate((bu1[V0, :], bu1[V1, :], bu2[:, :])):
                        load(to, bcol[CS + i:D:3, :], allow_slow_non_contiguous=True)

                @block.vector
                def _(dve):
                    v = Steps(dve, w_steps)
                    nc.vector.memset(ws[:, :, :], 0.0)
                    nc.vector.memset(one[:, :], 0.0)
                    for i in range(2):
                        ins = nc.vector.memset(wv[i][:, :, :], 0.0)
                    ins.then_inc(w_clear, 1)
                    dve.wait_ge(w_clear, 1)
                    v.done(nc.vector.memset(one[CV:CV + 1, CV:CV + 1], 1.0))
                    dve.wait_ge(w_in, 16 * 25)
                    scaled = lambda ap, f: v.done(nc.vector.tensor_scalar(ap, ap, float(f), None, ALU.mult))
                    f1, f2, f4 = R2 * (CS * NS) ** -0.5, R2 * RT * (CV * NS) ** -0.5, R2 * (CV * NS) ** -0.5
                    scaled(ws[S0, :, :], f1)
                    scaled(ws[CS:P, :, :], f4)
                    scaled(ws2[:, :, :], f4)
                    for i in range(2):
                        scaled(wv[i][S0, :, :], f1)
                        scaled(wv[i][CS:P, :, :], f2)
                    scaled(wv2[:, :, :], f2)
                    for a, b in zip(raw, wu):
                        v.done(nc.vector.tensor_copy(b[:, 0:CS], a[:, 0:CS]))
                        for i in range(3):
                            v.done(nc.vector.tensor_copy(b[:, CS + CV * i:CS + CV * (i + 1)], a[:, CS + i:D:3]))
                    v.after()
            products = [(1, CV + 1, one[:, :], 1, CV + 1, 4 * NS)]
            for b in range(NS):
                products += [(0, P, ws[:, b, :], 0, P, b), (1, CV, ws2[:, b, :], 1, CV, b)]
                for i in range(2):
                    products.append((0, P, wv[i][:, b, :], 0, P, NS + 3 * b + i))
                products += [(1, CV, wv[0][S0, b, V0], 0, CS, NS + 3 * b + 2), (0, CS, wv2[:, b, :], 1, CV, NS + 3 * b + 2)]
            stage_node_sums(nc, K, K["table1"], bins, acc1, acc2, S_E32, 4 * NS, products, True, "l1s")

        ut1, ut2 = sb("update1", [P, NP]), sb("update2", [CV, NP])
        with ExitStack() as inner:
            sbi = lambda n, s, d=F32: inner.enter_context(nc.sbuf_tensor("l1_" + n, s, d))
            ps = lambda n: inner.enter_context(nc.psum_tensor("l1_" + n, [P, 512], F32))
            semi = inner.enter_context(Semaphores(nc))
            ag1, ag2 = sbi("agg1", [P, NC_W]), sbi("agg2", [CV, NC_W])
            whole = (ht1, ht2, acc1, acc2)
            part = [sbi(f"nodes{j}", [t.shape[0], NC_W]) for j, t in enumerate(whole)]
            h1, h2, s1, s2 = part
            pa1, pa2, pu1, pu2 = ps("p_agg1"), ps("p_agg2"), ps("p_upd1"), ps("p_upd2")
            taken, agg, agg_copied, upd, upd_copied = (semi(n) for n in ("taken", "agg", "agg_copied", "upd", "upd_copied"))
            with nc.Block() as block:
                @block.vector
                def _(dve):
                    with dve.Fori(0, NP // NC_W) as c:
                        dve.wait_ge(upd, c + 1)
                        for t, of in zip(part, whole):
                            ins = nc.vector.tensor_copy(t[:, :], of[:, bass.ds(c * NC_W, NC_W)])
                        ins.then_inc(taken, 1)

                @block.tensor
                def _(pe):
                    pe.sem_inc(upd, 1)
                    with pe.Fori(0, NP // NC_W) as c:
                        pe.wait_ge(taken, c + 1)
                        for to, cols, rows in ((pa1, slice(0, P), P), (pa2, slice(P, D), CV)):
                            nc.tensor.matmul(to[0:rows, 0:NC_W], wm1[:, cols], s1[:, :], start=True, stop=False)
                            ins = nc.tensor.matmul(to[0:rows, 0:NC_W], wm2[:, cols], s2[:, :], start=False, stop=True)
                        ins.then_inc(agg, 1)
                        pe.wait_ge(agg_copied, c + 1)
                        pe.wait_ge(upd_copied, c + 1)
                        for to, cols, rows in ((pu1, slice(0, P), P), (pu2, slice(P, D), CV)):
                            o = to[0:rows, 0:NC_W]
                            nc.tensor.matmul(o, wu[0][:, cols], h1[:, :], start=True, stop=False)
                            nc.tensor.matmul(o, wu[1][:, cols], h2[:, :], start=False, stop=False)
                            nc.tensor.matmul(o, wu[2][:, cols], ag1[:, :], start=False, stop=False)
                            ins = nc.tensor.matmul(o, wu[3][:, cols], ag2[:, :], start=False, stop=True)
                        ins.then_inc(upd, 1)

                @block.scalar
                def _(act):
                    act.sem_inc(upd_copied, 1)
                    with act.Fori(0, NP // NC_W) as c:
                        n = bass.ds(c * NC_W, NC_W)
                        act.wait_ge(agg, c + 1)
                        nc.scalar.copy(ag1[:, :], pa1[:, 0:NC_W])
                        nc.scalar.copy(ag2[:, :], pa2[0:CV, 0:NC_W]).then_inc(agg_copied, 1)
                        act.wait_ge(upd, c + 2)
                        nc.scalar.activation(ut1[:, n], pu1[:, 0:NC_W], ACT.Identity, bias=bu1[:, 0:1])
                        nc.scalar.activation(ut2[:, n], pu2[0:CV, 0:NC_W], ACT.Identity, bias=bu2[:, 0:1]).then_inc(upd_copied, 1)
        stage_back(nc, K, H, [(ut1, P, 0), (ut2, CV, P)], "l1b")


def stage_layer2(nc, A, K):
    R3, R8, R32 = 3.0 ** -0.5, CS ** -0.5, CV ** -0.5
    with ExitStack() as ctx:
        sb = lambda n, s, d=F32: ctx.enter_context(nc.sbuf_tensor("l2_" + n, s, d))
        sem = ctx.enter_context(Semaphores(nc))
        H = sb("h2", [P, NB, D])
        with ExitStack() as inner:
            sbi = lambda n, s, d=F32: inner.enter_context(nc.sbuf_tensor("l2_" + n, s, d))
            ht1, ht2 = sbi("h_by_feature1", [P, NP]), sbi("h_by_feature2", [CV, NP])
            stage_norm(nc, K, H, "l2n")
            stage_turn(nc, K, H, ht1, ht2, K["table2"], "l2t")
            acc1, acc2 = sbi("sums1", [P, NP]), sbi("sums2", [CV + 1, NP])
            ws, ws2 = sbi("w_scalar", [P, 2, P]), sbi("w_scalar2", [CV, 2, CV])
            wv = [sbi(f"w_vector{i}", [P, P]) for i in range(2)]
            wv2 = sbi("w_vector2", [CV, CS])
            bins = sbi("bins", [1, 10 * P], I32)
            w_in, w_clear, w_steps = sem("w_in"), sem("w_clear"), sem("w_steps")
            S0, V0, V1 = slice(0, CS), slice(CS, CS + CV), slice(CS + CV, P)
            with nc.Block() as block:
                @block.sync
                def _(sp):
                    sp.wait_ge(w_clear, 1)

                    def load(to, of):
                        sp.dma_start(to, of).then_inc(w_in, 16)

                    for k, (s, v) in enumerate((("Wm_ss", "Wm_vs"), ("Lm_s", "Lm_v"))):
                        load(ws[S0, k, S0], A["L2_gnn_" + s])
                        for to in (ws[V0, k, V0], ws[V1, k, V1], ws2[:, k, :]):
                            load(to, A["L2_gnn_" + v])
                    for i, V in enumerate((V0, V1)):
                        load(wv[i][S0, V], A["L2_gnn_Wm_sv"])
                        load(wv[i][V, S0], A["L2_gnn_Wm_vv"])
                    load(wv2[:, :], A["L2_gnn_Wm_vv"])
                    load(bins[0:1, :], K["bins_s"].rearrange("(o n) -> o n", o=1))
                    sp.dma_start(K["h_turned"][0:P, :], ht1[:, :]).then_inc(w_in, 16)
                    sp.dma_start(K["h_turned"][P:D, :], ht2[:, :]).then_inc(w_in, 16)

                @block.vector
                def _(dve):
                    v = Steps(dve, w_steps)
                    nc.vector.memset(ws[:, :, :], 0.0)
                    for i in range(2):
                        ins = nc.vector.memset(wv[i][:, :], 0.0)
                    ins.then_inc(w_clear, 1)
                    dve.wait_ge(w_in, 16 * 16)
                    scaled = lambda ap, f: v.done(nc.vector.tensor_scalar(ap, ap, float(f), None, ALU.mult))
                    scaled(ws[S0, :, :], R8)
                    scaled(ws[CS:P, :, :], R32)
                    scaled(ws2[:, :, :], R32)
                    for i in range(2):
                        scaled(wv[i][S0, :], R8)
                        scaled(wv[i][CS:P, :], R3 * R32)
                    scaled(wv2[:, :], R3 * R32)
                    v.after()
            DIST, ONE = 3, 4
            products = []
            for k, ch in enumerate((DIST, ONE)):
                products += [(0, P, ws[:, k, :], 0, P, ch), (1, CV, ws2[:, k, :], 1, CV, ch)]
            for i in range(2):
                products.append((0, P, wv[i][:, :], 0, P, i))
            products += [(1, CV, wv[0][S0, V0], 0, CS, 2), (0, CS, wv2[:, :], 1, CV, 2)]
            stage_node_sums(nc, K, K["table2"], bins, acc1, acc2, S_E4, 4, products, False, "l2s")
            a_out = sem("a_out")
            with nc.Block() as block:
                @block.sync
                def _(sp):
                    sp.dma_start(K["a_turned"][0:P, :], acc1[:, :]).then_inc(a_out, 16)
                    sp.dma_start(K["a_turned"][P:D, :], acc2[0:CV, :]).then_inc(a_out, 16)
                    sp.wait_ge(a_out, 32)

        us, uv = sb("update_s", [CS, NP]), [sb(f"update_v{i}", [CV, NP]) for i in range(3)]
        with ExitStack() as inner:
            sbi = lambda n, s, d=F32: inner.enter_context(nc.sbuf_tensor("l2_" + n, s, d))
            semi = inner.enter_context(Semaphores(nc))
            KB = 8
            SPAN = P // 4
            w_ss = [sbi(f"w_ss{h}", [P, 16, CS]) for h in range(2)]
            w_vv, w_sv, w_vs = sbi("w_vv", [P, 8, CS]), sbi("w_sv", [P, 16, CV]), sbi("w_vs", [P, 16, CV])
            l_s, l_v = sbi("l_s", [CS, CS]), sbi("l_v", [CV, CV])
            xs4, a04 = sbi("xs_by32", [P, 16, P]), sbi("a0_by32", [P, 16, P])
            xv4 = sbi("xv_by32", [P, 3, 8, P])
            a0, a1, xv = sbi("a0_four_times", [P, 2, P]), sbi("a1_four_times", [P, 3, P]), sbi("xv_four_times", [P, 3, P])
            hs, hv = sbi("h_scalars", [CS, P]), sbi("h_vectors", [CV, 3, P])
            psum = lambda n, rows: inner.enter_context(nc.psum_tensor("l2_" + n, [rows, 512], F32))
            p_s, p_v = psum("p_upd_s", CS), [psum(f"p_upd_v{i}", CV) for i in range(3)]
            w_in, w_steps = semi("w_in2"), semi("w_steps2")
            hT, aT = K["h_turned"], K["a_turned"]
            steps = []
            for i in range(3):
                steps.append(("xv4", xv4[:, i, :, :], ("a1", a1[:, i, :]), [w_vv[:, j, :] for j in range(KB)], p_s))
            for i in range(3):
                for k in range(0, 16, KB):
                    steps.append(("xs4", xs4[:, k:k + KB, :], ("a1", a1[:, i, :]), [w_sv[:, k + j, :] for j in range(KB)], p_v[i]))
            for h in range(2):
                for k in range(0, 16, KB):
                    steps.append(("xs4", xs4[:, k:k + KB, :], ("a0", a0[:, h, :]), [w_ss[h][:, k + j, :] for j in range(KB)], p_s))
            for i in range(3):
                for k in range(0, 16, KB):
                    steps.append(("a04", a04[:, k:k + KB, :], ("xv", xv[:, i, :]), [w_vs[:, k + j, :] for j in range(KB)], p_v[i]))
            STEPS = len(steps)
            BUFS = 13
            prod = [sbi(f"outer{m}", [P, KB, P]) for m in range(BUFS)]
            had = [m - BUFS if m >= BUFS else (m + BUFS if m + BUFS < STEPS else m) - STEPS for m in range(STEPS)]
            names = ("xv4", "a1", "xs4", "a0", "a04", "xv")
            last_use = {g: max(m for m, s in enumerate(steps) if g in (s[0], s[2][0])) + 1 for g in names}
            loads = {"xv4": 12, "a1": 4, "xs4": 4, "a0": 4, "a04": 4, "xv": 4, "lin": 2}
            arrived = {g: semi(f"{g}_in") for g in loads}
            made, used, seen, upd, upd_copied = (semi(n) for n in ("made", "used", "seen", "upd", "upd_copied"))
            with nc.Block() as block:
                @block.scalar
                def _(act):
                    def load(to, of):
                        act.dma_start(to, of).then_inc(w_in, 16)

                    for j in range(4):
                        rows = slice(j * SPAN, (j + 1) * SPAN)
                        for h in range(2):
                            load(w_ss[h][rows, :, :], A["L2_gnn_Wu_ss"][j:CS:4, h * SPAN:(h + 1) * SPAN, :].rearrange("k v w -> v k w"))
                        load(w_vv[rows, :, :], A["L2_gnn_Wu_vv"][j:CV:4, :, :].rearrange("k v w -> v k w"))
                        load(w_sv[rows, :, :], A["L2_gnn_Wu_sv"][j:CS:4, :, :].rearrange("k v w -> v k w"))
                        load(w_vs[rows, :, :], A["L2_gnn_Wu_vs"][:, j:CS:4, :])
                    load(l_s[:, :], A["L2_gnn_Lu_s"])
                    load(l_v[:, :], A["L2_gnn_Lu_v"])
                    act.sem_inc(upd_copied, 1)
                    with act.Fori(0, NB) as t:
                        act.wait_ge(upd, t + 1)
                        n = bass.ds(t * P, P)
                        nc.scalar.copy(us[:, n], p_s[:, 0:P])
                        for i in range(3):
                            ins = nc.scalar.copy(uv[i][:, n], p_v[i][:, 0:P])
                        ins.then_inc(upd_copied, 1)

                @block.sync
                def _(sp):
                    def spread(group, to, of, first, rows, n):
                        for j in range(4):
                            v = of[first + j:first + rows:4, n]
                            v = bass.AP(v.tensor, v.offset, [[0, SPAN]] + [list(d) for d in v.ap])
                            sp.dma_start(to[j * SPAN:(j + 1) * SPAN, :, :], v).then_inc(arrived[group], 16)

                    def free_to_load(group, t):
                        sp.wait_ge(made, t * STEPS + last_use[group])
                        sp.sem_inc(seen, 1)

                    with sp.Fori(0, NB) as t:
                        n = bass.ds(t * P, P)
                        vectors = lambda of: of[CS:D, n].rearrange("(i c) n -> c i n", i=3)
                        sp.wait_ge(used, t * STEPS + 1)
                        sp.sem_inc(seen, 1)
                        sp.dma_start(hs[:, :], hT[0:CS, n]).then_inc(arrived["lin"], 16)
                        sp.dma_start(hv[:, :, :], vectors(hT)).then_inc(arrived["lin"], 16)
                        free_to_load("xv4", t)
                        for i in range(3):
                            spread("xv4", xv4[:, i, :, :], hT, CS + CV * i, CV, n)
                        free_to_load("a1", t)
                        for j in range(4):
                            sp.dma_start(a1[j * SPAN:(j + 1) * SPAN, :, :], vectors(aT)).then_inc(arrived["a1"], 16)
                        free_to_load("xs4", t)
                        spread("xs4", xs4, hT, 0, CS, n)
                        free_to_load("a0", t)
                        for j in range(4):
                            sp.dma_start(a0[j * SPAN:(j + 1) * SPAN, :, :], aT[0:CS, n].rearrange("(h v) n -> v h n", h=2)).then_inc(arrived["a0"], 16)
                        free_to_load("a04", t)
                        spread("a04", a04, aT, 0, CS, n)
                        free_to_load("xv", t)
                        for j in range(4):
                            sp.dma_start(xv[j * SPAN:(j + 1) * SPAN, :, :], vectors(hT)).then_inc(arrived["xv"], 16)

                @block.vector
                def _(dve):
                    v = Steps(dve, w_steps)
                    dve.wait_ge(w_in, 16 * 22)
                    scaled = lambda ap, f: v.done(nc.vector.tensor_scalar(ap, ap, float(f), None, ALU.mult))
                    for h in range(2):
                        scaled(w_ss[h][:, :, :], 1.0 / CS)
                    scaled(w_vv[:, :, :], R3 / CV)
                    scaled(w_sv[:, :, :], (CS * CV) ** -0.5)
                    scaled(w_vs[:, :, :], (CS * CV) ** -0.5)
                    scaled(l_s[:, :], R8)
                    scaled(l_v[:, :], R32)
                    v.after()
                    dve.sem_inc(made, STEPS)
                    with dve.Fori(0, NB) as t:
                        waited = set()
                        for m, (g, x, (g2, a), _, _) in enumerate(steps):
                            for name in (g, g2):
                                if name not in waited:
                                    dve.wait_ge(arrived[name], t * (16 * loads[name]) + 16 * loads[name])
                                    waited.add(name)
                            dve.wait_ge(used, t * STEPS + (STEPS + had[m] + 1))
                            nc.vector.tensor_tensor(prod[m % BUFS][:, :, :], x, free(a, [0, KB], [1, P]), ALU.mult).then_inc(made, 1)

                @block.tensor
                def _(pe):
                    pe.sem_inc(used, STEPS)
                    with pe.Fori(0, NB) as t:
                        pe.wait_ge(upd_copied, t + 1)
                        pe.sem_inc(seen, 1)
                        pe.wait_ge(made, t * STEPS + (STEPS + 1))
                        pe.sem_inc(seen, 1)
                        pe.wait_ge(arrived["lin"], t * 32 + 32)
                        pe.sem_inc(seen, 1)
                        nc.tensor.matmul(p_s[:, 0:P], l_s[:, :], hs[:, :], start=True, stop=False)
                        for i in range(3):
                            nc.tensor.matmul(p_v[i][:, 0:P], l_v[:, :], hv[:, i, :], start=True, stop=False)
                        last = {id(s[4]): m for m, s in enumerate(steps)}
                        for m, (_, _, _, weights, bank) in enumerate(steps):
                            pe.wait_ge(made, t * STEPS + (STEPS + m + 1))
                            pe.sem_inc(seen, 1)
                            for j, w in enumerate(weights):
                                ins = nc.tensor.matmul(bank[:, 0:P], w, prod[m % BUFS][:, j, :], start=False, stop=m == last[id(bank)] and j == KB - 1)
                            ins.then_inc(used, 1)
                        pe.wait_ge(used, t * STEPS + 2 * STEPS)
                        pe.sem_inc(upd, 1)
        stage_back(nc, K, H, [(us, CS, 0)] + [(uv[i], CV, CS + CV * i) for i in range(3)], "l2b")

BF16 = mybir.dt.bfloat16
HEADS, AS, AV = 4, 16, 8
HW = AS + 3 * AV + 1
NEVER = 1e30


def stage_equivariant_norm(nc, K, H, S, gs, bs, gv):
    with ExitStack() as ctx:
        sb = lambda n, s, d=F32: ctx.enter_context(nc.sbuf_tensor("l3e_" + n, s, d))
        sem = ctx.enter_context(Semaphores(nc))
        square = sb("square", [P, NB, D])
        mean, var, rms, rstd, rrms, eps = (sb(n, [P, NB]) for n in ("mean", "var", "rms", "rstd", "rrms", "eps"))
        steps, squares_ready, roots_ready = sem("norm_steps"), sem("squares_ready"), sem("roots_ready")
        over = lambda t, n: free(t[:, :], [1, NB], [0, n])
        gain = lambda t, n: free(t[:, :], [0, NB], [1, n])
        s, v3 = S[:, :, 0:CS], S[:, :, CS:D]
        vec = lambda t: free(t[:, 0, CS:CS + 1], [D, NB], [CV, 3], [1, CV])
        with nc.Block() as block:
            @block.vector
            def _(dve):
                v = Steps(dve, steps)
                v.done(nc.vector.memset(eps[:, :], LN_EPS))
                v.link(nc.vector.tensor_reduce(mean[:, :], H[:, :, 0:CS], AX.X, ALU.add))
                v.link(nc.vector.tensor_scalar(mean[:, :], mean[:, :], 1.0 / CS, None, ALU.mult))
                v.link(nc.vector.tensor_tensor(s, H[:, :, 0:CS], over(mean, CS), ALU.subtract))
                v.done(nc.vector.tensor_tensor(square[:, :, 0:CS], s, s, ALU.mult))
                v.link(nc.vector.tensor_tensor(square[:, :, CS:D], H[:, :, CS:D], H[:, :, CS:D], ALU.mult))
                v.done(nc.vector.tensor_reduce(var[:, :], square[:, :, 0:CS], AX.X, ALU.add))
                nc.vector.tensor_reduce(rms[:, :], square[:, :, CS:D], AX.X, ALU.add).then_inc(squares_ready, 1)
                dve.wait_ge(roots_ready, 1)
                v.done(nc.vector.reciprocal(rstd[:, :], var[:, :]))
                v.link(nc.vector.reciprocal(rrms[:, :], rms[:, :]))
                v.link(nc.vector.tensor_tensor(s, s, over(rstd, CS), ALU.mult))
                v.link(nc.vector.tensor_tensor(s, s, gain(gs, CS), ALU.mult))
                v.done(nc.vector.tensor_tensor(s, s, gain(bs, CS), ALU.add))
                v.link(nc.vector.tensor_tensor(v3, H[:, :, CS:D], over(rrms, 3 * CV), ALU.mult))
                for i in range(3):
                    vi = S[:, :, CS + CV * i:CS + CV * (i + 1)]
                    v.done(nc.vector.tensor_tensor(vi, vi, gain(gv, CV), ALU.mult))
                v.after()

            @block.scalar
            def _(act):
                act.wait_ge(squares_ready, 1)
                nc.scalar.activation(var[:, :], var[:, :], ACT.Sqrt, bias=eps[:, 0:1], scale=1.0 / CS)
                nc.scalar.activation(rms[:, :], rms[:, :], ACT.Sqrt, bias=eps[:, 0:1], scale=1.0 / CV).then_inc(roots_ready, 1)


def stage_layer3(nc, A, K):
    W3 = lambda n: A["L3_gnn_" + n]
    PAIRS = SLOTS_D // PAIR
    TURN = 4
    TURNS = -(-(PAIRS + 3) // TURN) * TURN
    MS, FW, WN = CS + CV, 4 * P, 2 * CS + 3 * CV
    LEAD = 3 * PAIR
    with ExitStack() as ctx:
        sb = lambda n, s, d=F32: ctx.enter_context(nc.sbuf_tensor("l3_" + n, s, d))
        sem = ctx.enter_context(Semaphores(nc))
        H = sb("h", [P, NB, D])
        stage_norm(nc, K, H, "l3n")
        w_rbf = sb("w_rbf", [PW, PAIR, WN])
        w_a, w_v = sb("w_a", [P, D]), sb("w_v", [P, CV])
        w_hs, w_hv = sb("w_hs", [P, CS]), sb("w_hv", [P, CV])
        alpha_dot = sb("alpha_dot", [P, CS])
        bins = sb("bins", [1, LEAD + 10 * P], I32)
        sel, apart = sb("sel", [3 * HEADS, HEADS, P], BF16), sb("apart", [P, P], BF16)
        wp1, wp2 = sb("wp1", [P, D]), sb("wp2", [CV, D])
        ident_b = sb("ident_b", [P, P], BF16)
        tab_d = sb("table_dst", [P, NB, D])
        with ExitStack() as inner:
            sbi = lambda n, s, d=F32: inner.enter_context(nc.sbuf_tensor("l3_" + n, s, d))
            psi = lambda n: inner.enter_context(nc.psum_tensor("l3_" + n, [P, 512], F32))
            S, tab_s = sbi("normed", [P, NB, D]), sbi("table_src", [P, NB, D])
            wq1, wq2 = sbi("wq1", [P, 2 * D]), sbi("wq2", [CV, 2 * D])
            gs, bs, gv = sbi("gamma_s", [P, CS]), sbi("beta_s", [P, CS]), sbi("gamma_v", [P, CV])
            wg, val_t = sbi("w_gate", [CS, CV]), sbi("w_val_turned", [CS, MS])
            p_seen, head_rows = sbi("loads_seen", [1, 1]), sbi("head_rows", [3 * HEADS, HEADS])
            w2s, w2v = sbi("w2_s", [P, 1]), sbi("w2_v", [P, 1])
            p_t, p_g = psi("p_w_turned"), psi("p_w_gate")
            w_in, w_clear, w_steps, w_loaded, w_turned, w_copied, gated = (
                sem(n) for n in ("w_in", "w_clear", "w_steps", "w_loaded", "w_turned", "w_copied", "gated"))
            V = [slice(CS + CV * i, CS + CV * (i + 1)) for i in range(3)]
            n_loads, LOADS = [], 30
            with nc.Block() as block:
                @block.sync
                def _(sp):
                    sp.wait_ge(w_clear, 1)

                    def load(to, of, **kw):
                        n_loads.append(1)
                        sp.dma_start(to, of, **kw).then_inc(w_in, 16)

                    over_parts = lambda v, n: bass.AP(v.tensor, v.offset, [[0, P], [1, n]])
                    load(gs[:, :], over_parts(W3("gamma_s"), CS))
                    load(bs[:, :], over_parts(W3("beta_s"), CS))
                    load(gv[:, :], over_parts(W3("gamma_v"), CV))
                    load(alpha_dot[:, :], over_parts(W3("alpha_dot"), CS))
                    for w1, w2, c, ws, wv in ((wq1, wq2, 0, "Ws_src", "Wv_src"), (wq1, wq2, D, "Ws_dst", "Wv_dst"), (wp1, wp2, 0, "Wps", "Wpv")):
                        load(w1[0:CS, c:c + CS], W3(ws))
                        for i in range(2):
                            load(w1[V[i], c + V[i].start:c + V[i].stop], W3(wv))
                        load(w2[:, c + V[2].start:c + V[2].stop], W3(wv))
                    for s in range(PAIR):
                        at = s * WORDS_D + D_E16
                        load(w_rbf[at:at + 16, s, :], W3("W_rbf"))
                    load(w_a[0:MS, 0:CS], W3("W_alpha"))
                    load(w_a[0:MS, CS:2 * CS], W3("Ws_val"))
                    load(w_v[:, :], W3("Wv_val"))
                    load(wg[:, :], W3("Wg"))
                    load(w_hs[0:MS, :], W3("Ws_vlin"))
                    load(w_hv[:, :], W3("Wv_vlin"))
                    col = lambda n: W3(n).rearrange("(f o) -> f o", o=1)
                    for to, at, n in ((w2s, 0, "w2_ss"), (w2s, CS, "w2_vv0"), (w2v, 0, "w2_sv"), (w2v, CS, "w2_vs"), (w2v, MS, "w2_vv1")):
                        f = CS if at == 0 else CV
                        load(to[at:at + f, :], col(n), allow_slow_non_contiguous=True)
                    load(bins[0:1, LEAD:], K["bins_d"].rearrange("(o n) -> o n", o=1))

                @block.vector
                def _(dve):
                    v = Steps(dve, w_steps)
                    for t in (wq1, wq2, wp1, wp2, w_a, w_hs, w2s):
                        nc.vector.memset(t[:, :], 0.0)
                    nc.vector.memset(bins[0:1, 0:LEAD], 0)
                    nc.vector.memset(w_rbf[:, :, :], 0.0).then_inc(w_clear, 1)
                    i12 = K["ident"][0:3 * HEADS, :]

                    v.link(nc.vector.tensor_tensor(head_rows[:, :], i12[:, 0:HEADS], i12[:, HEADS:2 * HEADS], ALU.add))
                    v.link(nc.vector.tensor_tensor(head_rows[:, :], head_rows[:, :], i12[:, 2 * HEADS:3 * HEADS], ALU.add))
                    v.done(nc.vector.tensor_copy(sel[:, :, :], free(head_rows[:, :], [1, HEADS], [0, P])))
                    v.done(nc.vector.tensor_copy(ident_b[:, :], K["ident"][:, :]))
                    v.done(nc.vector.tensor_scalar(apart[:, :], K["ident"][:, :], 1.0, NEVER, ALU.subtract, ALU.mult))
                    dve.wait_ge(w_in, 16 * LOADS)
                    nc.vector.memset(p_seen[:, :], 0.0).then_inc(w_loaded, 1)
                    scaled = lambda ap, f: v.done(nc.vector.tensor_scalar(ap, ap, f, None, ALU.mult))
                    r2, r3 = 2.0 ** -0.5, 3.0 ** -0.5
                    scaled(w_rbf[:, :, 2 * CS + CV:2 * CS + 2 * CV], r3)
                    scaled(w_rbf[:, :, 2 * CS + 2 * CV:WN], r2)
                    v.after()
                    scaled(w_hs[:, :], w2s[:, 0:1])
                    scaled(w_hv[:, :], w2v[:, 0:1])
                    v.after()
                    scaled(w_hs[0:CS, :], 0.5)
                    scaled(w_hs[CS:MS, :], 0.5 * r3)
                    scaled(w_hv[0:MS, :], 0.5)
                    scaled(w_hv[MS:P, :], 0.5 * r2)
                    dve.wait_ge(gated, 1)
                    v.done(nc.vector.tensor_copy(w_a[0:MS, 2 * CS:D], p_g[0:MS, 0:CV]))
                    v.after()

                @block.tensor
                def _(pe):
                    pe.wait_ge(w_loaded, 1)
                    nc.tensor.transpose(p_t[0:CS, 0:MS], w_a[0:MS, CS:2 * CS], K["ident"][0:MS, 0:MS]).then_inc(w_turned, 1)
                    pe.wait_ge(w_copied, 1)
                    nc.tensor.matmul(p_g[0:MS, 0:CV], val_t[:, :], wg[:, :], start=True, stop=True).then_inc(gated, 1)

                @block.scalar
                def _(act):
                    act.wait_ge(w_turned, 1)
                    nc.scalar.copy(val_t[:, :], p_t[0:CS, 0:MS]).then_inc(w_copied, 1)
            assert len(n_loads) == LOADS, len(n_loads)
            stage_equivariant_norm(nc, K, H, S, gs, bs, gv)
            stage_project(nc, K, S, wq1, wq2, None, tab_s, tab_d, "l3p")
            tab_out = sem("tab_out")
            with nc.Block() as block:
                @block.sync
                def _(sp):
                    sp.dma_start(K["table0"].rearrange("(b p) f -> p b f", p=P), tab_s[:, :, :]).then_inc(tab_out, 16)
                    sp.wait_ge(tab_out, 16)

        acc, top = sb("sums", [P, NB, HEADS, HW]), sb("maxima", [P, NB, HEADS])
        with ExitStack() as inner:
            sbi = lambda n, s, d=F32: inner.enter_context(nc.sbuf_tensor("l3_" + n, s, d))
            ps = lambda n, s, d=F32: inner.enter_context(nc.psum_tensor("l3_" + n, s, d))
            semi = inner.enter_context(Semaphores(nc))
            four = lambda n, s, d=F32: [sbi(f"{n}{u}", s, d) for u in range(4)]
            two = lambda n, s, d=F32: [sbi(f"{n}{u}", s, d) for u in range(2)]
            pay, xg = four("edge_rows", [P, PAIR, WORDS_D]), four("source_rows", [P, PAIR, D])
            hot = four("node_onehot", [P, PAIR, P])
            hot_t, hot_tb = four("onehot_turned", [P, PAIR * P]), four("onehot_turned_b", [P, PAIR * P], BF16)
            pay_t = sbi("edge_rows_turned", [PW, P])
            msg = sbi("message", [P, PAIR, D])
            us, uv = sbi("weighted_s", [P, PAIR, 2, CS]), sbi("weighted_v", [P, PAIR, 3, 3, CV])
            F, G_ = two("product1", [P, PAIR, 4, P]), two("product2", [P, PAIR, 4, P])
            f_t, g_t = two("product1_turned", [P, 4 * P]), two("product2_turned", [P, 4 * P])
            dots = sbi("dot_parts", [P, PAIR, 3, CV])
            crossed, crossed_back = two("crossed", [P, PAIR, 3, CV]), two("crossed_back", [P, PAIR, 3, CV])
            th, sg, val_v = sbi("half_tanh", [P, PAIR, MS]), sbi("twice_sigmoid", [P, PAIR, MS]), sbi("val_v", [P, PAIR, 3, CV])
            slope, leaky, lsum = sbi("slope", [P, PAIR, CS]), sbi("leaky", [P, PAIR, CS]), sbi("logits", [P, PAIR, HEADS])
            none = sbi("empty_row", [P, PAIR])
            logit = two("logits_kept", [P, PAIR, HEADS])
            rest = sbi("rest", [P, PAIR, 2, HEADS])
            a3, a3_t = sbi("logit_parts", [P, PAIR, 3, HEADS], BF16), sbi("logit_parts_turned", [3 * HEADS, PAIR * P], BF16)
            qm, mn, drop, shrink = (sbi(n, [P, HEADS]) for n in ("pair_max", "new_max", "max_step", "shrink"))
            ea, Z = sbi("weight_logits", [P, PAIR, HEADS]), sbi("weighted", [P, PAIR, HEADS, HW])

            p_f = ps("p_front", [P, 512])
            p_a3 = p_f[0:3 * HEADS, 3 * P:4 * P].bitcast(BF16)
            p_w, p_d = ps("p_weights", [P, PAIR, 256]), ps("p_dst", [P, 512])
            p_t = [ps(f"p_turn{u}", [P, 512]) for u in range(2)]
            p_a, p_h, p_m = ps("p_logits_values", [P, PAIR, 256]), ps("p_heads", [P, 512]), ps("p_max", [P, 2, PAIR * P])
            heads = lambda s: p_h[:, s * D:(s + 1) * D].rearrange("p (h c) -> p h c", h=HEADS)
            MG, SUM = 2 * D, 2 * D

            pay_in = [semi(f"pay_in{u}") for u in range(4)]
            xg_in = [semi(f"xg_in{u}") for u in range(4)]
            ahead = ("hot_made", "front_turned", "front_copied", "front_done")
            once = ("us_made", "uv_made", "a_done", "a_scaled", "a_crossed",
                    "logits_done", "tanh_done", "lsum_made", "a3_made", "a3_turned", "a3_copied", "heads_done", "max_made", "max_gathered",
                    "shrink_done", "ea_made", "ex_done", "sg_made", "val_made", "b_done", "z_made", "summed", "acc_done")
            twice = ("f_turned", "f_copied", "g_turned", "g_copied", "masked", "max_taken")
            rows_readers = ("rows_used", "b_scaled", "b_crossed")
            plain = ("cleared", "steps", "pool_steps", "pe_seen", "pool_seen", "sp_seen", "dve_seen")
            m = {n: semi(n) for n in ahead + once + twice + rows_readers + plain}
            credit = {n: 1 for n in once} | {n: 2 for n in twice} | {n: 3 for n in rows_readers}

            def value(name, it, u, off=0, k=None):
                per = 2 if name in twice else 1
                return it * (TURN * per) + ((u + off) * per + (per if k is None else k) + credit.get(name, 1))
            PT = 4 * P
            with nc.Block() as block:
                @block.sync
                def _(sp):
                    sp.wait_ge(m["cleared"], 1)
                    def load(it, u):
                        for n in rows_readers:
                            sp.wait_ge(m[n], value(n, it, u, -3))
                            sp.sem_inc(m["sp_seen"], 1)
                        r = (it * TURN + u) * (PAIR * P)
                        sp.dma_start(pay[u][:, :, :], K["rows_d"][bass.ds(r, PAIR * P), :].rearrange("(s p) w -> p s w", p=P)).then_inc(pay_in[u], 16)

                    with sp.Fori(0, TURNS // TURN) as it:
                        for u in range(TURN):
                            load(it, u)
                    load(TURNS // TURN, 0)

                @block.gpsimd
                def _(pool):
                    TT = nc.gpsimd.tensor_tensor

                    def wait(n, v):
                        pool.wait_ge(m[n], v)
                        pool.sem_inc(m["pool_seen"], 1)

                    def gather(u, loaded):
                        pool.wait_ge(pay_in[u], loaded)
                        pool.sem_inc(m["pool_seen"], 1)
                        for s in range(PAIR):
                            pool.indirect_dma_start(xg[u][:, s, :], None, K["table0"],
                                                    bass.IndirectOffsetOnAxis(ap=pay[u][:, s, D_SRC:D_SRC + 1].bitcast(U32), axis=0)).then_inc(xg_in[u], 16)

                    def cross(v, n, w, pay_, out, done):
                        y1 = lambda i, *d: free(pay_[:, 0, D_E4 + 1 + i:D_E4 + 2 + i], [WORDS_D, PAIR], *d)
                        there, back = crossed[n], crossed_back[n]
                        v.done(TT(there[:, :, 0:2, :], w(1, 2), y1(2, [1, 2], [0, CV]), ALU.mult))
                        v.done(TT(there[:, :, 2, :], w(0, 1)[:, :, 0, :], y1(1, [0, CV]), ALU.mult))
                        v.done(TT(back[:, :, 0, :], w(2, 1)[:, :, 0, :], y1(1, [0, CV]), ALU.mult))
                        v.done(TT(back[:, :, 1:3, :], w(0, 2), y1(2, [1, 2], [0, CV]), ALU.mult))
                        v.after()
                        TT(free(out[:, 0, 1, MS:MS + 1], [PT, PAIR], [P, 3], [1, CV]), there[:, :, :, :], back[:, :, :, :], ALU.subtract).then_inc(m[done], 1)

                    wait("cleared", 1)
                    gather(0, 16)
                    v = Steps(pool, m["pool_steps"], per=TURN * 13)
                    with pool.Fori(0, TURNS // TURN) as it:
                        v.begin(it)
                        for u in range(TURN):
                            t = lambda n, off=0, k=None: value(n, it, u, off, k)
                            prev = (u - 1) % 4
                            gather((u + 1) % 4, it * 16 + 16 * ((u + 1) // 4 + 1))
                            wait("uv_made", t("uv_made"))
                            cross(v, 0, lambda i, n: uv[:, :, i:i + n, 2, :], pay[u], F[u % 2], "a_crossed")
                            lk = logit[prev % 2]
                            wait("lsum_made", t("lsum_made"))
                            v.done(TT(lk[:, :, :], lsum[:, :, :], free(none[:, :], [1, PAIR], [0, HEADS]), ALU.add))
                            wait("a3_turned", t("a3_turned", -1))
                            v.after()
                            pool.sem_inc(m["pool_seen"], 1)
                            v.link(nc.gpsimd.tensor_copy(a3[:, :, 0, :], lk[:, :, :]))
                            v.link(TT(rest[:, :, 0, :], lk[:, :, :], a3[:, :, 0, :], ALU.subtract))
                            pool.sem_inc(m["pool_seen"], 1)
                            v.link(nc.gpsimd.tensor_copy(a3[:, :, 1, :], rest[:, :, 0, :]))
                            v.link(TT(rest[:, :, 1, :], rest[:, :, 0, :], a3[:, :, 1, :], ALU.subtract))
                            pool.sem_inc(m["pool_seen"], 1)
                            nc.gpsimd.tensor_copy(a3[:, :, 2, :], rest[:, :, 1, :]).then_inc(m["a3_made"], 1)
                            wait("val_made", t("val_made"))
                            cross(v, 1, lambda i, n: val_v[:, :, i:i + n, :], pay[prev], G_[prev % 2], "b_crossed")
                        v.end()
                    pool.wait_ge(xg_in[0], (TURNS // TURN + 1) * 16 * PAIR)

                @block.tensor
                def _(pe):
                    bin_reg = pe.alloc_register("l3_pe_bin")
                    flat = lambda tile: tile.rearrange("p s w -> p (s w)")

                    def seen(n, v):
                        pe.wait_ge(m[n], v)
                        pe.sem_inc(m["pe_seen"], 1)

                    def front_turn(u):
                        for s in range(PAIR):
                            nc.tensor.transpose(p_f[:, s * P:(s + 1) * P], hot[u][:, s, :], K["ident"][:, :])
                        nc.tensor.transpose(p_f[0:PW, 2 * P:3 * P], flat(pay[u][:, :, :]), K["ident"][:, :]).then_inc(m["front_turned"], 1)

                    def front(u, b):
                        for s in range(PAIR):
                            nc.tensor.matmul(p_w[:, s, 0:WN], pay_t[:, :], w_rbf[:, s, :], start=True, stop=True)
                        for s in range(PAIR):
                            ins = nc.tensor.matmul(p_d[:, s * D:(s + 1) * D], hot_t[u][:, s * P:(s + 1) * P], tab_d[:, bass.ds(b, 1), :].rearrange("p o f -> p (o f)"), start=True, stop=True)
                        ins.then_inc(m["front_done"], 1)

                    def load_bin(slot):
                        pe.reg_load([bin_reg], bins[0:1, bass.ds(slot + LEAD, 1)])

                    def bin_loaded():
                        return pe.snap(bin_reg, min_val=0, max_val=NB - 1)

                    def masked(half, u):
                        for j in range(2):
                            nc.tensor.matmul(p_m[:, j, :], sel[:, 2 * half + j, :], a3_t[:, :], start=True, stop=False)
                            ins = nc.tensor.matmul(p_m[:, j, :], apart[:, :], hot_tb[u][:, :], start=False, stop=True)
                        ins.then_inc(m["masked"], 1)

                    pe.wait_ge(m["cleared"], 1)
                    seen("hot_made", 1)
                    front_turn(0)
                    seen("front_copied", 1)
                    load_bin(0)
                    front(0, bin_loaded())
                    load_bin(PAIR)
                    with pe.Fori(0, TURNS // TURN) as it:
                        for u in range(TURN):
                            wait = lambda n, off=0, k=None: seen(n, value(n, it, u, off, k))
                            ahead_u, prev, prev2 = (u + 1) % 4, (u - 1) % 4, (u - 2) % 4
                            for n in ("a_done", "a_scaled", "a_crossed"):
                                wait(n, -1)
                            wait("g_copied", -1)
                            for s in range(PAIR):
                                for c in range(4):
                                    ins = nc.tensor.transpose(p_t[s][:, c * P:(c + 1) * P], F[prev % 2][:, s, c, :], K["ident"][:, :])
                                ins.then_inc(m["f_turned"], 1)
                            wait("max_taken", 0, 1)
                            masked(1, prev2)
                            wait("val_made", -1)
                            for s in range(PAIR):
                                wait("f_copied", 0, s + 1)
                                nc.tensor.matmul(p_a[:, s, 0:D], f_t[s][:, 0:P], w_a[:, :], start=True, stop=True)
                                for i in range(3):
                                    ins = nc.tensor.matmul(p_a[:, s, D + CV * i:D + CV * (i + 1)], f_t[s][:, (i + 1) * P:(i + 2) * P], w_v[:, :], start=True, stop=True)
                            ins.then_inc(m["logits_done"], 1)
                            for n in ("b_done", "b_scaled", "b_crossed"):
                                wait(n, -1)
                            for s in range(PAIR):
                                for c in range(4):
                                    ins = nc.tensor.transpose(p_t[s][:, c * P:(c + 1) * P], G_[prev2 % 2][:, s, c, :], K["ident"][:, :])
                                ins.then_inc(m["g_turned"], 1)
                            wait("a3_copied", -1)
                            wait("hot_made")
                            front_turn(ahead_u)
                            wait("max_made")
                            wait("uv_made")
                            for s in range(PAIR):
                                ins = nc.tensor.matmul(p_d[:, MG + s * HEADS:MG + (s + 1) * HEADS], hot_t[prev2][:, s * P:(s + 1) * P], mn[:, :], start=True, stop=True)
                            ins.then_inc(m["max_gathered"], 1)
                            wait("acc_done")
                            for s in range(PAIR):
                                wait("g_copied", 0, s + 1)
                                split = lambda w, n: w.rearrange("p (h c) -> p h c", c=n)
                                nc.tensor.matmul(heads(s)[:, :, 0:AS], g_t[s][:, 0:P], split(w_hs[:, :], AS), start=True, stop=True)
                                for i in range(3):
                                    ins = nc.tensor.matmul(heads(s)[:, :, AS + AV * i:AS + AV * (i + 1)], g_t[s][:, (i + 1) * P:(i + 2) * P], split(w_hv[:, :], AV), start=True, stop=True)
                            ins.then_inc(m["heads_done"], 1)
                            wait("front_copied")
                            wait("ea_made")
                            front(ahead_u, bin_loaded())
                            wait("a3_made")
                            for s in range(PAIR):
                                ins = nc.tensor.transpose(p_a3[:, s * P:(s + 1) * P], a3[:, s, :, :].rearrange("p k h -> p (k h)"), ident_b[:, :])
                            ins.then_inc(m["a3_turned"], 1)
                            load_bin((it * TURN + u + 2) * PAIR)
                            wait("z_made")
                            for s in range(PAIR):
                                ins = nc.tensor.matmul(p_h[:, SUM:SUM + HEADS * HW], hot[prev2][:, s, :], Z[:, s, :, :].rearrange("p h c -> p (h c)"), start=s == 0, stop=s == PAIR - 1)
                            ins.then_inc(m["summed"], 1)
                            wait("a3_copied")
                            wait("max_taken")
                            masked(0, prev)

                @block.scalar
                def _(act):
                    def front(u):
                        nc.scalar.copy(hot_t[u][:, :], p_f[:, 0:2 * P])
                        nc.scalar.copy(hot_tb[u][:, :], p_f[:, 0:2 * P])
                        nc.scalar.copy(pay_t[:, :], p_f[0:PW, 2 * P:3 * P]).then_inc(m["front_copied"], 1)

                    act.wait_ge(m["cleared"], 1)
                    act.wait_ge(m["front_turned"], 1)
                    front(0)
                    with act.Fori(0, TURNS // TURN) as it:
                        for u in range(TURN):
                            def wait(n, off=0, k=None):
                                act.wait_ge(m[n], value(n, it, u, off, k))

                            prev = (u - 1) % 4
                            y1 = lambda q, s, i: pay[q][:, s, D_E4 + 1 + i:D_E4 + 2 + i]
                            wait("logits_done", -1)
                            for s in range(PAIR):
                                wait("f_turned", 0, s + 1)
                                nc.scalar.copy(f_t[s][:, :], p_t[s][:, :]).then_inc(m["f_copied"], 1)
                            wait("us_made")
                            for s in range(PAIR):
                                for i in range(3):
                                    ins = nc.scalar.activation(F[u % 2][:, s, 1 + i, 0:CS], us[:, s, 1, :], ACT.Copy, scale=y1(u, s, i))
                            ins.then_inc(m["a_scaled"], 1)
                            wait("logits_done")
                            wait("b_done", -1)
                            nc.scalar.activation(slope[:, :, :], p_a[:, :, 0:CS], ACT.Copy, scale=0.2)
                            nc.scalar.activation(th[:, :, :], p_a[:, :, CS:D], ACT.Tanh, scale=0.5).then_inc(m["tanh_done"], 1)
                            wait("heads_done", -1)
                            for s in range(PAIR):
                                wait("g_turned", 0, s + 1)
                                nc.scalar.copy(g_t[s][:, :], p_t[s][:, :]).then_inc(m["g_copied"], 1)
                            wait("front_turned")
                            wait("front_done", -1)
                            front((u + 1) % 4)
                            wait("max_made")
                            nc.scalar.activation(shrink[:, :], drop[:, :], ACT.Exp).then_inc(m["shrink_done"], 1)
                            def scale_b(s):
                                for i in range(3):
                                    ins = nc.scalar.activation(G_[prev % 2][:, s, 1 + i, 0:CS], sg[:, s, 0:CS], ACT.Copy, scale=y1(prev, s, i))
                                return ins

                            wait("sg_made")
                            scale_b(0)
                            wait("ea_made")
                            wait("summed", -1)
                            nc.scalar.activation(Z[:, :, :, HW - 1], ea[:, :, :], ACT.Exp).then_inc(m["ex_done"], 1)
                            wait("a3_turned")
                            wait("masked", 0, 1)
                            nc.scalar.copy(a3_t[:, :], p_a3).then_inc(m["a3_copied"], 1)
                            scale_b(1).then_inc(m["b_scaled"], 1)

                @block.vector
                def _(dve):
                    v = Steps(dve, m["steps"])
                    for group in (pay, xg, hot, hot_t, hot_tb, F, G_, logit, (a3, Z, acc, shrink, mn, ea, drop)):
                        for tile in group:
                            nc.vector.memset(tile[...], 0.0)
                    nc.vector.memset(a3_t[:, :], -NEVER)
                    nc.vector.memset(p_m[:, :, :], -NEVER)
                    nc.vector.memset(p_h[:, :], 0.0)
                    v.done(nc.vector.memset(top[:, :, :], -NEVER))
                    v.after()
                    for n, c in credit.items():
                        dve.sem_inc(m[n], c)
                    dve.sem_inc(m["cleared"], 1)
                    bin_c, bin_e = dve.alloc_register("l3_bin_c"), dve.alloc_register("l3_bin_e")
                    TT = nc.vector.tensor_tensor
                    y0 = lambda q, *d: free(pay[q][:, 0, D_E4:D_E4 + 1], [WORDS_D, PAIR], *d)
                    y1 = lambda q, *d: free(pay[q][:, 0, D_E4 + 1:D_E4 + 2], [WORDS_D, PAIR], *d)
                    parts = lambda out, c, n: free(out[:, 0, 1, c:c + 1], [PT, PAIR], [P, 3], [1, n])

                    def onehot(u, loaded):
                        dve.wait_ge(pay_in[u], loaded)
                        TT(hot[u][:, :, :], free(K["iota_f"][:, 1:2], [0, PAIR], [1, P]),
                           free(pay[u][:, 0, D_LOC:D_LOC + 1], [WORDS_D, PAIR], [0, P]), ALU.is_equal).then_inc(m["hot_made"], 1)

                    def load_bins(slot):
                        dve.reg_load([bin_e], bins[0:1, bass.ds(slot, 1)])
                        dve.reg_load([bin_c], bins[0:1, bass.ds(slot + PAIR, 1)])

                    onehot(0, 16)
                    load_bins(0)
                    w = Steps(dve, m["steps"], per=TURN * 15, base=v.k)
                    with dve.Fori(0, TURNS // TURN) as it:
                        w.begin(it)
                        for u in range(TURN):
                            def wait(n, off=0, k=None):
                                dve.wait_ge(m[n], value(n, it, u, off, k))

                            prev = (u - 1) % 4
                            be, bc = dve.snap(bin_e, min_val=0, max_val=NB - 1), dve.snap(bin_c, min_val=0, max_val=NB - 1)
                            acc_b = acc[:, bass.ds(be, 1), :, :].rearrange("p o h c -> p (o h) c")
                            top_b = top[:, bass.ds(bc, 1), :].rearrange("p o h -> p (o h)")
                            wait("front_done", -1)
                            dve.wait_ge(xg_in[u], it * (16 * PAIR) + 16 * PAIR)
                            msg_made = w.done(TT(msg[:, :, :], p_d[:, 0:2 * D].rearrange("p (s f) -> p s f", s=PAIR), xg[u][:, :, :], ALU.add))
                            wait("shrink_done", -1)
                            wait("acc_done", -1)
                            shrunk = w.done(TT(acc_b, acc_b, free(shrink[:, :], [1, HEADS], [0, HW]), ALU.mult))
                            wait("f_turned", -1)
                            wait("a_scaled", -1)
                            wait("a_crossed", -1)
                            w.after(msg_made)
                            TT(us[:, :, :, :], p_w[:, :, 0:2 * CS].rearrange("p s (a c) -> p s a c", a=2), free(msg[:, :, 0:1], [D, PAIR], [0, 2], [1, CS]), ALU.mult).then_inc(m["us_made"], 1)
                            wait("masked", -1, 2)
                            nc.vector.tensor_reduce(qm[:, 0:2], p_m[:, :, :], AX.X, ALU.max).then_inc(m["max_taken"], 1)
                            for i in range(3):
                                ins = TT(uv[:, :, i, :, :], p_w[:, :, 2 * CS:WN].rearrange("p s (a c) -> p s a c", a=3),
                                         free(msg[:, 0, CS + CV * i:CS + CV * i + 1], [D, PAIR], [0, 3], [1, CV]), ALU.mult)
                            ins.then_inc(m["uv_made"], 1)
                            wait("summed", -1)
                            w.after(shrunk)
                            TT(acc_b, acc_b, p_h[:, SUM:SUM + HEADS * HW].rearrange("p (h c) -> p h c", h=HEADS), ALU.add).then_inc(m["acc_done"], 1)
                            wait("masked", 0, 1)
                            nc.vector.tensor_reduce(qm[:, 2:4], p_m[:, :, :], AX.X, ALU.max).then_inc(m["max_taken"], 1)
                            wait("uv_made")
                            dots_made = w.done(TT(dots[:, :, :, :], uv[:, :, :, 1, :], y1(u, [1, 3], [0, CV]), ALU.mult))
                            f = F[u % 2]
                            w.done(TT(f[:, :, 0, 0:CS], us[:, :, 0, :], y0(u, [0, CS]), ALU.mult))
                            wait("max_taken")
                            mn_made = w.done(TT(mn[:, :], top_b, qm[:, :], ALU.max))
                            w.done(TT(parts(f, CS, CV), uv[:, :, :, 0, :], y0(u, [0, 3], [0, CV]), ALU.mult))
                            w.after(dots_made)
                            dots_made = w.done(TT(dots[:, :, 0, :], dots[:, :, 0, :], dots[:, :, 1, :], ALU.add))
                            w.after(mn_made)
                            dropped = w.done(TT(drop[:, :], top_b, mn[:, :], ALU.subtract))
                            onehot((u + 1) % 4, it * 16 + 16 * ((u + 1) // 4 + 1))
                            w.after(dots_made)
                            TT(f[:, :, 0, CS:MS], dots[:, :, 0, :], dots[:, :, 2, :], ALU.add).then_inc(m["a_done"], 1)
                            w.after(dropped)
                            dve.sem_inc(m["dve_seen"], 1)
                            nc.vector.tensor_copy(top_b, mn[:, :]).then_inc(m["max_made"], 1)
                            wait("tanh_done")
                            leaky_made = w.done(TT(leaky[:, :, :], p_a[:, :, 0:CS], slope[:, :, :], ALU.max))
                            wait("b_scaled", -1)
                            nc.vector.tensor_scalar(sg[:, :, :], th[:, :, :], 1.0, None, ALU.add).then_inc(m["sg_made"], 1)
                            wait("a3_made", -1)
                            w.done(nc.vector.tensor_scalar(none[:, :], pay[prev][:, :, D_LOC], 0.5, -NEVER, ALU.is_lt, ALU.mult))
                            w.after(leaky_made)
                            leaky_made = w.done(TT(leaky[:, :, :], leaky[:, :, :], free(alpha_dot[:, :], [0, PAIR], [1, CS]), ALU.mult))
                            wait("b_crossed", -1)
                            wait("sg_made")
                            TT(val_v[:, :, :, :], free(sg[:, 0, CS:CS + 1], [MS, PAIR], [0, 3], [1, CV]),
                               p_a[:, :, D:256].rearrange("p s (i c) -> p s i c", i=3), ALU.mult).then_inc(m["val_made"], 1)
                            w.after(leaky_made)
                            nc.vector.tensor_reduce(lsum[:, :, :], leaky[:, :, :].rearrange("p s (h c) -> p s h c", h=HEADS), AX.X, ALU.add).then_inc(m["lsum_made"], 1)
                            wait("max_gathered")
                            wait("ex_done", -1)
                            TT(ea[:, :, :], logit[u % 2][:, :, :], p_d[:, MG:MG + PAIR * HEADS].rearrange("p (s h) -> p s h", s=PAIR), ALU.subtract).then_inc(m["ea_made"], 1)
                            g = G_[prev % 2]
                            wait("g_turned", -1)
                            wait("val_made")
                            dots_made = w.done(TT(dots[:, :, :, :], val_v[:, :, :, :], y1(prev, [1, 3], [0, CV]), ALU.mult))
                            w.done(TT(g[:, :, 0, 0:CS], sg[:, :, 0:CS], y0(prev, [0, CS]), ALU.mult))
                            w.after(dots_made)
                            dots_made = w.done(TT(dots[:, :, 0, :], dots[:, :, 0, :], dots[:, :, 1, :], ALU.add))
                            w.done(TT(parts(g, CS, CV), val_v[:, :, :, :], y0(prev, [0, 3], [0, CV]), ALU.mult))
                            w.after(dots_made)
                            TT(g[:, :, 0, CS:MS], dots[:, :, 0, :], dots[:, :, 2, :], ALU.add).then_inc(m["b_done"], 1)
                            load_bins((it * TURN + u + 1) * PAIR)
                            wait("ex_done")
                            wait("heads_done")
                            for s, done in ((0, "rows_used"), (1, "z_made")):
                                TT(Z[:, s, :, 0:HW - 1], heads(s), free(Z[:, s, 0, HW - 1:HW], [HW, HEADS], [0, HW - 1]), ALU.mult).then_inc(m[done], 1)
                        w.end()

        with ExitStack() as inner:
            sbi = lambda n, s, d=F32: inner.enter_context(nc.sbuf_tensor("l3_" + n, s, d))
            semi = inner.enter_context(Semaphores(nc))
            den, agg, upd = sbi("weight_sums", [P, NB, HEADS]), sbi("head_means", [P, NB, D]), sbi("update", [P, NB, D])
            steps, x_done = semi("steps"), semi("x_done")
            with nc.Block() as block:
                @block.vector
                def _(dve):
                    v = Steps(dve, steps)
                    v.link(nc.vector.tensor_scalar(den[:, :, :], acc[:, :, :, HW - 1], 1e-16, None, ALU.add))
                    v.link(nc.vector.reciprocal(den[:, :, :], den[:, :, :]))
                    for h in range(HEADS):
                        over = lambda n: free(den[:, 0, h:h + 1], [HEADS, NB], [0, n])
                        v.done(nc.vector.tensor_tensor(agg[:, :, h * AS:(h + 1) * AS], acc[:, :, h, 0:AS], over(AS), ALU.mult))
                        for i in range(3):
                            c = CS + CV * i + h * AV
                            v.done(nc.vector.tensor_tensor(agg[:, :, c:c + AV], acc[:, :, h, AS + AV * i:AS + AV * (i + 1)], over(AV), ALU.mult))
                    v.after()
            stage_project(nc, K, agg, wp1, wp2, None, upd, None, "l3q")
            with nc.Block() as block:
                @block.vector
                def _(dve):
                    v = Steps(dve, x_done)
                    for t_ in (H, upd):
                        v.link(nc.vector.tensor_tensor(K["X"][:, :, :], K["X"][:, :, :], t_[:, :, :], ALU.add))


def build(nc, A, out):
    with ExitStack() as ctx:
        K = consts(nc, ctx, A)
        stage_setup(nc, A, K)
        stage_sort(nc, A, K)
        stage_layer0(nc, A, K)
        stage_layer1(nc, A, K)
        stage_layer2(nc, A, K)
        stage_layer3(nc, A, K)
        stage_finish(nc, A, K, out)


def kernel(**inputs):
    import concourse.bacc as bacc
    from concourse.bass_utils import run_bass_kernel_spmd

    nc = bacc.Bacc("TRN2", target_bir_lowering=False, num_devices=1)
    arrays, A = {}, {}
    for name, value in inputs.items():
        a = np.ascontiguousarray(value)
        arrays["in_" + name] = a
        A[name] = nc.dram_tensor("in_" + name, a.shape, mybir.dt.from_np(a.dtype), kind="ExternalInput").ap()
    out = nc.dram_tensor("out_x", (N, D), F32, kind="ExternalOutput").ap()
    build(nc, A, out)
    r = run_bass_kernel_spmd(nc, [arrays], core_ids=[0])
    return r.results[0]["out_x"]
```
